# Optimizing a Trainium2 kernel written in Bass

```python
import numpy as np
import jax
import jax.numpy as jnp

def _softmax(x, axis=-1):
    return jax.nn.softmax(x, axis=axis)

def _gelu(x):
    return jax.nn.gelu(x, approximate=True)

def _silu(x):
    return jax.nn.silu(x)

def _sigmoid(x):
    return jax.nn.sigmoid(x)

def _layernorm(x, axis=-1, eps=1e-05):
    m = jnp.mean(x, axis=axis, keepdims=True)
    v = jnp.var(x, axis=axis, keepdims=True)
    return (x - m) / jnp.sqrt(v + eps)

def _scatter_add(tgt, idx, src, axis=0):
    return tgt.at[idx].add(src)

def _segment_sum(src, seg, n):
    return jax.ops.segment_sum(src, seg, n)
kernel_name = 'mk_metaformer_d2_conv_nchw2048_r4_70dbf0'

def setup_inputs(seed: int=0):
    np.random.seed(seed)
    _w = jnp.asarray

    def _rec_inputs():
        import jax
        import jax.numpy as jnp
        _gk = jax.random.key(seed)
        x = -0.000125 + 0.9999 * jax.random.normal(jax.random.fold_in(_gk, 1), (4, 512, 16, 16), jnp.float32)
        return x
    x = _rec_inputs()

    def _L0_conv_setup():
        import jax, jax.numpy as jnp
        import numpy as np
        C = 512
        RED = 8
        D = C // RED
        key = jax.random.key(seed)
        ks = jax.random.split(key, 8)
        n, h, w = (4, 16, 16)
        x = jax.random.normal(ks[0], (n, C, h, w), dtype=jnp.float32)
        w1 = jax.random.normal(ks[1], (D, C), dtype=jnp.float32) * 0.02
        b1 = jnp.zeros((D,), dtype=jnp.float32)
        w2 = jax.random.normal(ks[2], (D, C), dtype=jnp.float32) * 0.02
        b2 = jnp.zeros((D,), dtype=jnp.float32)
        w3 = jax.random.normal(ks[3], (C, C), dtype=jnp.float32) * 0.02
        b3 = jnp.zeros((C,), dtype=jnp.float32)
        alpha = jnp.zeros((1,), dtype=jnp.float32)
        return {'x': x, 'w1': w1, 'b1': b1, 'w2': w2, 'b2': b2, 'w3': w3, 'b3': b3, 'alpha': alpha}
    _L0_conv_all = _L0_conv_setup()
    _L0_conv_in = {k: v for k, v in _L0_conv_all.items() if k in ('w1', 'b1', 'w2', 'b2', 'w3', 'b3', 'alpha')}
    del _L0_conv_all

    def _L0_ffn_setup():
        import jax, jax.numpy as jnp
        import numpy as np
        TOP_K = 4
        EPS = 1e-06

        def _rmsnorm(x, w):
            var = jnp.mean(x * x, axis=-1, keepdims=True)
            return x * jax.lax.rsqrt(var + EPS) * w
        key = jax.random.key(seed)
        ks = jax.random.split(key, 8)
        B, S, H, E, I, IS = (32, 1, 512, 16, 1024, 1024)
        s = 0.02
        return {'hidden_states': jax.random.normal(ks[0], (B, S, H), jnp.float32), 'ln_weight': jnp.ones((H,), jnp.float32), 'router_weight': jax.random.normal(ks[1], (H, E), jnp.float32) * s, 'gate_up_proj': jax.random.normal(ks[2], (E, H, 2 * I), jnp.float32) * s, 'down_proj': jax.random.normal(ks[3], (E, I, H), jnp.float32) * s, 'shared_gate_w': jax.random.normal(ks[4], (H, IS), jnp.float32) * s, 'shared_up_w': jax.random.normal(ks[5], (H, IS), jnp.float32) * s, 'shared_down_w': jax.random.normal(ks[6], (IS, H), jnp.float32) * s}
    _L0_ffn_all = _L0_ffn_setup()
    _L0_ffn_in = {k: v for k, v in _L0_ffn_all.items() if k in ('ln_weight', 'router_weight', 'gate_up_proj', 'down_proj', 'shared_gate_w', 'shared_up_w', 'shared_down_w')}
    del _L0_ffn_all

    def _L1_conv_setup():
        import jax, jax.numpy as jnp
        import numpy as np
        N, C, H, WD = (4, 512, 48, 24)
        KH = 9
        key = jax.random.key(seed)
        k1, k2, k3 = jax.random.split(key, 3)
        fea = jax.random.normal(k1, (N, C, H, WD), dtype=jnp.float32)
        W = jax.random.normal(k2, (C, C, KH, 1), dtype=jnp.float32) * 0.01
        b = jax.random.normal(k3, (C,), dtype=jnp.float32) * 0.01
        return {'fea': fea, 'W': W, 'b': b}
    _L1_conv_all = _L1_conv_setup()
    _L1_conv_in = {k: v for k, v in _L1_conv_all.items() if k in ('W', 'b')}
    del _L1_conv_all

    def _L1_ffn_setup():
        import jax, jax.numpy as jnp
        import numpy as np
        EPS = 1e-05

        def _rmsnorm(x, eps=1e-06):
            return x * jax.lax.rsqrt(jnp.mean(x * x, axis=-1, keepdims=True) + eps)

        def _act_quant(x):
            scale = 127.0 / jnp.clip(jnp.max(jnp.abs(x), axis=-1, keepdims=True), EPS)
            return jnp.clip(jnp.round(x * scale), -32, 127) / scale

        def _weight_quant(w):
            scale = 1.0 / jnp.clip(jnp.mean(jnp.abs(w)), EPS)
            return jnp.clip(jnp.round(w * scale), -1, 1) / scale

        def _ste(a, q):
            return a + jax.lax.stop_gradient(q - a)

        def _bitlinear(x, w):
            xn = _rmsnorm(x)
            xq = _ste(xn, _act_quant(xn))
            wq = _ste(w, _weight_quant(w))
            return jnp.einsum('bsd,hd->bsh', xq, wq)
        key = jax.random.key(seed)
        k_x, k1, k2, k3 = jax.random.split(key, 4)
        B, S, D, H = (4, 1024, 512, 1408)
        return {'x': jax.random.normal(k_x, (B, S, D), dtype=jnp.float32), 'w1': jax.random.normal(k1, (H, D), dtype=jnp.float32) * 0.02, 'w2': jax.random.normal(k2, (H, D), dtype=jnp.float32) * 0.02, 'w3': jax.random.normal(k3, (D, H), dtype=jnp.float32) * 0.02}
    _L1_ffn_all = _L1_ffn_setup()
    _L1_ffn_in = {k: v for k, v in _L1_ffn_all.items() if k in ('w1', 'w2', 'w3')}
    del _L1_ffn_all
    return {'x': x, 'L0_conv_w1': _L0_conv_in['w1'], 'L0_conv_b1': _L0_conv_in['b1'], 'L0_conv_w2': _L0_conv_in['w2'], 'L0_conv_b2': _L0_conv_in['b2'], 'L0_conv_w3': _L0_conv_in['w3'], 'L0_conv_b3': _L0_conv_in['b3'], 'L0_conv_alpha': _L0_conv_in['alpha'], 'L0_ffn_ln_weight': _L0_ffn_in['ln_weight'], 'L0_ffn_router_weight': _L0_ffn_in['router_weight'], 'L0_ffn_gate_up_proj': _L0_ffn_in['gate_up_proj'], 'L0_ffn_down_proj': _L0_ffn_in['down_proj'], 'L0_ffn_shared_gate_w': _L0_ffn_in['shared_gate_w'], 'L0_ffn_shared_up_w': _L0_ffn_in['shared_up_w'], 'L0_ffn_shared_down_w': _L0_ffn_in['shared_down_w'], 'L1_conv_W': _L1_conv_in['W'], 'L1_conv_b': _L1_conv_in['b'], 'L1_ffn_w1': _L1_ffn_in['w1'], 'L1_ffn_w2': _L1_ffn_in['w2'], 'L1_ffn_w3': _L1_ffn_in['w3']}

def reference(x, L0_conv_w1, L0_conv_b1, L0_conv_w2, L0_conv_b2, L0_conv_w3, L0_conv_b3, L0_conv_alpha, L0_ffn_ln_weight, L0_ffn_router_weight, L0_ffn_gate_up_proj, L0_ffn_down_proj, L0_ffn_shared_gate_w, L0_ffn_shared_up_w, L0_ffn_shared_down_w, L1_conv_W, L1_conv_b, L1_ffn_w1, L1_ffn_w2, L1_ffn_w3):
    import jax
    import jax.numpy as jnp

    def _L0_conv_ref(x, w1, b1, w2, b2, w3, b3, alpha):
        import jax, jax.numpy as jnp
        import numpy as np
        C = 512
        RED = 8
        D = C // RED
        n, c, h, w = x.shape
        hw = h * w
        xf = x.reshape(n, c, hw)
        e1 = jax.nn.relu(jnp.einsum('dc,ncp->ndp', w1, xf) + b1[None, :, None])
        e2 = jax.nn.relu(jnp.einsum('dc,ncp->ndp', w2, xf) + b2[None, :, None])
        assembly = jax.nn.relu(jnp.einsum('oc,ncp->nop', w3, xf) + b3[None, :, None])
        scores = jnp.einsum('ndi,ndj->nij', e1, e2)
        attn = jax.nn.softmax(scores, axis=-1)
        out = jnp.einsum('ncj,nij->nci', xf, attn)
        y = alpha[0] * out + assembly
        return y.reshape(n, c, h, w)

    def _L0_ffn_ref(hidden_states, ln_weight, router_weight, gate_up_proj, down_proj, shared_gate_w, shared_up_w, shared_down_w):
        import jax, jax.numpy as jnp
        import numpy as np
        TOP_K = 4
        EPS = 1e-06

        def _rmsnorm(x, w):
            var = jnp.mean(x * x, axis=-1, keepdims=True)
            return x * jax.lax.rsqrt(var + EPS) * w
        B, S, H = hidden_states.shape
        E = router_weight.shape[1]
        x = _rmsnorm(hidden_states, ln_weight).reshape(-1, H)
        T = x.shape[0]
        logits = x @ router_weight
        probs = jax.nn.softmax(logits, axis=-1)
        top_vals, top_idx = jax.lax.top_k(probs, TOP_K)
        aff = jnp.zeros((T, E), x.dtype).at[jnp.arange(T)[:, None], top_idx].set(top_vals)
        gu = jnp.einsum('th,ehi->eti', x, gate_up_proj)
        gate, up = jnp.split(gu, 2, axis=-1)
        h = jax.nn.silu(gate) * up
        expert_out = jnp.einsum('eti,eih->eth', h, down_proj)
        routed = jnp.einsum('te,eth->th', aff, expert_out)
        sh = jax.nn.silu(x @ shared_gate_w) * (x @ shared_up_w)
        shared = sh @ shared_down_w
        return (routed + shared).reshape(B, S, H)

    def _L1_conv_ref(fea, W, b):
        import jax, jax.numpy as jnp
        import numpy as np
        N, C, H, WD = (4, 512, 48, 24)
        KH = 9
        kh = W.shape[2]
        Wm = W[:, :, (kh - 1) // 2, 0]
        bb = b[None, :, None]

        def step(carry, x):
            new = jax.nn.relu(jnp.einsum('oc,ncw->now', Wm, carry) + bb) + x
            return (new, new)
        xs = jnp.moveaxis(fea, 2, 0)
        _, ys = jax.lax.scan(step, xs[0], xs[1:])
        down = jnp.concatenate([xs[:1], ys], axis=0)
        _, ys2 = jax.lax.scan(step, down[-1], down[:-1], reverse=True)
        stack = jnp.concatenate([ys2, down[-1:]], axis=0)
        return jnp.moveaxis(stack, 0, 2)

    def _L1_ffn_ref(x, w1, w2, w3):
        import jax, jax.numpy as jnp
        import numpy as np
        EPS = 1e-05

        def _rmsnorm(x, eps=1e-06):
            return x * jax.lax.rsqrt(jnp.mean(x * x, axis=-1, keepdims=True) + eps)

        def _act_quant(x):
            scale = 127.0 / jnp.clip(jnp.max(jnp.abs(x), axis=-1, keepdims=True), EPS)
            return jnp.clip(jnp.round(x * scale), -32, 127) / scale

        def _weight_quant(w):
            scale = 1.0 / jnp.clip(jnp.mean(jnp.abs(w)), EPS)
            return jnp.clip(jnp.round(w * scale), -1, 1) / scale

        def _ste(a, q):
            return a + jax.lax.stop_gradient(q - a)

        def _bitlinear(x, w):
            xn = _rmsnorm(x)
            xq = _ste(xn, _act_quant(xn))
            wq = _ste(w, _weight_quant(w))
            return jnp.einsum('bsd,hd->bsh', xq, wq)
        gate = jax.nn.silu(_bitlinear(x, w1))
        up = _bitlinear(x, w2)
        return _bitlinear(gate * up, w3)

    def _gn(v, G=32, eps=1e-05):
        B_, C_, H_, W_ = v.shape
        g = v.reshape(B_, G, C_ // G, H_, W_)
        m = jnp.mean(g, axis=(2, 3, 4), keepdims=True)
        s = jnp.var(g, axis=(2, 3, 4), keepdims=True)
        return ((g - m) / jnp.sqrt(s + eps)).reshape(v.shape)

    def _ln_c(v, eps=1e-06):
        m = jnp.mean(v, axis=1, keepdims=True)
        s = jnp.var(v, axis=1, keepdims=True)
        return (v - m) / jnp.sqrt(s + eps)

    def _ln_t(v, eps=1e-05):
        m = jnp.mean(v, axis=-1, keepdims=True)
        s = jnp.var(v, axis=-1, keepdims=True)
        return (v - m) / jnp.sqrt(s + eps)

    def _to_tokens(v):
        B_, C_, H_, W_ = v.shape
        return v.reshape(B_, C_, H_ * W_).transpose(0, 2, 1)

    def _from_tokens(t, like):
        B_, C_, H_, W_ = like.shape
        return t.transpose(0, 2, 1).reshape(B_, C_, H_, W_)
    x = x + _L0_conv_ref(_ln_c(x), L0_conv_w1, L0_conv_b1, L0_conv_w2, L0_conv_b2, L0_conv_w3, L0_conv_b3, L0_conv_alpha)
    t = _to_tokens(x)
    t = t + _L0_ffn_ref(_ln_t(t), L0_ffn_ln_weight, L0_ffn_router_weight, L0_ffn_gate_up_proj, L0_ffn_down_proj, L0_ffn_shared_gate_w, L0_ffn_shared_up_w, L0_ffn_shared_down_w)
    x = _from_tokens(t, x)
    x = x + _L1_conv_ref(_ln_c(x), L1_conv_W, L1_conv_b)
    t = _to_tokens(x)
    t = t + _L1_ffn_ref(_ln_t(t), L1_ffn_w1, L1_ffn_w2, L1_ffn_w3)
    x = _from_tokens(t, x)
    return x

_drawn_inputs = setup_inputs


def setup_inputs(seed=0):
    import zlib

    import numpy as np

    out = dict(_drawn_inputs(seed))
    spreads = {'L0_conv_b1': (0.0, 0.1),
     'L0_conv_b2': (0.0, 0.1),
     'L0_conv_b3': (0.0, 0.1),
     'L0_ffn_ln_weight': (1.0, 0.6)}
    factors = {'L0_ffn_router_weight': 3.97,
     'L0_ffn_gate_up_proj': 3.501,
     'L0_ffn_down_proj': 3.503,
     'L1_conv_b': 29.413}
    for name, (base, spread) in spreads.items():
        noise = np.random.default_rng([zlib.crc32(name.encode()), seed]).standard_normal(out[name].shape)
        drawn = base * np.exp(spread * noise) if base else spread * noise
        out[name] = jnp.asarray(drawn.astype(out[name].dtype))
    for name, factor in factors.items():
        out[name] = (out[name] * factor).astype(out[name].dtype)
    return out
```

```python
from contextlib import ExitStack

import numpy as np

import concourse.bass as bass
from concourse import mybir
from concourse.alu_op_type import AluOpType as ALU

FP32 = mybir.dt.float32
F32R = mybir.dt.float32r
BF16 = mybir.dt.bfloat16
U32 = mybir.dt.uint32
ACT = mybir.ActivationFunctionType
AX = mybir.AxisListType

P = 128
BATCH, C, IMH, IMW = 4, 512, 16, 16
SP = IMH * IMW
TOK = BATCH * SP
NT = TOK // P
KC = C // P
D = 64
EXPERTS, TOPK = 16, 4
FF = 1024
CAP = 320
MAX_ROUNDS = -(-TOK // CAP)
ROUND_SLOTS = EXPERTS * CAP
SLOTS = (MAX_ROUNDS * EXPERTS + 2) * CAP
LN_C_EPS, LN_T_EPS, RMS_EPS = 1e-6, 1e-5, 1e-6


RSQRT_SEED = 1597463007.0


def rsqrt(nc, link, out, v, scale, eps, scratch):
    V, n = nc.vector, out.shape[-1]
    a, t = scratch[:, 0:n], scratch[:, n:2 * n]
    link(V.tensor_scalar(a, v, scale, eps, ALU.mult, ALU.add))
    link(V.tensor_scalar(t.bitcast(U32), a.bitcast(U32), 1, None, ALU.logical_shift_right))
    link(V.tensor_scalar(out.bitcast(U32), t.bitcast(U32), -1.0, RSQRT_SEED, ALU.mult, ALU.add))
    for _ in range(3):
        link(V.tensor_tensor(t, out, out, ALU.mult))
        link(V.scalar_tensor_tensor(t, t, -0.5, a, ALU.mult, ALU.mult))
        link(V.scalar_tensor_tensor(out, t, 1.5, out, ALU.add, ALU.mult))


def attention_and_routing(nc, io, keep):
    ctx = ExitStack()
    with ctx:
        def sb(name, shape, dt=FP32):
            return ctx.enter_context(nc.sbuf_tensor(name, shape, dt))

        def bank(name):
            return ctx.enter_context(nc.psum_tensor(name, [P, 512], FP32))

        def sem(name):
            return ctx.enter_context(nc.semaphore(name))

        x_cm = sb("x_cm", [P, KC, TOK])
        x_tm = keep["x_tm"]
        xn_tm = sb("xn_tm", [P, NT, C])
        xn_cm = sb("xn_cm", [P, KC, TOK])
        w12 = sb("w12", [P, KC, 2 * D])
        w3 = sb("w3", [P, KC, C])
        b12 = sb("b12", [D, 2])
        b3 = sb("b3", [1, C])
        alpha = sb("alpha", [P, 1])
        lnw = sb("lnw", [P, C])
        router = sb("router", [P, KC, EXPERTS])
        stats = sb("stats", [P, NT, 6])
        mv = sb("mv", [P, NT, 2])
        rstd = sb("rstd", [P, NT])
        e12 = sb("e12", [D, 2, 2, SP])
        nmax = sb("nmax", [P, NT])
        prob = sb("prob", [P, 2, SP])
        psum_row = sb("psum_row", [P, NT])
        gain = sb("gain", [P, NT])
        prob_t = sb("prob_t", [P, 2, SP])
        part = sb("part", [P, C])
        stats1 = sb("stats1", [P, NT, 6])
        mv1 = sb("mv1", [P, NT, 2])
        rstd1 = sb("rstd1", [P, NT])
        z = sb("z", [P, 2, C])
        zsq = sb("zsq", [P, C])
        ssq = sb("ssq", [P, NT])
        scratch = sb("scratch", [P, 2])
        rms1 = sb("rms1", [P, NT])
        zn = sb("zn", [P, NT, C])
        zn_cm = sb("zn_cm", [P, 2, KC, P])
        logits = sb("logits", [P, NT, EXPERTS])
        top = sb("top", [P, NT, 8])
        top_at = sb("top_at", [P, NT, 8], U32)
        top_at_f = sb("top_at_f", [P, NT, TOPK])
        neg_top = sb("neg_top", [P, NT])
        elog = sb("elog", [P, NT, EXPERTS])
        esum = sb("esum", [P, NT])
        resum = sb("resum", [P, NT])
        etop = sb("etop", [P, NT, TOPK])
        expert_ids = sb("expert_ids", [P, EXPERTS])
        onehot = sb("onehot", [P, TOPK, NT, EXPERTS])
        mask = sb("mask", [P, NT, EXPERTS])
        before = sb("before", [P, NT, EXPERTS])
        totals = sb("totals", [P, NT, EXPERTS])
        run = sb("run", [P, NT + 1, EXPERTS])
        wraps = sb("wraps", [P, NT, EXPERTS])
        wrap1 = sb("wrap1", [P, NT, EXPERTS])
        slot_e = sb("slot_e", [P, NT, EXPERTS])
        base = sb("base", [P, EXPERTS])
        picked = sb("picked", [P, NT, EXPERTS])
        slot_f = sb("slot_f", [P, NT, TOPK])
        most = sb("most", [P, 1])
        most2 = sb("most2", [P, 4])
        token_ids = sb("token_ids", [P, NT], U32)
        zero_list = sb("zero_list", [P, SLOTS // P], U32)
        upper = sb("upper", [P, P])
        ones = sb("ones", [P, P])
        ident = keep["ident"]
        aff, slots, rounds = keep["aff"], keep["slots"], keep["rounds"]

        pa = [bank("pa0"), bank("pa1")]
        pb = [bank("pb0"), bank("pb1")]
        pe_ = bank("pe_")
        ps = bank("ps")
        pt = bank("pt")
        pg = bank("pg")

        x_in = [sem(f"x_in{n}") for n in range(BATCH)]
        w_in = sem("w_in")
        const_ready = sem("const_ready")
        pool_step = sem("pool_step")
        x_turned = sem("x_turned")
        x_kept = sem("x_kept")
        xn_ready = sem("xn_ready")
        xn_turned = sem("xn_turned")
        xn_cm_ready = sem("xn_cm_ready")
        e_summed = sem("e_summed")
        e_ready = sem("e_ready")
        scored = sem("scored")
        max_ready = sem("max_ready")
        prob_ready = sem("prob_ready")
        prob_turned = sem("prob_turned")
        prob_t_ready = sem("prob_t_ready")
        mixed = sem("mixed")
        x1_ready = sem("x1_ready")
        z_ready = sem("z_ready")
        ssq_ready = sem("ssq_ready")
        zn_ready = sem("zn_ready")
        zn_turned = sem("zn_turned")
        zn_cm_ready = sem("zn_cm_ready")
        routed = sem("routed")
        logits_ready = sem("logits_ready")
        neg_top_ready = sem("neg_top_ready")
        elog_ready = sem("elog_ready")
        mask_ready = sem("mask_ready")
        counted = sem("counted")
        slots_ready = sem("slots_ready")
        zeroed = sem("zeroed")
        zn_out = sem("zn_out")
        listed = sem("listed")
        dve_step = sem("dve_step")

        block = ctx.enter_context(nc.Block())

        @block.sync
        def _(sp):
            for n in range(BATCH):
                sp.dma_start(x_cm[:, :, n * SP:(n + 1) * SP],
                             io["x"][n].rearrange("(k p) h w -> p k (h w)", p=P)).then_inc(x_in[n], 16)
            for t in range(NT):
                sp.wait_ge(zn_ready, t + 1)
                sp.dma_start(io["tokens"][t * P:(t + 1) * P, :], zn[:, t, :]).then_inc(zn_out, 16)
            sp.wait_ge(zn_out, 16 * NT)

        @block.gpsimd
        def _(pool):
            pool.memset(ident[:, :], 0.0).then_inc(pool_step, 1)
            pool.memset(ones[:, :], 1.0).then_inc(pool_step, 1)
            pool.memset(zero_list[:, :], 0).then_inc(pool_step, 1)
            pool.wait_ge(pool_step, 3)
            pool.affine_select(out=ident[:, :], in_=ident[:, :], compare_op=ALU.not_equal, fill=1.0,
                               base=0, pattern=[[-1, P]], channel_multiplier=1).then_inc(const_ready, 1)
            pool.affine_select(out=upper[:, :], in_=ones[:, :], compare_op=ALU.is_gt, fill=0.0,
                               base=0, pattern=[[1, P]], channel_multiplier=-1).then_inc(const_ready, 1)
            pool.iota(expert_ids[:, :], pattern=[[1, EXPERTS]], base=0, channel_multiplier=0,
                      allow_small_or_imprecise_dtypes=True).then_inc(const_ready, 1)
            pool.iota(base[:, :], pattern=[[CAP, EXPERTS]], base=CAP, channel_multiplier=0,
                      allow_small_or_imprecise_dtypes=True).then_inc(const_ready, 1)
            pool.iota(token_ids[:, :], pattern=[[P, NT]], base=0, channel_multiplier=1).then_inc(const_ready, 1)
            pool.dma_start(io["slot_token"].rearrange("(p a) o -> p (a o)", p=P), zero_list[:, :]).then_inc(zeroed, 16)
            pool.wait_ge(zeroed, 16)
            pool.wait_ge(const_ready, 5)
            pool.wait_ge(slots_ready, 1)
            for t in range(NT):
                for k in range(TOPK):
                    pool.indirect_dma_start(
                        out=io["slot_token"], out_offset=bass.IndirectOffsetOnAxis(ap=slots[:, t, k:k + 1], axis=0),
                        in_=token_ids[:, t:t + 1], in_offset=None).then_inc(listed, 16)
            pool.wait_ge(listed, 16 * NT * TOPK)

        @block.scalar
        def _(act):
            act.dma_start(w12[:, :, 0:D], io["w1t"].rearrange("(k p) m -> p k m", p=P)).then_inc(w_in, 16)
            act.dma_start(w12[:, :, D:2 * D], io["w2t"].rearrange("(k p) m -> p k m", p=P)).then_inc(w_in, 16)
            act.dma_start(w3[:, :, :], io["w3t"].rearrange("(k p) m -> p k m", p=P)).then_inc(w_in, 16)
            act.dma_start(b12[:, 0:1], io["b1"].rearrange("(a b) -> a b", b=1)).then_inc(w_in, 16)
            act.dma_start(b12[:, 1:2], io["b2"].rearrange("(a b) -> a b", b=1)).then_inc(w_in, 16)
            act.dma_start(b3[:, :], io["b3"].rearrange("(a b) -> a b", a=1)).then_inc(w_in, 16)
            act.dma_start(alpha[:, :], io["alpha"].rearrange("(a b) -> a b", a=1).to_broadcast([P, 1])).then_inc(w_in, 16)
            act.dma_start(lnw[:, :], io["lnw"].rearrange("(a b) -> a b", a=1).to_broadcast([P, C])).then_inc(w_in, 16)
            act.dma_start(router[:, :, :], io["router"].rearrange("(k p) m -> p k m", p=P)).then_inc(w_in, 16)
            for t in range(NT):
                act.wait_ge(x_turned, t + 1)
                nc.scalar.copy(x_tm[:, t, :], pa[t % 2][:, :]).then_inc(x_kept, 1)
                act.wait_ge(xn_turned, t + 1)
                nc.scalar.copy(xn_cm[:, :, t * P:(t + 1) * P],
                               pb[t % 2][:, :].rearrange("p (k m) -> p k m", k=KC)).then_inc(xn_cm_ready, 1)
            act.wait_ge(w_in, 9 * 16)

            def gate_scalar(s):
                act.wait_ge(zn_turned, s + 1)
                if s >= 2:
                    act.wait_ge(routed, s - 1)
                nc.scalar.copy(zn_cm[:, s % 2, :, :], pg[:, :].rearrange("p (k m) -> p k m", k=KC)).then_inc(zn_cm_ready, 1)
                act.wait_ge(neg_top_ready, s + 1)
                nc.scalar.activation(elog[:, s, :], logits[:, s, :], ACT.Exp, bias=neg_top[:, s:s + 1],
                                     accum_out=esum[:, s:s + 1]).then_inc(elog_ready, 1)
                nc.scalar.activation(etop[:, s, :], top[:, s, 0:TOPK], ACT.Exp,
                                     bias=neg_top[:, s:s + 1]).then_inc(elog_ready, 1)

            for s in range(NT):
                n = s // 2
                if s % 2 == 0:
                    act.wait_ge(e_summed, n + 1)
                    if n >= 2:
                        act.wait_ge(scored, 2 * (n - 1))
                    for j in range(2):
                        nc.scalar.activation(e12[:, n % 2, j, :], pe_[0:D, j * SP:(j + 1) * SP], ACT.Relu,
                                             bias=b12[:, j:j + 1]).then_inc(e_ready, 1)
                act.wait_ge(max_ready, s + 1)
                if s >= 2:
                    act.wait_ge(prob_turned, s - 1)
                nc.scalar.activation(prob[:, s % 2, :], ps[:, 0:SP], ACT.Exp,
                                     bias=nmax[:, s:s + 1], accum_out=psum_row[:, s:s + 1]).then_inc(prob_ready, 1)
                act.wait_ge(prob_turned, s + 1)
                if s >= 2:
                    act.wait_ge(mixed, s - 1)
                nc.scalar.copy(prob_t[:, s % 2, :], pt[:, 0:SP]).then_inc(prob_t_ready, 1)
                if s >= 1:
                    gate_scalar(s - 1)
                act.wait_ge(z_ready, s + 1)
                if s >= 1:
                    act.wait_ge(ssq_ready, s)
                nc.scalar.activation(zsq[:, :], z[:, s % 2, :], ACT.Square,
                                     accum_out=ssq[:, s:s + 1]).then_inc(ssq_ready, 1)
            gate_scalar(NT - 1)

        @block.tensor
        def _(pe):
            pe.wait_ge(const_ready, 2)
            for t in range(NT + 1):
                if t < NT:
                    if t % 2 == 0:
                        pe.wait_ge(x_in[t // 2], 16)
                    if t >= 2:
                        pe.wait_ge(x_kept, t - 1)
                    for k in range(KC):
                        mm = nc.tensor.transpose(pa[t % 2][:, k * P:(k + 1) * P], x_cm[:, k, t * P:(t + 1) * P],
                                                 ident[:, :])
                    mm.then_inc(x_turned, 1)
                if t >= 1:
                    s = t - 1
                    pe.wait_ge(xn_ready, s + 1)
                    if s >= 2:
                        pe.wait_ge(xn_cm_ready, s - 1)
                    for k in range(KC):
                        mm = nc.tensor.transpose(pb[s % 2][:, k * P:(k + 1) * P], xn_tm[:, s, k * P:(k + 1) * P],
                                                 ident[:, :])
                    mm.then_inc(xn_turned, 1)
            pe.wait_ge(w_in, 9 * 16)
            pe.wait_ge(xn_cm_ready, NT)

            def route(s):
                pe.wait_ge(zn_ready, s + 1)
                if s >= 1:
                    pe.wait_ge(logits_ready, s)
                for k in range(KC):
                    mm = nc.tensor.transpose(pg[:, k * P:(k + 1) * P], zn[:, s, k * P:(k + 1) * P], ident[:, :])
                mm.then_inc(zn_turned, 1)
                pe.wait_ge(zn_cm_ready, s + 1)
                for k in range(KC):
                    mm = nc.tensor.matmul(pg[:, 0:EXPERTS], zn_cm[:, s % 2, k, :], router[:, k, :],
                                          start=(k == 0), stop=(k == KC - 1))
                mm.then_inc(routed, 1)

            for s in range(NT):
                n = s // 2
                if s % 2 == 0:
                    if n >= 1:
                        pe.wait_ge(e_ready, 2 * n)
                    for j in range(2):
                        for k in range(KC):
                            mm = nc.tensor.matmul(pe_[0:D, j * SP:(j + 1) * SP], w12[:, k, j * D:(j + 1) * D],
                                                  xn_cm[:, k, n * SP:(n + 1) * SP], start=(k == 0), stop=(k == KC - 1))
                    mm.then_inc(e_summed, 1)
                    pe.wait_ge(e_ready, 2 * n + 2)
                if s >= 1:
                    pe.wait_ge(prob_ready, s)
                i = s % 2
                nc.tensor.matmul(ps[:, 0:SP], e12[:, n % 2, 0, i * P:(i + 1) * P], e12[:, n % 2, 1, :],
                                 start=True, stop=True).then_inc(scored, 1)
                if s >= 2:
                    pe.wait_ge(x1_ready, s - 1)
                nc.tensor.matmul(pa[s % 2][:, :], ones[0:1, :], b3[:, :], start=True, stop=False)
                for k in range(KC):
                    nc.tensor.matmul(pa[s % 2][:, :], xn_cm[:, k, s * P:(s + 1) * P], w3[:, k, :],
                                     start=False, stop=(k == KC - 1))
                pe.wait_ge(prob_ready, s + 1)
                if s >= 1:
                    pe.wait_ge(prob_t_ready, s)
                for j in range(2):
                    mm = nc.tensor.transpose(pt[:, j * P:(j + 1) * P], prob[:, s % 2, j * P:(j + 1) * P], ident[:, :])
                mm.then_inc(prob_turned, 1)
                if s >= 1:
                    route(s - 1)
                pe.wait_ge(prob_t_ready, s + 1)
                for j in range(2):
                    mm = nc.tensor.matmul(pb[s % 2][:, :], prob_t[:, s % 2, j * P:(j + 1) * P], xn_tm[:, 2 * n + j, :],
                                          start=(j == 0), stop=(j == 1))
                mm.then_inc(mixed, 1)
            route(NT - 1)
            pe.wait_ge(mask_ready, 1)
            nc.tensor.matmul(ps[:, 0:P], upper[:, :], mask[:, :, :].rearrange("p t e -> p (t e)"), start=True, stop=True)
            nc.tensor.matmul(ps[:, P:2 * P], ones[:, :], mask[:, :, :].rearrange("p t e -> p (t e)"),
                             start=True, stop=True).then_inc(counted, 1)

        @block.vector
        def _(dve):
            steps = [0]

            def link(ins):
                steps[0] += 1
                ins.then_inc(dve_step, 1)
                dve.wait_ge(dve_step, steps[0])

            V = nc.vector
            for t in range(NT):
                dve.wait_ge(x_kept, t + 1)
                link(V.bn_stats(stats[:, t, :], x_tm[:, t, :]))
                link(V.bn_aggr(mv[:, t, :], stats[:, t, :]))
                rsqrt(nc, link, rstd[:, t:t + 1], mv[:, t, 1:2], 1.0, LN_C_EPS, scratch)
                V.tensor_scalar(xn_tm[:, t, :], x_tm[:, t, :], mv[:, t, 0:1], rstd[:, t:t + 1],
                                ALU.subtract, ALU.mult).then_inc(xn_ready, 1)
            dve.wait_ge(w_in, 9 * 16)
            dve.wait_ge(const_ready, 5)

            def gate(s):
                dve.wait_ge(routed, s + 1)
                V.tensor_copy(logits[:, s, :], pg[:, 0:EXPERTS]).then_inc(logits_ready, 1)
                dve.wait_ge(logits_ready, s + 1)
                link(V.max(top[:, s, :], logits[:, s, :]))
                V.tensor_scalar(neg_top[:, s:s + 1], top[:, s, 0:1], -1.0, None, ALU.mult).then_inc(neg_top_ready, 1)
                V.max_index(top_at[:, s, :], top[:, s, :], logits[:, s, :]).then_inc(dve_step, 1)
                steps[0] += 1

            for s in range(NT):
                dve.wait_ge(scored, s + 1)
                V.tensor_reduce(nmax[:, s:s + 1], ps[:, 0:SP], AX.X, ALU.max,
                                negate=True).then_inc(max_ready, 1)
                dve.wait_ge(prob_ready, s + 1)
                link(V.reciprocal(gain[:, s:s + 1], psum_row[:, s:s + 1]))
                link(V.tensor_tensor(gain[:, s:s + 1], gain[:, s:s + 1], alpha[:, :], ALU.mult))
                if s >= 1:
                    gate(s - 1)
                dve.wait_ge(mixed, s + 1)
                dve.wait_ge(x_kept, s + 1)
                link(V.scalar_tensor_tensor(part[:, :], pa[s % 2][:, :], 0.0, x_tm[:, s, :], ALU.max, ALU.add))
                V.scalar_tensor_tensor(x_tm[:, s, :], pb[s % 2][:, :], gain[:, s:s + 1], part[:, :],
                                       ALU.mult, ALU.add).then_inc(x1_ready, 1)
                dve.wait_ge(x1_ready, s + 1)
                link(V.bn_stats(stats1[:, s, :], x_tm[:, s, :]))
                link(V.bn_aggr(mv1[:, s, :], stats1[:, s, :]))
                rsqrt(nc, link, rstd1[:, s:s + 1], mv1[:, s, 1:2], 1.0, LN_T_EPS, scratch)
                V.tensor_scalar(z[:, s % 2, :], x_tm[:, s, :], mv1[:, s, 0:1], rstd1[:, s:s + 1],
                                ALU.subtract, ALU.mult).then_inc(z_ready, 1)
                dve.wait_ge(z_ready, s + 1)
                dve.wait_ge(ssq_ready, s + 1)
                rsqrt(nc, link, rms1[:, s:s + 1], ssq[:, s:s + 1], 1.0 / C, RMS_EPS, scratch)
                V.scalar_tensor_tensor(zn[:, s, :], z[:, s % 2, :], rms1[:, s:s + 1], lnw[:, :],
                                       ALU.mult, ALU.mult).then_inc(zn_ready, 1)
            gate(NT - 1)
            dve.wait_ge(dve_step, steps[0])
            dve.wait_ge(elog_ready, 2 * NT)
            link(V.reciprocal(resum[:, :], esum[:, :]))
            link(V.tensor_tensor(aff[:, :, :], etop[:, :, :],
                                 resum[:, :].rearrange("p (t o) -> p t o", o=1).to_broadcast([P, NT, TOPK]), ALU.mult))
            link(V.tensor_copy(top_at_f[:, :, :], top_at[:, :, 0:TOPK]))
            for k in range(TOPK):
                link(V.tensor_tensor(onehot[:, k, :, :],
                                     top_at_f[:, :, k:k + 1].to_broadcast([P, NT, EXPERTS]),
                                     expert_ids[:, :].rearrange("p (o e) -> p o e", o=1).to_broadcast([P, NT, EXPERTS]),
                                     ALU.is_equal))
            link(V.tensor_tensor(mask[:, :, :], onehot[:, 0, :, :], onehot[:, 1, :, :], ALU.add))
            link(V.tensor_tensor(mask[:, :, :], mask[:, :, :], onehot[:, 2, :, :], ALU.add))
            V.tensor_tensor(mask[:, :, :], mask[:, :, :], onehot[:, 3, :, :], ALU.add).then_inc(mask_ready, 1)
            link(V.memset(run[:, 0, :], 0.0))
            dve.wait_ge(counted, 1)
            link(V.tensor_copy(totals[:, :, :], ps[:, P:2 * P].rearrange("p (t e) -> p t e", e=EXPERTS)))
            for t in range(NT):
                link(V.tensor_tensor(run[:, t + 1, :], run[:, t, :], totals[:, t, :], ALU.add))
            link(V.tensor_tensor(before[:, :, :], ps[:, 0:P].rearrange("p (t e) -> p t e", e=EXPERTS),
                                 run[:, 0:NT, :], ALU.add))
            link(V.tensor_tensor(slot_e[:, :, :], before[:, :, :],
                                 base[:, :].rearrange("p (o e) -> p o e", o=1).to_broadcast([P, NT, EXPERTS]), ALU.add))
            for r in range(1, MAX_ROUNDS):
                link(V.tensor_scalar(wraps[:, :, :], before[:, :, :], float(r * CAP), float(ROUND_SLOTS - CAP),
                                     ALU.is_ge, ALU.mult))
                link(V.tensor_tensor(slot_e[:, :, :], slot_e[:, :, :], wraps[:, :, :], ALU.add))
            for k in range(TOPK):
                link(V.tensor_tensor(picked[:, :, :], onehot[:, k, :, :], slot_e[:, :, :], ALU.mult))
                link(V.tensor_reduce(slot_f[:, :, k:k + 1], picked[:, :, :], AX.X, ALU.add))
            link(V.tensor_copy(slots[:, :, :], slot_f[:, :, :]))
            link(V.tensor_reduce(most[:, :], run[:, NT, :], AX.X, ALU.max))
            for r in range(1, MAX_ROUNDS):
                link(V.tensor_scalar(most2[:, r:r + 1], most[:, :], float(r * CAP), None, ALU.is_gt))
            link(V.memset(most2[:, 0:1], 1.0))
            link(V.tensor_reduce(most[:, :], most2[:, :], AX.X, ALU.add))
            V.tensor_copy(rounds[:, :], most[:, :]).then_inc(slots_ready, 1)


FH = FF // P
PIECE = 2048
PIECES = 6
RING = 3
HALF = TOK // 2
SHARED_UNITS = TOK // HALF
DOWN_K = 4


def tiles_of(n):
    return [min(P, n - j * P) for j in range(-(-n // P))]


def experts(nc, io, keep):
    ctx = ExitStack()
    with ctx:
        def sb(name, shape, dt=FP32):
            return ctx.enter_context(nc.sbuf_tensor(name, shape, dt))

        def bank(name):
            return ctx.enter_context(nc.psum_tensor(name, [P, 512], FP32))

        def sem(name):
            return ctx.enter_context(nc.semaphore(name))

        x_tm, ident, rounds = keep["x_tm"], keep["ident"], keep["rounds"]
        raw = sb("raw", [P, RING, PIECE])
        w_hi = sb("w_hi", [P, RING, PIECE], F32R)
        w_lo = sb("w_lo", [P, RING, PIECE], F32R)
        rows = sb("rows", [P, 4, C])
        slot_ids = sb("slot_ids", [P, 4], U32)
        x_hi = sb("x_hi", [P, KC, HALF], F32R)
        x_lo = sb("x_lo", [P, KC, HALF], F32R)
        gated = sb("gated", [P, 2, HALF])
        hid = sb("hid", [P, 2, HALF])
        h_hi = sb("h_hi", [P, FH, HALF], F32R)
        h_lo = sb("h_lo", [P, FH, HALF], F32R)
        y_sb = sb("y_sb", [P, 3, C])

        gate_ps = [bank("gate_ps0"), bank("gate_ps1")]
        up_ps = [bank("up_ps0"), bank("up_ps1")]
        y_ps = [bank(f"y_ps{j}") for j in range(4)]
        turn_ps = [gate_ps[0], up_ps[0], gate_ps[1], up_ps[1]]

        raw_in = [sem(f"raw_in{j}") for j in range(RING)]
        hi_ready = sem("hi_ready")
        split_ready = sem("split_ready")
        half_summed = sem("half_summed")
        shared_in = sem("shared_in")
        ids_in = sem("ids_in")
        rows_in = sem("rows_in")
        rows_turned = sem("rows_turned")
        x_hi_ready = sem("x_hi_ready")
        x_lo_ready = sem("x_lo_ready")
        gu_summed = sem("gu_summed")
        silu_ready = sem("silu_ready")
        hid_ready = sem("hid_ready")
        h_hi_ready = sem("h_hi_ready")
        h_ready = sem("h_ready")
        y_summed = sem("y_summed")
        y_copied = sem("y_copied")
        y_added = sem("y_added")
        y_out = sem("y_out")
        y_free = sem("y_free")

        block = ctx.enter_context(nc.Block())
        ROUTED = tiles_of(CAP)
        SHARED = tiles_of(HALF)

        def gu_view(buf, slot):
            return buf[:, slot, :].rearrange("p (k g c) -> p k g c", k=KC, g=2)

        def down_view(buf, slot):
            return buf[:, slot, :].rearrange("p (k c) -> p k c", k=DOWN_K)

        def rounds_of(eng):
            return eng.value_load(rounds[0:1, 0:1], min_val=1, max_val=MAX_ROUNDS)

        @block.sync
        def _(sp):
            def load(U, j, sources):
                slot = j % RING
                sp.wait_ge(split_ready, U * PIECES + j + 1)
                for dst, src in sources:
                    sp.dma_start(dst, src).then_inc(raw_in[slot], 16)

            def pieces(U, gate, up, down):
                for j in range(PIECES):
                    if j < 4:
                        v = gu_view(raw, j % RING)
                        cols = slice(j * 256, (j + 1) * 256)
                        load(U, j, [(v[:, :, 0, :], gate[:, :, cols]), (v[:, :, 1, :], up[:, :, cols])])
                    else:
                        v = down_view(raw, j % RING)
                        k = (j - 4) * DOWN_K
                        load(U, j, [(v[:, 0:2, :], down[:, k:k + 2, :]), (v[:, 2:4, :], down[:, k + 2:k + 4, :])])

            for U in range(SHARED_UNITS):
                if U:
                    sp.wait_ge(rows_turned, KC * U)
                sp.dma_start(rows[:, :, :], io["tokens"][U * HALF:(U + 1) * HALF, :]
                             .rearrange("(j p) c -> p j c", p=P)).then_inc(shared_in, 16)
                pieces(U, io["sgate"].rearrange("(k p) f -> p k f", p=P), io["sup"].rearrange("(k p) f -> p k f", p=P),
                       io["sdown"].rearrange("(k p) c -> p k c", p=P))
            n = rounds_of(sp)
            with sp.Fori(0, n) as r:
                with sp.Fori(0, EXPERTS) as e:
                    gu = io["gate_up"][bass.ds(e, 1), :, :].rearrange("o (k p) f -> p (o k) f", p=P)
                    dn = io["down"][bass.ds(e, 1), :, :].rearrange("o (k p) c -> p (o k) c", p=P)
                    pieces(r * EXPERTS + e + SHARED_UNITS, gu[:, :, 0:FF], gu[:, :, FF:2 * FF], dn)

        @block.gpsimd
        def _(pool):
            def gather(u):
                pool.wait_ge(rows_turned, (u + SHARED_UNITS) * KC)
                base = (u + 1) * CAP
                ids = io["slot_token"]
                pool.dma_start(slot_ids[:, 0:2], ids[bass.ds(base, 2 * P), :]
                               .rearrange("(p j) o -> p (j o)", p=P)).then_inc(ids_in, 16)
                pool.dma_start(slot_ids[0:CAP - 2 * P, 2:3], ids[bass.ds(base + 2 * P, CAP - 2 * P), :]).then_inc(ids_in, 16)
                pool.wait_ge(ids_in, u * 32 + 32)
                pool.nop(nofuse=True)
                for j, w in enumerate(ROUTED):
                    pool.indirect_dma_start(
                        out=rows[0:w, j, :], out_offset=None, in_=io["tokens"],
                        in_offset=bass.IndirectOffsetOnAxis(ap=slot_ids[0:w, j:j + 1], axis=0)).then_inc(rows_in, 16)

            def store(v):
                pool.wait_ge(y_copied, v * len(ROUTED) + len(ROUTED))
                base = v * CAP
                pool.dma_start(io["slot_y"][bass.ds(base, 2 * P), :].rearrange("(p j) c -> p j c", p=P),
                               y_sb[:, 0:2, :]).then_inc(y_out, 16)
                pool.dma_start(io["slot_y"][bass.ds(base + 2 * P, CAP - 2 * P), :],
                               y_sb[0:CAP - 2 * P, 2, :]).then_inc(y_out, 16)
                pool.wait_ge(y_out, v * 32 + 32)
                pool.sem_inc(y_free, 1)

            pool.sem_inc(y_free, 1)
            gather(0)
            n = rounds_of(pool)
            with pool.Fori(0, n * EXPERTS) as u:
                gather(u + 1)
                store(u)
            store(n * EXPERTS)
            pool.wait_ge(rows_in, n * (EXPERTS * 48) + 48)

        @block.scalar
        def _(act):
            S = nc.scalar

            def hi(U, j):
                act.wait_ge(raw_in[j % RING], (U * (PIECES // RING) + j // RING) * 32 + 32)
                if j == 0:
                    act.wait_ge(gu_summed, U * FH)
                elif j == 1:
                    act.wait_ge(half_summed, U)
                elif j == 2:
                    act.wait_ge(y_summed, U)
                else:
                    act.wait_ge(gu_summed, U * FH + 2 * (j - 2))
                S.copy(w_hi[:, j % RING, :], raw[:, j % RING, :]).then_inc(hi_ready, 1)

            def hidden(U, m, n):
                act.wait_ge(gu_summed, U * FH + m + 1)
                S.activation(gated[:, m % 2, 0:n], gate_ps[m % 2][:, 0:n], ACT.Silu).then_inc(silu_ready, 1)
                act.wait_ge(hid_ready, U * FH + m + 1 + 2)
                S.copy(h_hi[:, m, 0:n], hid[:, m % 2, 0:n]).then_inc(h_hi_ready, 1)

            def turn(U, n):
                for k in range(KC):
                    act.wait_ge(rows_turned, U * KC + k + 1)
                    S.copy(x_hi[:, k, 0:n], turn_ps[k][:, 0:n]).then_inc(x_hi_ready, 1)

            def empty(v):
                act.wait_ge(y_summed, v + SHARED_UNITS)
                act.wait_ge(y_free, v + 1)
                for j, w in enumerate(ROUTED):
                    S.copy(y_sb[0:w, j, :], y_ps[j][0:w, :]).then_inc(y_copied, 1)

            def unit(U, n, n_next, after_two):
                hi(U, 0)
                hi(U, 1)
                after_two()
                for j in range(4):
                    hidden(U, 2 * j, n)
                    hidden(U, 2 * j + 1, n)
                    hi(U, j + 2)
                turn(U + 1, n_next)

            turn(0, HALF)
            for U in range(SHARED_UNITS):
                unit(U, HALF, HALF if U + 1 < SHARED_UNITS else CAP, lambda: None)
            act.wait_ge(y_added, SHARED_UNITS)
            n = rounds_of(act)
            with act.Fori(0, n * EXPERTS) as u:
                unit(u + SHARED_UNITS, CAP, CAP, lambda: empty(u))
            empty(n * EXPERTS)

        @block.vector
        def _(dve):
            V = nc.vector

            def lo(U, j):
                dve.wait_ge(hi_ready, U * PIECES + j + 1)
                V.tensor_tensor(w_lo[:, j % RING, :], raw[:, j % RING, :], w_hi[:, j % RING, :].bitcast(FP32),
                                ALU.subtract).then_inc(split_ready, 1)

            def hidden(U, m, n):
                dve.wait_ge(silu_ready, U * FH + m + 1)
                V.tensor_tensor(hid[:, m % 2, 0:n], gated[:, m % 2, 0:n], up_ps[m % 2][:, 0:n],
                                ALU.mult).then_inc(hid_ready, 1)
                dve.wait_ge(h_hi_ready, U * FH + m + 1)
                V.tensor_tensor(h_lo[:, m, 0:n], hid[:, m % 2, 0:n], h_hi[:, m, 0:n].bitcast(FP32),
                                ALU.subtract).then_inc(h_ready, 1)

            def turn(U, n):
                for k in range(KC):
                    dve.wait_ge(x_hi_ready, U * KC + k + 1)
                    V.tensor_tensor(x_lo[:, k, 0:n], turn_ps[k][:, 0:n], x_hi[:, k, 0:n].bitcast(FP32),
                                    ALU.subtract).then_inc(x_lo_ready, 1)

            def add_shared(U):
                dve.wait_ge(y_summed, U + 1)
                for j in range(len(SHARED)):
                    t = U * len(SHARED) + j
                    last = V.tensor_tensor(x_tm[:, t, :], x_tm[:, t, :], y_ps[j][:, :], ALU.add)
                last.then_inc(y_added, 1)

            def unit(U, n, n_next, after_two):
                lo(U, 0)
                lo(U, 1)
                after_two()
                for j in range(4):
                    hidden(U, 2 * j, n)
                    hidden(U, 2 * j + 1, n)
                    lo(U, j + 2)
                turn(U + 1, n_next)

            dve.sem_inc(split_ready, RING)
            dve.sem_inc(hid_ready, 2)
            turn(0, HALF)
            for U in range(SHARED_UNITS):
                unit(U, HALF, HALF if U + 1 < SHARED_UNITS else CAP, (lambda: None) if U == 0 else (lambda: add_shared(0)))
            add_shared(SHARED_UNITS - 1)
            n = rounds_of(dve)
            with dve.Fori(0, n * EXPERTS) as u:
                unit(u + SHARED_UNITS, CAP, CAP, lambda: None)

        @block.tensor
        def _(pe):
            T = nc.tensor

            def turn(tiles):
                for k in range(KC):
                    for j, w in enumerate(tiles):
                        mm = T.transpose(turn_ps[k][:, j * P:j * P + w], rows[0:w, j, k * P:(k + 1) * P], ident[0:w, 0:w])
                    mm.then_inc(rows_turned, 1)

            def three(out, hi_a, lo_a, hi_b, lo_b, first, last):
                T.matmul(out, hi_a, hi_b, start=first, stop=False)
                T.matmul(out, hi_a, lo_b, start=False, stop=False)
                return T.matmul(out, lo_a, hi_b, start=False, stop=last)

            def unit(U, tiles, next_tiles, next_rows, y_free):
                n = sum(tiles)
                pe.wait_ge(x_lo_ready, U * KC + KC)
                for j in range(4):
                    pe.wait_ge(split_ready, U * PIECES + j + 1 + RING)
                    hi_w, lo_w = gu_view(w_hi, j % RING), gu_view(w_lo, j % RING)
                    for i in range(2):
                        m = 2 * j + i
                        pe.wait_ge(hid_ready, U * FH + m + 1)
                        for g, ps in enumerate((gate_ps[i], up_ps[i])):
                            for k in range(KC):
                                c = slice(i * P, (i + 1) * P)
                                mm = three(ps[:, 0:n], hi_w[:, k, g, c], lo_w[:, k, g, c], x_hi[:, k, 0:n], x_lo[:, k, 0:n],
                                           k == 0, k == KC - 1)
                        mm.then_inc(gu_summed, 1)
                for d in range(2):
                    j = 4 + d
                    pe.wait_ge(split_ready, U * PIECES + j + 1 + RING)
                    if d == 0 and y_free:
                        pe.wait_ge(*y_free)
                    hi_w, lo_w = down_view(w_hi, j % RING), down_view(w_lo, j % RING)
                    for k in range(DOWN_K):
                        m = d * DOWN_K + k
                        pe.wait_ge(h_ready, U * FH + m + 1)
                        for i, w in enumerate(tiles):
                            c = slice(i * P, i * P + w)
                            mm = three(y_ps[i][0:w, :], h_hi[:, m, c], h_lo[:, m, c], hi_w[:, k, :], lo_w[:, k, :],
                                       m == 0, m == FH - 1)
                    if d == 0:
                        mm.then_inc(half_summed, 1)
                        pe.wait_ge(h_ready, U * FH + FH)
                        pe.wait_ge(next_rows[0], next_rows[1])
                        turn(next_tiles)
                    else:
                        mm.then_inc(y_summed, 1)

            pe.wait_ge(shared_in, 16)
            turn(SHARED)
            for U in range(SHARED_UNITS):
                if U + 1 < SHARED_UNITS:
                    unit(U, SHARED, SHARED, (shared_in, 16 * (U + 2)), U and (y_added, U))
                else:
                    unit(U, SHARED, ROUTED, (rows_in, 16 * len(ROUTED)), U and (y_added, U))
            pe.wait_ge(y_added, SHARED_UNITS)
            n = rounds_of(pe)
            with pe.Fori(0, n * EXPERTS) as u:
                unit(u + SHARED_UNITS, ROUTED, ROUTED, (rows_in, (u + 2) * (16 * len(ROUTED))),
                     (y_copied, (u + 1) * len(ROUTED)))


def combine(nc, io, keep):
    ctx = ExitStack()
    with ctx:
        NG = 4
        got = ctx.enter_context(nc.sbuf_tensor("got", [P, NG, C], FP32))
        got_in = [ctx.enter_context(nc.semaphore(f"got_in{j}")) for j in range(NG)]
        added = ctx.enter_context(nc.semaphore("added"))
        block = ctx.enter_context(nc.Block())
        x_tm, aff, slots = keep["x_tm"], keep["aff"], keep["slots"]

        @block.gpsimd
        def _(pool):
            def gather(source):
                for i in range(NT * TOPK):
                    t, k = divmod(i, TOPK)
                    if i >= NG:
                        pool.wait_ge(added, i - NG + 1)
                    pool.indirect_dma_start(
                        out=got[:, i % NG, :], out_offset=None, in_=source,
                        in_offset=bass.IndirectOffsetOnAxis(ap=slots[:, t, k:k + 1], axis=0)).then_inc(got_in[i % NG], 16)

            n = pool.value_load(keep["rounds"][0:1, 0:1], min_val=1, max_val=MAX_ROUNDS)
            with pool.If(n < 2):
                gather(io["slot_y"][0:ROUND_SLOTS + CAP, :])
            with pool.Else():
                gather(io["slot_y"])

        @block.vector
        def _(dve):
            for i in range(NT * TOPK):
                t, k = divmod(i, TOPK)
                dve.wait_ge(got_in[i % NG], 16 * (i // NG + 1))
                if k:
                    dve.wait_ge(added, i)
                nc.vector.scalar_tensor_tensor(x_tm[:, t, :], got[:, i % NG, :], aff[:, t, k:k + 1], x_tm[:, t, :],
                                               ALU.mult, ALU.add).then_inc(added, 1)


W1, W3 = 1408, 1408 // P
ROUND = 12582912.0
QEPS = 1e-5
SIDE = BATCH * IMW


def scan(nc, io, keep):
    ctx = ExitStack()
    with ctx:
        def sb(name, shape, dt=FP32):
            return ctx.enter_context(nc.sbuf_tensor(name, shape, dt))

        def bank(name):
            return ctx.enter_context(nc.psum_tensor(name, [P, 512], FP32))

        def sem(name):
            return ctx.enter_context(nc.semaphore(name))

        x_tm, ident, feat = keep["x_tm"], keep["ident"], keep["feat"]
        ternary, inv_ws = keep["ternary"], keep["inv_ws"]
        conv = sb("conv", [P, KC, C])
        conv_b = sb("conv_b", [1, C])
        ones_row = sb("ones_row", [1, SIDE])
        ones_sq = sb("ones_sq", [P, P])
        st = sb("st", [P, NT, 6])
        mv = sb("mv2", [P, NT, 2])
        rstd = sb("rstd2", [P, NT])
        scratch = sb("scratch2", [P, 2 * NT])
        xc = sb("xc", [P, 2, C])
        weights = sb("weights", [P, 3, KC * W1])
        scaled = sb("scaled", [P, 2, KC * W1])
        abs_sum = sb("abs_sum", [P, 3])
        w_scale = sb("w_scale", [P, 3])

        step_ps = [[bank(f"step_ps{a}{b}") for b in range(2)] for a in range(2)]
        turn_ps = [bank("turn2_ps0"), bank("turn2_ps1")]
        sum_ps = bank("sum_ps")

        conv_in = sem("conv_in")
        w_in = [sem(f"w_in{i}") for i in range(3)]
        ones_ready = sem("ones_ready")
        xc_ready = sem("xc_ready")
        xc_turned = sem("xc_turned")
        feat_ready = sem("feat_ready")
        stepped = sem("stepped")
        scanned = sem("scanned")
        abs_ready = sem("abs_ready")
        abs_summed = sem("abs_summed")
        scale_ready = sem("scale_ready")
        clipped = sem("clipped")
        shifted = sem("shifted")
        ternary_ready = sem("ternary_ready")
        dve_step = sem("dve_step2")
        block = ctx.enter_context(nc.Block())

        rows = feat[:, :, :].rearrange("p k (n h w) -> p k n h w", n=BATCH, h=IMH)

        def steps(eng, one):
            with eng.Fori(0, (IMH - 2) // 2) as i:
                one(2 * i, 2 * i, 2 * i + 1, 0)
                one(2 * i + 1, 2 * i + 1, 2 * i + 2, 1)
            one(IMH - 2, IMH - 2, IMH - 1, 0)
            one(IMH - 1, IMH - 1, IMH - 2, 1)
            with eng.Fori(0, (IMH - 2) // 2) as i:
                one(2 * i + IMH, IMH - 2 - 2 * i, IMH - 3 - 2 * i, 0)
                one(2 * i + IMH + 1, IMH - 3 - 2 * i, IMH - 4 - 2 * i, 1)

        @block.sync
        def _(sp):
            sp.dma_start(conv[:, :, :], io["conv_w"].rearrange("(k p) m -> p k m", p=P)).then_inc(conv_in, 16)
            sp.dma_start(conv_b[:, :], io["conv_b"].rearrange("(a b) -> a b", a=1)).then_inc(conv_in, 16)
            for i, name in enumerate(("f1", "f2", "f3")):
                sp.dma_start(weights[:, i, :].rearrange("p (k m) -> p k m", m=io[name].shape[1]),
                             io[name].rearrange("(k p) m -> p k m", p=P)).then_inc(w_in[i], 16)

        @block.gpsimd
        def _(pool):
            pool.memset(ones_row[:, :], 1.0).then_inc(ones_ready, 1)
            pool.memset(ones_sq[:, :], 1.0).then_inc(ones_ready, 1)
            pool.wait_ge(scale_ready, 1)
            for i in range(3):
                if i >= 2:
                    pool.wait_ge(ternary_ready, i - 1)
                nc.gpsimd.tensor_scalar(scaled[:, i % 2, :], weights[:, i, :], w_scale[:, i:i + 1], 1.0,
                                        ALU.mult, ALU.min).then_inc(clipped, 1)
                pool.wait_ge(clipped, i + 1)
                nc.gpsimd.tensor_scalar(scaled[:, i % 2, :], scaled[:, i % 2, :], -1.0, ROUND,
                                        ALU.max, ALU.add).then_inc(shifted, 1)

        @block.scalar
        def _(act):
            for t in range(NT):
                act.wait_ge(xc_turned, t + 1)
                nc.scalar.copy(feat[:, :, t * P:(t + 1) * P],
                               turn_ps[t % 2][:, :].rearrange("p (k m) -> p k m", k=KC)).then_inc(feat_ready, 1)
            for i in range(3):
                act.wait_ge(w_in[i], 16)
                if i:
                    act.wait_ge(abs_ready, i)
                nc.scalar.activation(scaled[:, 0, :], weights[:, i, :], ACT.Abs,
                                     accum_out=abs_sum[:, i:i + 1]).then_inc(abs_ready, 1)
            for i in range(3):
                act.wait_ge(shifted, i + 1)
                nc.scalar.activation(ternary[:, i, :], scaled[:, i % 2, :], ACT.Copy, bias=-ROUND).then_inc(ternary_ready, 1)

        @block.tensor
        def _(pe):
            T = nc.tensor
            for t in range(NT):
                pe.wait_ge(xc_ready, t + 1)
                if t >= 2:
                    pe.wait_ge(feat_ready, t - 1)
                for k in range(KC):
                    mm = T.transpose(turn_ps[t % 2][:, k * P:(k + 1) * P], xc[:, t % 2, k * P:(k + 1) * P], ident[:, :])
                mm.then_inc(xc_turned, 1)
            pe.wait_ge(ones_ready, 2)
            pe.wait_ge(conv_in, 32)
            pe.wait_ge(feat_ready, NT)

            def one(s, source, new, parity):
                pe.wait_ge(scanned, 2 * s + 1)
                for m in range(KC):
                    ps = step_ps[parity][m // 2]
                    T.matmul(ps[:, (m % 2) * SIDE:(m % 2 + 1) * SIDE], conv_b[:, m * P:(m + 1) * P], ones_row[:, :],
                             start=(m % 2 == 0), stop=False, skip_group_check=True)
                for k in range(KC):
                    if k % 2 == 0:
                        pe.wait_ge(scanned, 2 * s + k // 2 + 2)
                        pe.nop(nofuse=True)
                    for m in range(KC):
                        ps = step_ps[parity][m // 2]
                        mm = T.matmul(ps[:, (m % 2) * SIDE:(m % 2 + 1) * SIDE].rearrange("p (n w) -> p n w", n=BATCH),
                                      conv[:, k, m * P:(m + 1) * P], rows[:, k, :, source, :],
                                      start=False, stop=(k == KC - 1), skip_group_check=True)
                        if k == KC - 1 and m % 2:
                            mm.then_inc(stepped, 1)

            steps(pe, one)
            pe.wait_ge(abs_ready, 3)
            T.matmul(sum_ps[:, 0:3], ones_sq[:, :], abs_sum[:, :], start=True, stop=True).then_inc(abs_summed, 1)

        @block.vector
        def _(dve):
            V = nc.vector
            done = [0]

            def link(ins):
                done[0] += 1
                ins.then_inc(dve_step, 1)
                dve.wait_ge(dve_step, done[0])

            dve.sem_inc(scanned, 3)
            for t in range(NT):
                link(V.bn_stats(st[:, t, :], x_tm[:, t, :]))
                link(V.bn_aggr(mv[:, t, :], st[:, t, :]))
            rsqrt(nc, link, rstd[:, :], mv[:, :, 1], 1.0, LN_C_EPS, scratch)
            for t in range(NT):
                if t >= 2:
                    dve.wait_ge(xc_turned, t - 1)
                V.tensor_scalar(xc[:, t % 2, :], x_tm[:, t, :], mv[:, t, 0:1], rstd[:, t:t + 1],
                                ALU.subtract, ALU.mult).then_inc(xc_ready, 1)
            dve.wait_ge(feat_ready, NT)

            def one(s, source, new, parity):
                for g in range(2):
                    dve.wait_ge(stepped, 2 * s + g + 1)
                    dve.nop(nofuse=True)
                    for m in (2 * g, 2 * g + 1):
                        ps = step_ps[parity][g][:, (m % 2) * SIDE:(m % 2 + 1) * SIDE].rearrange("p (n w) -> p n w", n=BATCH)
                        ins = V.scalar_tensor_tensor(rows[:, m, :, new, :], ps, 0.0, rows[:, m, :, new, :],
                                                     ALU.max, ALU.add)
                    ins.then_inc(scanned, 1)

            steps(dve, one)
            dve.wait_ge(abs_summed, 1)
            link(V.tensor_scalar(inv_ws[:, :], sum_ps[:, 0:3], 1.0 / (C * W1), QEPS, ALU.mult, ALU.max))
            V.reciprocal(w_scale[:, :], inv_ws[:, :]).then_inc(scale_ready, 1)


def ternary_ffn(nc, io, keep):
    ctx = ExitStack()
    with ctx:
        def sb(name, shape, dt=FP32):
            return ctx.enter_context(nc.sbuf_tensor(name, shape, dt))

        def bank(name):
            return ctx.enter_context(nc.psum_tensor(name, [P, 512], FP32))

        def sem(name):
            return ctx.enter_context(nc.semaphore(name))

        x_tm, ident, feat = keep["x_tm"], keep["ident"], keep["feat"]
        ternary, inv_ws = keep["ternary"], keep["inv_ws"]
        ident_b = sb("ident_b", [P, P], BF16)
        st = sb("st3", [P, NT, 6])
        mv = sb("mv3", [P, NT, 2])
        rstd = sb("rstd3", [P, NT])
        scratch = sb("scratch3", [P, 2])
        z = sb("z3", [P, 2, C])
        zsq = sb("zsq3", [P, C])
        stat = sb("stat", [P, NT, 16])
        zr = sb("zr", [P, C])
        q = sb("q", [P, 2, C], BF16)
        q_cm = sb("q_cm", [P, 2, KC, P], BF16)
        silu = sb("silu", [P, 2, 512])
        h = sb("h", [P, 2, W1])
        hsq = sb("hsq", [P, W1])
        hr = sb("hr", [P, 2, W1])
        hq = sb("hq", [P, 2, W1], BF16)
        h_cm = sb("h_cm", [P, 2, W3, P], BF16)
        out_cm = sb("out_cm", [P, KC, TOK])

        gu_ps = [bank("g0"), bank("u0"), bank("g1"), bank("u1")]
        ht_ps = [bank("ht0"), bank("ht1")]
        x_ps = bank("x_ps")
        y_ps = bank("y3_ps")

        ident_ready = sem("ident_ready")
        stack_turned = sem("stack_turned")
        x3_ready = sem("x3_ready")
        z_ready = sem("z3_ready")
        zsq_ready = sem("zsq3_ready")
        q_ready = sem("q_ready")
        q_turned = sem("q_turned")
        q_cm_ready = sem("q_cm_ready")
        gu_summed = sem("gu3_summed")
        silu_ready = sem("silu3_ready")
        h_ready = sem("h3_ready")
        hsq_ready = sem("hsq_ready")
        hscale_ready = sem("hscale_ready")
        hr_ready = sem("hr_ready")
        hq_ready = sem("hq_ready")
        h_turned = sem("h_turned")
        h_cm_ready = sem("h_cm_ready")
        y_summed = sem("y3_summed")
        x4_ready = sem("x4_ready")
        x4_turned = sem("x4_turned")
        out_ready = sem("out_ready")
        out_sent = sem("out_sent")
        dve_step = sem("dve_step3")
        block = ctx.enter_context(nc.Block())

        PARTS = [(0, 512), (512, 512), (1024, 384)]
        w1 = ternary[:, 0, :].rearrange("p (k m) -> p k m", m=W1)
        w2 = ternary[:, 1, :].rearrange("p (k m) -> p k m", m=W1)
        w3 = ternary[:, 2, :].rearrange("p (k m) -> p k m", m=C)
        INV_Q, Q, G_SCALE, U_SCALE, HMAX, HSS, HRMS, HA, HQ, Y_SCALE, ZMAX, ZSS, ZRMS, ZA = range(14)

        def col(t, i):
            return stat[:, t, i:i + 1]

        def half(ps, n=512):
            return ps[:, :].bitcast(BF16)[:, 0:n]

        @block.sync
        def _(sp):
            for n in range(BATCH):
                sp.wait_ge(out_ready, 2 * n + 2)
                sp.dma_start(io["out"][n].rearrange("(k p) h w -> p k (h w)", p=P),
                             out_cm[:, :, n * SP:(n + 1) * SP]).then_inc(out_sent, 16)
            sp.wait_ge(out_sent, 16 * BATCH)

        @block.scalar
        def _(act):
            S = nc.scalar
            S.copy(ident_b[:, :], ident[:, :]).then_inc(ident_ready, 1)

            def square_z(t):
                act.wait_ge(z_ready, t + 1)
                if t:
                    act.wait_ge(zsq_ready, t)
                S.activation(zsq[:, :], z[:, t % 2, :], ACT.Square, accum_out=col(t, ZSS)).then_inc(zsq_ready, 1)

            def q_copy(t):
                act.wait_ge(q_turned, t + 1)
                S.copy(q_cm[:, t % 2, :, :], half(ht_ps[1]).rearrange("p (k m) -> p k m", k=KC)).then_inc(q_cm_ready, 1)

            square_z(0)
            q_copy(0)
            square_z(1)
            for t in range(NT + 2):
                if t < NT:
                    for i, (c, n) in enumerate(PARTS):
                        g = 3 * t + i
                        act.wait_ge(gu_summed, g + 1)
                        if g >= 2:
                            act.wait_ge(h_ready, g - 1)
                        S.activation(silu[:, g % 2, 0:n], gu_ps[2 * (g % 2)][:, 0:n], ACT.Silu,
                                     scale=col(t, G_SCALE)).then_inc(silu_ready, 1)
                    act.wait_ge(h_ready, 3 * t + 3)
                    if t:
                        act.wait_ge(hsq_ready, t)
                    S.activation(hsq[:, :], h[:, t % 2, :], ACT.Square, accum_out=col(t, HSS)).then_inc(hsq_ready, 1)
                if 1 <= t <= NT:
                    s = t - 1
                    act.wait_ge(h_turned, s + 1)
                    S.copy(h_cm[:, s % 2, 0:8, :], half(ht_ps[0], 1024).rearrange("p (k m) -> p k m", k=8)).then_inc(h_cm_ready, 1)
                    S.copy(h_cm[:, s % 2, 8:W3, :], half(ht_ps[1], 384).rearrange("p (k m) -> p k m", k=3)).then_inc(h_cm_ready, 1)
                if t + 2 < NT:
                    square_z(t + 2)
                if t + 1 < NT:
                    q_copy(t + 1)
                if t < NT:
                    act.wait_ge(hscale_ready, t + 1)
                    S.activation(hr[:, t % 2, :], h[:, t % 2, :], ACT.Copy, bias=ROUND, scale=col(t, HQ)).then_inc(hr_ready, 1)
                if t >= 2:
                    s = t - 2
                    act.wait_ge(x4_turned, s + 1)
                    S.copy(out_cm[:, :, s * P:(s + 1) * P], x_ps[:, :].rearrange("p (k m) -> p k m", k=KC)).then_inc(out_ready, 1)

        @block.tensor
        def _(pe):
            T = nc.tensor
            pe.wait_ge(ident_ready, 1)

            def turn_stack(t):
                if t >= 1:
                    pe.wait_ge(x3_ready, t)
                if t >= 5:
                    pe.wait_ge(out_ready, t - 4)
                for k in range(KC):
                    mm = T.transpose(x_ps[:, k * P:(k + 1) * P], feat[:, k, t * P:(t + 1) * P], ident[:, :])
                mm.then_inc(stack_turned, 1)

            def turn_q(t):
                pe.wait_ge(q_ready, t + 1)
                if t >= 2:
                    pe.wait_ge(h_cm_ready, 2 * (t - 1))
                for k in range(KC):
                    mm = T.transpose(half(ht_ps[1])[:, k * P:(k + 1) * P], q[:, t % 2, k * P:(k + 1) * P], ident_b[:, :])
                mm.then_inc(q_turned, 1)

            turn_stack(0)
            turn_q(0)
            turn_stack(1)
            for t in range(NT + 2):
                if t < NT:
                    pe.wait_ge(q_cm_ready, t + 1)
                    for i, (c, n) in enumerate(PARTS):
                        g = 3 * t + i
                        if g >= 2:
                            pe.wait_ge(h_ready, g - 1)
                        for w, ps in ((w1, gu_ps[2 * (g % 2)]), (w2, gu_ps[2 * (g % 2) + 1])):
                            for k in range(KC):
                                mm = T.matmul(ps[:, 0:n], q_cm[:, t % 2, k, :], w[:, k, c:c + n],
                                              start=(k == 0), stop=(k == KC - 1))
                        mm.then_inc(gu_summed, 1)
                if 1 <= t <= NT:
                    s = t - 1
                    pe.wait_ge(hq_ready, s + 1)
                    if t < NT:
                        pe.wait_ge(q_cm_ready, t + 1)
                    if s >= 1:
                        pe.wait_ge(h_cm_ready, 2 * s)
                    for k in range(W3):
                        dst = half(ht_ps[0], 1024)[:, k * P:(k + 1) * P] if k < 8 else half(ht_ps[1])[:, (k - 8) * P:(k - 7) * P]
                        mm = T.transpose(dst, hq[:, s % 2, k * P:(k + 1) * P], ident_b[:, :])
                    mm.then_inc(h_turned, 1)
                if t + 2 < NT:
                    turn_stack(t + 2)
                if t + 1 < NT:
                    if t >= 1:
                        pe.wait_ge(h_cm_ready, 2 * t)
                    turn_q(t + 1)
                if 1 <= t <= NT:
                    s = t - 1
                    pe.wait_ge(h_cm_ready, 2 * s + 2)
                    if s >= 1:
                        pe.wait_ge(x4_ready, s)
                    for k in range(W3):
                        mm = T.matmul(y_ps[:, :], h_cm[:, s % 2, k, :], w3[:, k, :], start=(k == 0), stop=(k == W3 - 1))
                    mm.then_inc(y_summed, 1)
                if t >= 2:
                    s = t - 2
                    pe.wait_ge(x4_ready, s + 1)
                    pe.wait_ge(x3_ready, min(t + 3, NT))
                    if s >= 1:
                        pe.wait_ge(out_ready, s)
                    for k in range(KC):
                        mm = T.transpose(x_ps[:, k * P:(k + 1) * P], x_tm[:, s, k * P:(k + 1) * P], ident[:, :])
                    mm.then_inc(x4_turned, 1)

        @block.vector
        def _(dve):
            V = nc.vector
            done = [0]

            def link(ins):
                done[0] += 1
                ins.then_inc(dve_step, 1)
                dve.wait_ge(dve_step, done[0])

            def quant_scale(t, rms, top, a, to, inv):
                link(V.tensor_scalar(col(t, a), col(t, top), col(t, rms), QEPS, ALU.mult, ALU.max))
                link(V.tensor_scalar(col(t, inv), col(t, a), 1.0 / 127.0, None, ALU.mult))
                link(V.reciprocal(col(t, to), col(t, a)))
                return V.tensor_scalar(col(t, to), col(t, to), col(t, rms), 127.0, ALU.mult, ALU.mult)

            def norm(t):
                dve.wait_ge(stack_turned, t + 1)
                V.tensor_tensor(x_tm[:, t, :], x_tm[:, t, :], x_ps[:, :], ALU.add).then_inc(x3_ready, 1)
                dve.wait_ge(x3_ready, t + 1)
                link(V.bn_stats(st[:, t, :], x_tm[:, t, :]))
                link(V.bn_aggr(mv[:, t, :], st[:, t, :]))
                rsqrt(nc, link, rstd[:, t:t + 1], mv[:, t, 1:2], 1.0, LN_T_EPS, scratch)
                V.tensor_scalar(z[:, t % 2, :], x_tm[:, t, :], mv[:, t, 0:1], rstd[:, t:t + 1],
                                ALU.subtract, ALU.mult).then_inc(z_ready, 1)
                dve.wait_ge(z_ready, t + 1)
                link(V.tensor_reduce(col(t, ZMAX), z[:, t % 2, :], AX.X, ALU.max, apply_absolute_value=True))

            def quant(t):
                dve.wait_ge(zsq_ready, t + 1)
                rsqrt(nc, link, col(t, ZRMS), col(t, ZSS), 1.0 / C, RMS_EPS, scratch)
                link(quant_scale(t, ZRMS, ZMAX, ZA, Q, INV_Q))
                link(V.tensor_tensor(col(t, G_SCALE), col(t, INV_Q), inv_ws[:, 0:1], ALU.mult))
                link(V.tensor_tensor(col(t, U_SCALE), col(t, INV_Q), inv_ws[:, 1:2], ALU.mult))
                link(V.tensor_scalar(zr[:, :], z[:, t % 2, :], col(t, Q), ROUND, ALU.mult, ALU.add))
                V.tensor_scalar(q[:, t % 2, :], zr[:, :], -ROUND, -32.0, ALU.add, ALU.max).then_inc(q_ready, 1)

            norm(0)
            quant(0)
            norm(1)
            for t in range(NT + 1):
                if t < NT:
                    for i, (c, n) in enumerate(PARTS):
                        g = 3 * t + i
                        dve.wait_ge(silu_ready, g + 1)
                        V.scalar_tensor_tensor(h[:, t % 2, c:c + n], gu_ps[2 * (g % 2) + 1][:, 0:n], col(t, U_SCALE),
                                               silu[:, g % 2, 0:n], ALU.mult, ALU.mult).then_inc(h_ready, 1)
                    if t + 2 < NT:
                        norm(t + 2)
                    dve.wait_ge(h_ready, 3 * t + 3)
                    link(V.tensor_reduce(col(t, HMAX), h[:, t % 2, :], AX.X, ALU.max, apply_absolute_value=True))
                    dve.wait_ge(hsq_ready, t + 1)
                    rsqrt(nc, link, col(t, HRMS), col(t, HSS), 1.0 / W1, RMS_EPS, scratch)
                    quant_scale(t, HRMS, HMAX, HA, HQ, Y_SCALE).then_inc(hscale_ready, 1)
                    link(V.tensor_tensor(col(t, Y_SCALE), col(t, Y_SCALE), inv_ws[:, 2:3], ALU.mult))
                    if t + 1 < NT:
                        quant(t + 1)
                if t >= 1:
                    s = t - 1
                    dve.wait_ge(y_summed, s + 1)
                    V.scalar_tensor_tensor(x_tm[:, s, :], y_ps[:, :], col(s, Y_SCALE), x_tm[:, s, :],
                                           ALU.mult, ALU.add).then_inc(x4_ready, 1)
                if t < NT:
                    dve.wait_ge(hr_ready, t + 1)
                    V.tensor_scalar(hq[:, t % 2, :], hr[:, t % 2, :], -ROUND, -32.0, ALU.add, ALU.max).then_inc(hq_ready, 1)


def program(nc, io):
    with ExitStack() as ctx:
        def sb(name, shape, dt=FP32):
            return ctx.enter_context(nc.sbuf_tensor(name, shape, dt))
        keep = {
            "x_tm": sb("x_tm", [P, NT, C]),
            "ident": sb("ident", [P, P]),
            "aff": sb("aff", [P, NT, TOPK]),
            "slots": sb("slots", [P, NT, TOPK], U32),
            "rounds": sb("rounds", [P, 1], U32),
        }
        attention_and_routing(nc, io, keep)
        experts(nc, io, keep)
        combine(nc, io, keep)
        keep["feat"] = sb("feat", [P, KC, TOK])
        keep["ternary"] = sb("ternary", [P, 3, KC * W1], BF16)
        keep["inv_ws"] = sb("inv_ws", [P, 3])
        scan(nc, io, keep)
        ternary_ffn(nc, io, keep)


def kernel(**inputs):
    import concourse.bacc as bacc
    from concourse.bass_utils import run_bass_kernel_spmd

    nc = bacc.Bacc("TRN2", target_bir_lowering=False, num_devices=1)
    a = {k: np.asarray(v) for k, v in inputs.items()}
    host = {
        "x": a["x"],
        "w1t": a["L0_conv_w1"].T, "w2t": a["L0_conv_w2"].T, "w3t": a["L0_conv_w3"].T,
        "b1": a["L0_conv_b1"], "b2": a["L0_conv_b2"], "b3": a["L0_conv_b3"], "alpha": a["L0_conv_alpha"],
        "lnw": a["L0_ffn_ln_weight"], "router": a["L0_ffn_router_weight"],
        "gate_up": a["L0_ffn_gate_up_proj"], "down": a["L0_ffn_down_proj"],
        "sgate": a["L0_ffn_shared_gate_w"], "sup": a["L0_ffn_shared_up_w"], "sdown": a["L0_ffn_shared_down_w"],
        "conv_w": a["L1_conv_W"][:, :, 4, 0].T, "conv_b": a["L1_conv_b"],
        "f1": a["L1_ffn_w1"].T, "f2": a["L1_ffn_w2"].T, "f3": a["L1_ffn_w3"].T,
    }
    host = {k: np.ascontiguousarray(v) for k, v in host.items()}
    io = {k: nc.dram_tensor(f"in_{k}", v.shape, FP32, kind="ExternalInput").ap() for k, v in host.items()}
    io["tokens"] = nc.dram_tensor("tokens", (TOK, C), FP32, kind="Internal").ap()
    io["slot_token"] = nc.dram_tensor("slot_token", (SLOTS, 1), U32, kind="Internal").ap()
    io["slot_y"] = nc.dram_tensor("slot_y", (SLOTS, C), FP32, kind="Internal").ap()
    io["out"] = nc.dram_tensor("out", a["x"].shape, FP32, kind="ExternalOutput").ap()
    program(nc, io)
    r = run_bass_kernel_spmd(nc, [{f"in_{k}": v for k, v in host.items()}], core_ids=[0])
    return r.results[0]["out"]
```

```python
from contextlib import ExitStack

import numpy as np

import concourse.bass as bass
from concourse import mybir
from concourse.alu_op_type import AluOpType as ALU

FP32 = mybir.dt.float32
F32R = mybir.dt.float32r
BF16 = mybir.dt.bfloat16
U32 = mybir.dt.uint32
F16 = mybir.dt.float16
F8 = mybir.dt.float8e4
ACT = mybir.ActivationFunctionType
AX = mybir.AxisListType

P = 128
BATCH, C, IMH, IMW = 4, 512, 16, 16
SP = IMH * IMW
TOK = BATCH * SP
NT = TOK // P
KC = C // P
D = 64
EXPERTS, TOPK = 16, 4
FF = 1024
CAP = 320
MAX_ROUNDS = -(-TOK // CAP)
ROUND_SLOTS = EXPERTS * CAP
SLOTS = -(-(MAX_ROUNDS * EXPERTS + 1) * CAP // P) * P
NARROW = 2 * P
W1, W3 = 1408, 1408 // P
ROUND = 12582912.0
QEPS = 1e-5
LN_C_EPS, LN_T_EPS, RMS_EPS = 1e-6, 1e-5, 1e-6


RSQRT_SEED = 1597463007.0


def rsqrt(nc, link, out, v, scale, eps, scratch):
    V, n = nc.vector, out.shape[-1]
    a, t = scratch[:, 0:n], scratch[:, n:2 * n]
    link(V.tensor_scalar(a, v, scale, eps, ALU.mult, ALU.add))
    link(V.tensor_scalar(t.bitcast(U32), a.bitcast(U32), 1, None, ALU.logical_shift_right))
    link(V.tensor_scalar(out.bitcast(U32), t.bitcast(U32), -1.0, RSQRT_SEED, ALU.mult, ALU.add))
    for _ in range(3):
        link(V.tensor_tensor(t, out, out, ALU.mult))
        link(V.scalar_tensor_tensor(t, t, -0.5, a, ALU.mult, ALU.mult))
        link(V.scalar_tensor_tensor(out, t, 1.5, out, ALU.add, ALU.mult))


def attention_and_routing(nc, io, keep):
    ctx = ExitStack()
    with ctx:
        def sb(name, shape, dt=FP32):
            return ctx.enter_context(nc.sbuf_tensor(name, shape, dt))

        def bank(name):
            return ctx.enter_context(nc.psum_tensor(name, [P, 512], FP32))

        def sem(name):
            return ctx.enter_context(nc.semaphore(name))

        x_cm = sb("x_cm", [P, KC, TOK])
        x_tm = keep["x_tm"]
        xn_tm = sb("xn_tm", [P, NT, C])
        xn_cm = sb("xn_cm", [P, KC, TOK])
        w12 = sb("w12", [P, KC, 2 * D])
        w3 = sb("w3", [P, KC, C])
        b12 = sb("b12", [D, 2])
        b3 = sb("b3", [1, C])
        alpha = sb("alpha", [P, 1])
        lnw = sb("lnw", [P, C])
        router = sb("router", [P, KC, EXPERTS])
        stats = sb("stats", [P, NT, 6])
        mv = sb("mv", [P, NT, 2])
        rstd = sb("rstd", [P, NT])
        e12 = sb("e12", [D, 2, 2, SP])
        nmax = sb("nmax", [P, NT])
        prob = sb("prob", [P, 2, SP])
        psum_row = sb("psum_row", [P, NT])
        gain = sb("gain", [P, NT])
        prob_t = sb("prob_t", [P, 2, SP])
        part = sb("part", [P, C])
        stats1 = sb("stats1", [P, NT, 6])
        mv1 = sb("mv1", [P, NT, 2])
        rstd1 = sb("rstd1", [P, NT])
        z = sb("z", [P, 2, C])
        zsq = sb("zsq", [P, C], BF16)
        ssq = sb("ssq", [P, NT])
        scratch = sb("scratch", [P, 2])
        rms1 = sb("rms1", [P, NT])
        zn = sb("zn", [P, NT, C])
        abs_w = zn[:, :, :].rearrange("p t c -> p (t c)").bitcast(BF16)[:, 0:KC * W1]
        zn_cm = sb("zn_cm", [P, 2, KC, P])
        logits = sb("logits", [P, NT, EXPERTS])
        top = sb("top", [P, NT, 8])
        top_at = sb("top_at", [P, NT, 8], U32)
        top_at_f = sb("top_at_f", [P, NT, TOPK])
        neg_top = sb("neg_top", [P, NT])
        elog = sb("elog", [P, NT, EXPERTS])
        esum = sb("esum", [P, NT])
        resum = sb("resum", [P, NT])
        etop = sb("etop", [P, NT, TOPK])
        expert_ids = sb("expert_ids", [P, EXPERTS])
        onehot = sb("onehot", [P, TOPK, NT, EXPERTS])
        mask = sb("mask", [P, NT, EXPERTS])
        before = sb("before", [P, NT, EXPERTS])
        totals = sb("totals", [P, NT, EXPERTS])
        run = sb("run", [P, NT + 1, EXPERTS])
        wraps = sb("wraps", [P, NT, EXPERTS])
        slot_e = sb("slot_e", [P, NT, EXPERTS])
        base = sb("base", [P, EXPERTS])
        picked = sb("picked", [P, NT, EXPERTS])
        slot_f = sb("slot_f", [P, NT, TOPK])
        most = sb("most", [P, 1])
        most2 = sb("most2", [P, 4])
        room = sb("room", [P, MAX_ROUNDS, EXPERTS])
        zero_list = sb("zero_list", [P, SLOTS // P], U32)
        upper = sb("upper", [P, P])
        ones = sb("ones", [P, P])
        weights = sb("weights", [P, 3, KC * W1])
        abs_sum = sb("abs_sum", [P, 3])
        abs_all = sb("abs_all", [P, 3])
        w_scale = sb("w_scale", [P, 3])
        ternary, inv_ws = keep["ternary"], keep["inv_ws"]
        ident = keep["ident"]
        aff, slots, rounds = keep["aff"], keep["slots"], keep["rounds"]
        token_ids, narrow = keep["token_ids"], keep["narrow"]

        pa = [bank("pa0"), bank("pa1")]
        pb = [bank("pb0"), bank("pb1")]
        pe_ = bank("pe_")
        ps = bank("ps")
        pt = bank("pt")
        pg = bank("pg")

        x_in = [sem(f"x_in{n}") for n in range(BATCH)]
        w_in = sem("w_in")
        last_in = [sem(f"last_in{i}") for i in range(3)]
        abs_ready = sem("abs_ready")
        abs_summed = sem("abs_summed")
        scale_ready = sem("scale_ready")
        cut = sem("cut")
        rounded = sem("rounded")
        const_ready = sem("const_ready")
        pool_step = sem("pool_step")
        x_turned = sem("x_turned")
        x_kept = sem("x_kept")
        xn_ready = sem("xn_ready")
        xn_turned = sem("xn_turned")
        xn_cm_ready = sem("xn_cm_ready")
        e_summed = sem("e_summed")
        e_ready = sem("e_ready")
        scored = sem("scored")
        max_ready = sem("max_ready")
        prob_ready = sem("prob_ready")
        prob_turned = sem("prob_turned")
        prob_t_ready = sem("prob_t_ready")
        mixed = sem("mixed")
        x1_ready = sem("x1_ready")
        z_ready = sem("z_ready")
        ssq_ready = sem("ssq_ready")
        zn_ready = sem("zn_ready")
        zn_turned = sem("zn_turned")
        zn_cm_ready = sem("zn_cm_ready")
        routed = sem("routed")
        logits_ready = sem("logits_ready")
        neg_top_ready = sem("neg_top_ready")
        elog_ready = sem("elog_ready")
        mask_ready = sem("mask_ready")
        counted = sem("counted")
        zeroed = sem("zeroed")
        zn_out = sem("zn_out")
        dve_step = sem("dve_step")

        block = ctx.enter_context(nc.Block())

        @block.sync
        def _(sp):
            for n in range(BATCH):
                sp.dma_start(x_cm[:, :, n * SP:(n + 1) * SP],
                             io["x"][n].rearrange("(k p) h w -> p k (h w)", p=P)).then_inc(x_in[n], 16)
            for i, name in enumerate(("f1", "f2", "f3")):
                sp.dma_start(weights[:, i, :].rearrange("p (k m) -> p k m", m=io[name].shape[1]),
                             io[name].rearrange("(k p) m -> p k m", p=P)).then_inc(last_in[i], 16)
            for t in range(NT):
                sp.wait_ge(zn_ready, t + 1)
                sp.dma_start(io["tokens"][t * P:(t + 1) * P, :], zn[:, t, :]).then_inc(zn_out, 16)
            sp.wait_ge(zn_out, 16 * NT)

        @block.gpsimd
        def _(pool):
            pool.memset(ident[:, :], 0.0).then_inc(pool_step, 1)
            pool.memset(ones[:, :], 1.0).then_inc(pool_step, 1)
            pool.memset(zero_list[:, :], 0).then_inc(pool_step, 1)
            pool.wait_ge(pool_step, 3)
            pool.affine_select(out=ident[:, :], in_=ident[:, :], compare_op=ALU.not_equal, fill=1.0,
                               base=0, pattern=[[-1, P]], channel_multiplier=1).then_inc(const_ready, 1)
            pool.affine_select(out=upper[:, :], in_=ones[:, :], compare_op=ALU.is_gt, fill=0.0,
                               base=0, pattern=[[1, P]], channel_multiplier=-1).then_inc(const_ready, 1)
            pool.iota(expert_ids[:, :], pattern=[[1, EXPERTS]], base=0, channel_multiplier=0,
                      allow_small_or_imprecise_dtypes=True).then_inc(const_ready, 1)
            pool.iota(base[:, :], pattern=[[CAP, EXPERTS]], base=0, channel_multiplier=0,
                      allow_small_or_imprecise_dtypes=True).then_inc(const_ready, 1)
            pool.iota(token_ids[:, :], pattern=[[P, NT]], base=0, channel_multiplier=1).then_inc(const_ready, 1)
            pool.dma_start(io["slot_token"].rearrange("(p a) o -> p (a o)", p=P), zero_list[:, :]).then_inc(zeroed, 16)
            pool.wait_ge(abs_ready, 3)
            nc.gpsimd.partition_all_reduce(abs_all[:, :], abs_sum[:, :], P, bass.bass_isa.ReduceOp.add).then_inc(abs_summed, 1)
            pool.wait_ge(scale_ready, 1)
            for i in range(3):
                nc.gpsimd.tensor_scalar(weights[:, i, :], weights[:, i, :], w_scale[:, i:i + 1], 1.0,
                                        ALU.mult, ALU.min).then_inc(cut, 1)
                pool.wait_ge(cut, i + 1)
                nc.gpsimd.tensor_scalar(weights[:, i, :], weights[:, i, :], -1.0, ROUND,
                                        ALU.max, ALU.add).then_inc(rounded, 1)
            pool.wait_ge(zeroed, 16)

        @block.scalar
        def _(act):
            act.dma_start(w12[:, :, 0:D], io["w1t"].rearrange("(k p) m -> p k m", p=P)).then_inc(w_in, 16)
            act.dma_start(w12[:, :, D:2 * D], io["w2t"].rearrange("(k p) m -> p k m", p=P)).then_inc(w_in, 16)
            act.dma_start(w3[:, :, :], io["w3t"].rearrange("(k p) m -> p k m", p=P)).then_inc(w_in, 16)
            act.dma_start(b12[:, 0:1], io["b1"].rearrange("(a b) -> a b", b=1)).then_inc(w_in, 16)
            act.dma_start(b12[:, 1:2], io["b2"].rearrange("(a b) -> a b", b=1)).then_inc(w_in, 16)
            act.dma_start(b3[:, :], io["b3"].rearrange("(a b) -> a b", a=1)).then_inc(w_in, 16)
            act.dma_start(alpha[:, :], io["alpha"].rearrange("(a b) -> a b", a=1).to_broadcast([P, 1])).then_inc(w_in, 16)
            act.dma_start(lnw[:, :], io["lnw"].rearrange("(a b) -> a b", a=1).to_broadcast([P, C])).then_inc(w_in, 16)
            act.dma_start(router[:, :, :], io["router"].rearrange("(k p) m -> p k m", p=P)).then_inc(w_in, 16)
            for t in range(NT):
                act.wait_ge(x_turned, t + 1)
                nc.scalar.copy(x_tm[:, t, :], pa[t % 2][:, :]).then_inc(x_kept, 1)
                act.wait_ge(xn_turned, t + 1)
                nc.scalar.copy(xn_cm[:, :, t * P:(t + 1) * P],
                               pb[t % 2][:, :].rearrange("p (k m) -> p k m", k=KC)).then_inc(xn_cm_ready, 1)
            for i in range(3):
                act.wait_ge(last_in[i], 16)
                if i:
                    act.wait_ge(abs_ready, i)
                nc.scalar.activation(abs_w, weights[:, i, :], ACT.Abs,
                                     accum_out=abs_sum[:, i:i + 1]).then_inc(abs_ready, 1)
            act.wait_ge(w_in, 9 * 16)

            def gate_scalar(s):
                act.wait_ge(zn_turned, s + 1)
                if s >= 2:
                    act.wait_ge(routed, s - 1)
                nc.scalar.copy(zn_cm[:, s % 2, :, :], pg[:, :].rearrange("p (k m) -> p k m", k=KC)).then_inc(zn_cm_ready, 1)
                act.wait_ge(neg_top_ready, s + 1)
                nc.scalar.activation(elog[:, s, :], logits[:, s, :], ACT.Exp, bias=neg_top[:, s:s + 1],
                                     accum_out=esum[:, s:s + 1]).then_inc(elog_ready, 1)
                nc.scalar.activation(etop[:, s, :], top[:, s, 0:TOPK], ACT.Exp,
                                     bias=neg_top[:, s:s + 1]).then_inc(elog_ready, 1)

            for s in range(NT):
                n = s // 2
                if s % 2 == 0:
                    act.wait_ge(e_summed, n + 1)
                    if n >= 2:
                        act.wait_ge(scored, 2 * (n - 1))
                    for j in range(2):
                        nc.scalar.activation(e12[:, n % 2, j, :], pe_[0:D, j * SP:(j + 1) * SP], ACT.Relu,
                                             bias=b12[:, j:j + 1]).then_inc(e_ready, 1)
                act.wait_ge(max_ready, s + 1)
                if s >= 2:
                    act.wait_ge(prob_turned, s - 1)
                nc.scalar.activation(prob[:, s % 2, :], ps[:, 0:SP], ACT.Exp,
                                     bias=nmax[:, s:s + 1], accum_out=psum_row[:, s:s + 1]).then_inc(prob_ready, 1)
                act.wait_ge(prob_turned, s + 1)
                if s >= 2:
                    act.wait_ge(mixed, s - 1)
                nc.scalar.copy(prob_t[:, s % 2, :], pt[:, 0:SP]).then_inc(prob_t_ready, 1)
                if s >= 1:
                    gate_scalar(s - 1)
                if s >= 3 and s % 2:
                    i = s // 2 - 1
                    act.wait_ge(rounded, i + 1)
                    nc.scalar.activation(ternary[:, i, :], weights[:, i, :], ACT.Copy, bias=-ROUND, saturate=False)
                act.wait_ge(z_ready, s + 1)
                if s >= 1:
                    act.wait_ge(ssq_ready, s)
                nc.scalar.activation(zsq[:, :], z[:, s % 2, :], ACT.Square,
                                     accum_out=ssq[:, s:s + 1]).then_inc(ssq_ready, 1)
            gate_scalar(NT - 1)

        @block.tensor
        def _(pe):
            pe.wait_ge(const_ready, 2)
            for t in range(NT + 1):
                if t < NT:
                    if t % 2 == 0:
                        pe.wait_ge(x_in[t // 2], 16)
                    if t >= 2:
                        pe.wait_ge(x_kept, t - 1)
                    for k in range(KC):
                        mm = nc.tensor.transpose(pa[t % 2][:, k * P:(k + 1) * P], x_cm[:, k, t * P:(t + 1) * P],
                                                 ident[:, :])
                    mm.then_inc(x_turned, 1)
                if t >= 1:
                    s = t - 1
                    pe.wait_ge(xn_ready, s + 1)
                    if s >= 2:
                        pe.wait_ge(xn_cm_ready, s - 1)
                    for k in range(KC):
                        mm = nc.tensor.transpose(pb[s % 2][:, k * P:(k + 1) * P], xn_tm[:, s, k * P:(k + 1) * P],
                                                 ident[:, :])
                    mm.then_inc(xn_turned, 1)
            pe.wait_ge(w_in, 9 * 16)
            pe.wait_ge(xn_cm_ready, NT)

            def route(s):
                pe.wait_ge(zn_ready, s + 1)
                if s >= 1:
                    pe.wait_ge(logits_ready, s)
                for k in range(KC):
                    mm = nc.tensor.transpose(pg[:, k * P:(k + 1) * P], zn[:, s, k * P:(k + 1) * P], ident[:, :])
                mm.then_inc(zn_turned, 1)
                pe.wait_ge(zn_cm_ready, s + 1)
                for k in range(KC):
                    mm = nc.tensor.matmul(pg[:, 0:EXPERTS], zn_cm[:, s % 2, k, :], router[:, k, :],
                                          start=(k == 0), stop=(k == KC - 1))
                mm.then_inc(routed, 1)

            for s in range(NT):
                n = s // 2
                if s % 2 == 0:
                    if n >= 1:
                        pe.wait_ge(e_ready, 2 * n)
                    for j in range(2):
                        for k in range(KC):
                            mm = nc.tensor.matmul(pe_[0:D, j * SP:(j + 1) * SP], w12[:, k, j * D:(j + 1) * D],
                                                  xn_cm[:, k, n * SP:(n + 1) * SP], start=(k == 0), stop=(k == KC - 1))
                    mm.then_inc(e_summed, 1)
                    pe.wait_ge(e_ready, 2 * n + 2)
                if s >= 1:
                    pe.wait_ge(prob_ready, s)
                i = s % 2
                nc.tensor.matmul(ps[:, 0:SP], e12[:, n % 2, 0, i * P:(i + 1) * P], e12[:, n % 2, 1, :],
                                 start=True, stop=True).then_inc(scored, 1)
                if s >= 2:
                    pe.wait_ge(x1_ready, s - 1)
                nc.tensor.matmul(pa[s % 2][:, :], ones[0:1, :], b3[:, :], start=True, stop=False)
                for k in range(KC):
                    nc.tensor.matmul(pa[s % 2][:, :], xn_cm[:, k, s * P:(s + 1) * P], w3[:, k, :],
                                     start=False, stop=(k == KC - 1))
                pe.wait_ge(prob_ready, s + 1)
                if s >= 1:
                    pe.wait_ge(prob_t_ready, s)
                for j in range(2):
                    mm = nc.tensor.transpose(pt[:, j * P:(j + 1) * P], prob[:, s % 2, j * P:(j + 1) * P], ident[:, :])
                mm.then_inc(prob_turned, 1)
                if s >= 1:
                    route(s - 1)
                pe.wait_ge(prob_t_ready, s + 1)
                for j in range(2):
                    mm = nc.tensor.matmul(pb[s % 2][:, :], prob_t[:, s % 2, j * P:(j + 1) * P], xn_tm[:, 2 * n + j, :],
                                          start=(j == 0), stop=(j == 1))
                mm.then_inc(mixed, 1)
            route(NT - 1)
            pe.wait_ge(mask_ready, 1)
            nc.tensor.matmul(ps[:, 0:P], upper[:, :], mask[:, :, :].rearrange("p t e -> p (t e)"), start=True, stop=True)
            nc.tensor.matmul(ps[:, P:2 * P], ones[:, :], mask[:, :, :].rearrange("p t e -> p (t e)"),
                             start=True, stop=True).then_inc(counted, 1)

        @block.vector
        def _(dve):
            steps = [0]

            def link(ins):
                steps[0] += 1
                ins.then_inc(dve_step, 1)
                dve.wait_ge(dve_step, steps[0])

            V = nc.vector
            for t in range(NT):
                dve.wait_ge(x_kept, t + 1)
                link(V.bn_stats(stats[:, t, :], x_tm[:, t, :]))
                link(V.bn_aggr(mv[:, t, :], stats[:, t, :]))
                rsqrt(nc, link, rstd[:, t:t + 1], mv[:, t, 1:2], 1.0, LN_C_EPS, scratch)
                V.tensor_scalar(xn_tm[:, t, :], x_tm[:, t, :], mv[:, t, 0:1], rstd[:, t:t + 1],
                                ALU.subtract, ALU.mult).then_inc(xn_ready, 1)
            dve.wait_ge(abs_summed, 1)
            link(V.tensor_scalar(inv_ws[:, :], abs_all[:, :], 1.0 / (C * W1), QEPS, ALU.mult, ALU.max))
            V.reciprocal(w_scale[:, :], inv_ws[:, :]).then_inc(scale_ready, 1)
            dve.wait_ge(w_in, 9 * 16)
            dve.wait_ge(const_ready, 5)

            def gate(s):
                dve.wait_ge(routed, s + 1)
                V.tensor_copy(logits[:, s, :], pg[:, 0:EXPERTS]).then_inc(logits_ready, 1)
                dve.wait_ge(logits_ready, s + 1)
                link(V.max(top[:, s, :], logits[:, s, :]))
                V.tensor_scalar(neg_top[:, s:s + 1], top[:, s, 0:1], -1.0, None, ALU.mult).then_inc(neg_top_ready, 1)
                V.max_index(top_at[:, s, :], top[:, s, :], logits[:, s, :]).then_inc(dve_step, 1)
                steps[0] += 1

            for s in range(NT):
                dve.wait_ge(scored, s + 1)
                V.tensor_reduce(nmax[:, s:s + 1], ps[:, 0:SP], AX.X, ALU.max,
                                negate=True).then_inc(max_ready, 1)
                dve.wait_ge(prob_ready, s + 1)
                link(V.reciprocal(gain[:, s:s + 1], psum_row[:, s:s + 1]))
                link(V.tensor_tensor(gain[:, s:s + 1], gain[:, s:s + 1], alpha[:, :], ALU.mult))
                if s >= 1:
                    gate(s - 1)
                dve.wait_ge(mixed, s + 1)
                dve.wait_ge(x_kept, s + 1)
                link(V.scalar_tensor_tensor(part[:, :], pa[s % 2][:, :], 0.0, x_tm[:, s, :], ALU.max, ALU.add))
                V.scalar_tensor_tensor(x_tm[:, s, :], pb[s % 2][:, :], gain[:, s:s + 1], part[:, :],
                                       ALU.mult, ALU.add).then_inc(x1_ready, 1)
                dve.wait_ge(x1_ready, s + 1)
                link(V.bn_stats(stats1[:, s, :], x_tm[:, s, :]))
                link(V.bn_aggr(mv1[:, s, :], stats1[:, s, :]))
                rsqrt(nc, link, rstd1[:, s:s + 1], mv1[:, s, 1:2], 1.0, LN_T_EPS, scratch)
                V.tensor_scalar(z[:, s % 2, :], x_tm[:, s, :], mv1[:, s, 0:1], rstd1[:, s:s + 1],
                                ALU.subtract, ALU.mult).then_inc(z_ready, 1)
                dve.wait_ge(z_ready, s + 1)
                dve.wait_ge(ssq_ready, s + 1)
                rsqrt(nc, link, rms1[:, s:s + 1], ssq[:, s:s + 1], 1.0 / C, RMS_EPS, scratch)
                V.scalar_tensor_tensor(zn[:, s, :], z[:, s % 2, :], rms1[:, s:s + 1], lnw[:, :],
                                       ALU.mult, ALU.mult).then_inc(zn_ready, 1)
            gate(NT - 1)
            dve.wait_ge(dve_step, steps[0])
            dve.wait_ge(elog_ready, 2 * NT)
            link(V.reciprocal(resum[:, :], esum[:, :]))
            link(V.tensor_tensor(aff[:, :, :], etop[:, :, :],
                                 resum[:, :].rearrange("p (t o) -> p t o", o=1).to_broadcast([P, NT, TOPK]), ALU.mult))
            link(V.tensor_copy(top_at_f[:, :, :], top_at[:, :, 0:TOPK]))
            for k in range(TOPK):
                link(V.tensor_tensor(onehot[:, k, :, :],
                                     top_at_f[:, :, k:k + 1].to_broadcast([P, NT, EXPERTS]),
                                     expert_ids[:, :].rearrange("p (o e) -> p o e", o=1).to_broadcast([P, NT, EXPERTS]),
                                     ALU.is_equal))
            link(V.tensor_tensor(mask[:, :, :], onehot[:, 0, :, :], onehot[:, 1, :, :], ALU.add))
            link(V.tensor_tensor(mask[:, :, :], mask[:, :, :], onehot[:, 2, :, :], ALU.add))
            V.tensor_tensor(mask[:, :, :], mask[:, :, :], onehot[:, 3, :, :], ALU.add).then_inc(mask_ready, 1)
            link(V.memset(run[:, 0, :], 0.0))
            dve.wait_ge(counted, 1)
            link(V.tensor_copy(totals[:, :, :], ps[:, P:2 * P].rearrange("p (t e) -> p t e", e=EXPERTS)))
            for t in range(NT):
                link(V.tensor_tensor(run[:, t + 1, :], run[:, t, :], totals[:, t, :], ALU.add))
            link(V.tensor_tensor(before[:, :, :], ps[:, 0:P].rearrange("p (t e) -> p t e", e=EXPERTS),
                                 run[:, 0:NT, :], ALU.add))
            link(V.tensor_tensor(slot_e[:, :, :], before[:, :, :],
                                 base[:, :].rearrange("p (o e) -> p o e", o=1).to_broadcast([P, NT, EXPERTS]), ALU.add))
            for r in range(1, MAX_ROUNDS):
                link(V.tensor_scalar(wraps[:, :, :], before[:, :, :], float(r * CAP), float(ROUND_SLOTS - CAP),
                                     ALU.is_ge, ALU.mult))
                link(V.tensor_tensor(slot_e[:, :, :], slot_e[:, :, :], wraps[:, :, :], ALU.add))
            for k in range(TOPK):
                link(V.tensor_tensor(picked[:, :, :], onehot[:, k, :, :], slot_e[:, :, :], ALU.mult))
                link(V.tensor_reduce(slot_f[:, :, k:k + 1], picked[:, :, :], AX.X, ALU.add))
            link(V.tensor_copy(slots[:, :, :], slot_f[:, :, :]))
            link(V.tensor_reduce(most[:, :], run[:, NT, :], AX.X, ALU.max))
            for r in range(1, MAX_ROUNDS):
                link(V.tensor_scalar(most2[:, r:r + 1], most[:, :], float(r * CAP), None, ALU.is_gt))
            link(V.memset(most2[:, 0:1], 1.0))
            link(V.tensor_reduce(most[:, :], most2[:, :], AX.X, ALU.add))
            link(V.tensor_copy(rounds[:, :], most[:, :]))
            for r in range(MAX_ROUNDS):
                link(V.tensor_scalar(room[:, r, :], run[:, NT, :], float(r * CAP + NARROW), None, ALU.is_le))
            V.tensor_copy(narrow[:, :], room[:, :, :].rearrange("p r e -> p (r e)"))


FH = FF // P
PIECE = 2048
PIECES = 6
RING = 3
HALF = TOK // 2
DOWN_K = 4
BACK_RING = 8


def tiles_of(n):
    return [min(P, n - j * P) for j in range(-(-n // P))]


def experts(nc, io, keep):
    ctx = ExitStack()
    with ctx:
        def sb(name, shape, dt=FP32):
            return ctx.enter_context(nc.sbuf_tensor(name, shape, dt))

        def bank(name):
            return ctx.enter_context(nc.psum_tensor(name, [P, 512], FP32))

        def sem(name):
            return ctx.enter_context(nc.semaphore(name))

        x_tm, ident, rounds, narrow = keep["x_tm"], keep["ident"], keep["rounds"], keep["narrow"]
        aff, slots, token_ids = keep["aff"], keep["slots"], keep["token_ids"]
        raw = sb("raw", [P, RING, PIECE])
        w_hi = sb("w_hi", [P, RING, PIECE], F32R)
        w_lo = sb("w_lo", [P, RING, PIECE], F32R)
        rows = sb("rows", [P, 4, C])
        slot_ids = sb("slot_ids", [P, 4], U32)
        x_hi = sb("x_hi", [P, KC, HALF], F32R)
        x_lo = sb("x_lo", [P, KC, HALF], F32R)
        gated = sb("gated", [P, 2, HALF])
        hid = sb("hid", [P, 2, HALF])
        h_hi = sb("h_hi", [P, FH, HALF], F32R)
        h_lo = sb("h_lo", [P, FH, HALF], F32R)
        y_sb = sb("y_sb", [P, 3, C])
        got = sb("got", [P, BACK_RING, C])

        gate_ps = [bank("gate_ps0"), bank("gate_ps1")]
        up_ps = [bank("up_ps0"), bank("up_ps1")]
        y_ps = [bank(f"y_ps{j}") for j in range(4)]
        turn_ps = [gate_ps[0], up_ps[0], gate_ps[1], up_ps[1]]

        raw_in = [sem(f"raw_in{j}") for j in range(RING)]
        hi_ready = sem("hi_ready")
        split_ready = sem("split_ready")
        half_summed = sem("half_summed")
        shared_in = sem("shared_in")
        listed = sem("listed")
        ids_in = sem("ids_in")
        rows_in = sem("rows_in")
        rows_turned = sem("rows_turned")
        x_hi_ready = sem("x_hi_ready")
        x_lo_ready = sem("x_lo_ready")
        gu_summed = sem("gu_summed")
        silu_ready = sem("silu_ready")
        hid_ready = sem("hid_ready")
        h_hi_ready = sem("h_hi_ready")
        h_ready = sem("h_ready")
        y_summed = sem("y_summed")
        y_taken = sem("y_taken")
        y_out = sem("y_out")
        y_free = sem("y_free")
        got_in = [sem(f"got_in{j}") for j in range(BACK_RING)]
        added = sem("added")

        block = ctx.enter_context(nc.Block())
        ROUTED = tiles_of(CAP)
        SHARED = tiles_of(HALF)

        def gu_view(buf, slot):
            return buf[:, slot, :].rearrange("p (k g c) -> p k g c", k=KC, g=2)

        def down_view(buf, slot):
            return buf[:, slot, :].rearrange("p (k c) -> p k c", k=DOWN_K)

        def rounds_of(eng):
            return eng.value_load(rounds[0:1, 0:1], min_val=1, max_val=MAX_ROUNDS)

        @block.sync
        def _(sp):
            def load(U, j, sources):
                slot = j % RING
                sp.wait_ge(split_ready, U * PIECES + j + 1)
                for dst, src in sources:
                    sp.dma_start(dst, src).then_inc(raw_in[slot], 16)

            def pieces(U, gate, up, down, first, last):
                for j in range(first, last):
                    if j < 4:
                        v = gu_view(raw, j % RING)
                        cols = slice(j * 256, (j + 1) * 256)
                        load(U, j, [(v[:, :, 0, :], gate[:, :, cols]), (v[:, :, 1, :], up[:, :, cols])])
                    else:
                        v = down_view(raw, j % RING)
                        k = (j - 4) * DOWN_K
                        load(U, j, [(v[:, 0:2, :], down[:, k:k + 2, :]), (v[:, 2:4, :], down[:, k + 2:k + 4, :])])

            def shared_rows(i):
                sp.dma_start(rows[:, :, :], io["tokens"][i * HALF:(i + 1) * HALF, :]
                             .rearrange("(j p) c -> p j c", p=P)).then_inc(shared_in, 16)

            shared = (io["sgate"].rearrange("(k p) f -> p k f", p=P), io["sup"].rearrange("(k p) f -> p k f", p=P),
                      io["sdown"].rearrange("(k p) c -> p k c", p=P))
            shared_rows(0)
            pieces(0, *shared, 0, PIECES)
            n = rounds_of(sp)
            with sp.Fori(0, n) as r:
                with sp.Fori(0, EXPERTS) as e:
                    gu = io["gate_up"][bass.ds(e, 1), :, :].rearrange("o (k p) f -> p (o k) f", p=P)
                    dn = io["down"][bass.ds(e, 1), :, :].rearrange("o (k p) c -> p (o k) c", p=P)
                    pieces(r * EXPERTS + e + 1, gu[:, :, 0:FF], gu[:, :, FF:2 * FF], dn, 0, PIECES)
            last = n * EXPERTS + 1
            pieces(last, *shared, 0, RING)
            sp.wait_ge(rows_turned, (last + 1) * KC)
            shared_rows(1)
            pieces(last, *shared, RING, PIECES)

        @block.gpsimd
        def _(pool):
            def gather(u):
                pool.wait_ge(rows_turned, (u + 1) * KC)
                base = u * CAP
                ids = io["slot_token"]
                pool.dma_start(slot_ids[:, 0:2], ids[bass.ds(base, 2 * P), :]
                               .rearrange("(p j) o -> p (j o)", p=P)).then_inc(ids_in, 16)
                pool.dma_start(slot_ids[0:CAP - 2 * P, 2:3], ids[bass.ds(base + 2 * P, CAP - 2 * P), :]).then_inc(ids_in, 16)
                pool.wait_ge(ids_in, u * 32 + 32)
                pool.nop(nofuse=True)
                for j, w in enumerate(ROUTED):
                    pool.indirect_dma_start(
                        out=rows[0:w, j, :], out_offset=None, in_=io["tokens"],
                        in_offset=bass.IndirectOffsetOnAxis(ap=slot_ids[0:w, j:j + 1], axis=0)).then_inc(rows_in, 16)

            def store(u):
                pool.wait_ge(y_taken, u + 2)
                base = u * CAP
                pool.dma_start(io["slot_y"][bass.ds(base, 2 * P), :].rearrange("(p j) c -> p j c", p=P),
                               y_sb[:, 0:2, :]).then_inc(y_out, 16)
                pool.dma_start(io["slot_y"][bass.ds(base + 2 * P, CAP - 2 * P), :],
                               y_sb[0:CAP - 2 * P, 2, :]).then_inc(y_out, 16)
                pool.wait_ge(y_out, u * 32 + 32)
                pool.sem_inc(y_free, 1)

            def bring_back(source):
                for i in range(NT * TOPK):
                    t, k = divmod(i, TOPK)
                    if i >= BACK_RING:
                        pool.wait_ge(added, i - BACK_RING + 1)
                    pool.indirect_dma_start(
                        out=got[:, i % BACK_RING, :], out_offset=None, in_=source,
                        in_offset=bass.IndirectOffsetOnAxis(ap=slots[:, t, k:k + 1], axis=0)).then_inc(got_in[i % BACK_RING], 16)

            for t in range(NT):
                for k in range(TOPK):
                    pool.indirect_dma_start(
                        out=io["slot_token"], out_offset=bass.IndirectOffsetOnAxis(ap=slots[:, t, k:k + 1], axis=0),
                        in_=token_ids[:, t:t + 1], in_offset=None).then_inc(listed, 16)
            pool.sem_inc(y_free, 1)
            pool.wait_ge(listed, 16 * NT * TOPK)
            gather(0)
            n = rounds_of(pool)
            with pool.Fori(0, n * EXPERTS) as u:
                gather(u + 1)
                store(u)
            pool.wait_ge(rows_in, n * (EXPERTS * 48) + 48)
            pool.nop(nofuse=True)
            with pool.If(n < 2):
                bring_back(io["slot_y"][0:ROUND_SLOTS, :])
            with pool.Else():
                bring_back(io["slot_y"])

        @block.scalar
        def _(act):
            S = nc.scalar

            def hi(U, j):
                act.wait_ge(raw_in[j % RING], (U * (PIECES // RING) + j // RING) * 32 + 32)
                if j == 0:
                    act.wait_ge(gu_summed, U * FH)
                elif j == 1:
                    act.wait_ge(half_summed, U)
                elif j == 2:
                    act.wait_ge(y_summed, U)
                else:
                    act.wait_ge(gu_summed, U * FH + 2 * (j - 2))
                S.copy(w_hi[:, j % RING, :], raw[:, j % RING, :]).then_inc(hi_ready, 1)

            def hidden(U, m, n):
                act.wait_ge(gu_summed, U * FH + m + 1)
                S.activation(gated[:, m % 2, 0:n], gate_ps[m % 2][:, 0:n], ACT.Silu).then_inc(silu_ready, 1)
                act.wait_ge(hid_ready, U * FH + m + 1 + 2)
                S.copy(h_hi[:, m, 0:n], hid[:, m % 2, 0:n]).then_inc(h_hi_ready, 1)

            def turn(i, n):
                for k in range(KC):
                    act.wait_ge(rows_turned, i * KC + k + 1)
                    S.copy(x_hi[:, k, 0:n], turn_ps[k][:, 0:n]).then_inc(x_hi_ready, 1)

            def take(u):
                act.wait_ge(y_summed, u + 2)
                act.wait_ge(y_free, u + 1)
                for j, w in enumerate(ROUTED):
                    ins = S.copy(y_sb[0:w, j, :], y_ps[j][0:w, :])
                ins.then_inc(y_taken, 1)

            def unit(U, n):
                for j in range(4):
                    hidden(U, 2 * j, n)
                    hidden(U, 2 * j + 1, n)
                    hi(U, j + 2)

            turn(0, HALF)
            hi(0, 0)
            hi(0, 1)
            unit(0, HALF)
            turn(1, CAP)
            hi(1, 0)
            hi(1, 1)
            n = rounds_of(act)
            with act.Fori(0, n * EXPERTS) as u:
                unit(u + 1, CAP)
                turn(u + 2, CAP)
                hi(u + 2, 0)
                hi(u + 2, 1)
                take(u)
            last = n * EXPERTS + 1
            turn(last + 1, HALF)
            unit(last, HALF)

        @block.vector
        def _(dve):
            V = nc.vector

            def lo(U, j):
                dve.wait_ge(hi_ready, U * PIECES + j + 1)
                V.tensor_tensor(w_lo[:, j % RING, :], raw[:, j % RING, :], w_hi[:, j % RING, :].bitcast(FP32),
                                ALU.subtract).then_inc(split_ready, 1)

            def hidden(U, m, n):
                dve.wait_ge(silu_ready, U * FH + m + 1)
                V.tensor_tensor(hid[:, m % 2, 0:n], gated[:, m % 2, 0:n], up_ps[m % 2][:, 0:n],
                                ALU.mult).then_inc(hid_ready, 1)
                dve.wait_ge(h_hi_ready, U * FH + m + 1)
                V.tensor_tensor(h_lo[:, m, 0:n], hid[:, m % 2, 0:n], h_hi[:, m, 0:n].bitcast(FP32),
                                ALU.subtract).then_inc(h_ready, 1)

            def turn(i, n):
                for k in range(KC):
                    dve.wait_ge(x_hi_ready, i * KC + k + 1)
                    V.tensor_tensor(x_lo[:, k, 0:n], turn_ps[k][:, 0:n], x_hi[:, k, 0:n].bitcast(FP32),
                                    ALU.subtract).then_inc(x_lo_ready, 1)

            def add_shared(U, first):
                dve.wait_ge(y_summed, U + 1)
                for j in range(len(SHARED)):
                    t = first + j
                    last = V.tensor_tensor(x_tm[:, t, :], x_tm[:, t, :], y_ps[j][:, :], ALU.add)
                last.then_inc(y_taken, 1)

            def unit(U, n, beside):
                for j in range(4):
                    hidden(U, 2 * j, n)
                    beside(2 * j)
                    hidden(U, 2 * j + 1, n)
                    beside(2 * j + 1)
                    lo(U, j + 2)

            def add_back(i):
                t, k = divmod(i, TOPK)
                dve.wait_ge(got_in[i % BACK_RING], 16 * (i // BACK_RING + 1))
                if i:
                    dve.wait_ge(added, i)
                V.scalar_tensor_tensor(x_tm[:, t, :], got[:, i % BACK_RING, :], aff[:, t, k:k + 1], x_tm[:, t, :],
                                       ALU.mult, ALU.add).then_inc(added, 1)

            def beside_last(m):
                for i in range(3 * (m - 1), 3 * m):
                    if i >= 0:
                        add_back(i)

            dve.sem_inc(split_ready, RING)
            dve.sem_inc(hid_ready, 2)
            turn(0, HALF)
            lo(0, 0)
            lo(0, 1)
            unit(0, HALF, lambda m: None)
            turn(1, CAP)
            lo(1, 0)
            lo(1, 1)
            add_shared(0, 0)
            n = rounds_of(dve)
            with dve.Fori(0, n * EXPERTS) as u:
                unit(u + 1, CAP, lambda m: None)
                turn(u + 2, CAP)
                lo(u + 2, 0)
                lo(u + 2, 1)
            last = n * EXPERTS + 1
            turn(last + 1, HALF)
            unit(last, HALF, beside_last)
            for i in range(3 * (FH - 1), NT * TOPK):
                add_back(i)
            dve.wait_ge(added, NT * TOPK)
            add_shared(last, len(SHARED))

        @block.tensor
        def _(pe):
            T = nc.tensor

            def turn(tiles):
                for k in range(KC):
                    for j, w in enumerate(tiles):
                        mm = T.transpose(turn_ps[k][:, j * P:j * P + w], rows[0:w, j, k * P:(k + 1) * P], ident[0:w, 0:w])
                    mm.then_inc(rows_turned, 1)

            def three(out, hi_a, lo_a, hi_b, lo_b, first, last):
                T.matmul(out, hi_a, hi_b, start=first, stop=False)
                T.matmul(out, hi_a, lo_b, start=False, stop=False)
                return T.matmul(out, lo_a, hi_b, start=False, stop=last)

            def unit(U, tiles, next_rows):
                n = sum(tiles)
                for j in range(4):
                    pe.wait_ge(split_ready, U * PIECES + j + 1 + RING)
                    hi_w, lo_w = gu_view(w_hi, j % RING), gu_view(w_lo, j % RING)
                    for i in range(2):
                        m = 2 * j + i
                        pe.wait_ge(hid_ready, U * FH + m + 1)
                        for g, ps in enumerate((gate_ps[i], up_ps[i])):
                            for k in range(KC):
                                c = slice(i * P, (i + 1) * P)
                                mm = three(ps[:, 0:n], hi_w[:, k, g, c], lo_w[:, k, g, c], x_hi[:, k, 0:n], x_lo[:, k, 0:n],
                                           k == 0, k == KC - 1)
                        mm.then_inc(gu_summed, 1)
                for d in range(2):
                    j = 4 + d
                    pe.wait_ge(split_ready, U * PIECES + j + 1 + RING)
                    if d == 0 and not (isinstance(U, int) and U == 0):
                        pe.wait_ge(y_taken, U)
                    hi_w, lo_w = down_view(w_hi, j % RING), down_view(w_lo, j % RING)
                    for k in range(DOWN_K):
                        m = d * DOWN_K + k
                        pe.wait_ge(h_ready, U * FH + m + 1)
                        for i, w in enumerate(tiles):
                            c = slice(i * P, i * P + w)
                            mm = three(y_ps[i][0:w, :], h_hi[:, m, c], h_lo[:, m, c], hi_w[:, k, :], lo_w[:, k, :],
                                       m == 0, m == FH - 1)
                    if d == 0:
                        mm.then_inc(half_summed, 1)
                        pe.wait_ge(h_ready, U * FH + FH)
                        if next_rows:
                            pe.wait_ge(*next_rows)
                            turn(ROUTED)
                    else:
                        mm.then_inc(y_summed, 1)

            pe.wait_ge(shared_in, 16)
            turn(SHARED)
            pe.wait_ge(x_lo_ready, KC)
            unit(0, SHARED, (rows_in, 16 * len(ROUTED)))
            n = rounds_of(pe)
            with pe.Fori(0, n * EXPERTS) as u:
                pe.wait_ge(x_lo_ready, (u + 2) * KC)
                few = pe.value_load(narrow[0:1, bass.ds(u, 1)], min_val=0, max_val=1)
                next_rows = (rows_in, (u + 2) * (16 * len(ROUTED)))
                with pe.If(few > 0):
                    unit(u + 1, tiles_of(NARROW), next_rows)
                with pe.Else():
                    unit(u + 1, ROUTED, next_rows)
            last = n * EXPERTS + 1
            pe.wait_ge(x_lo_ready, (last + 1) * KC)
            pe.wait_ge(shared_in, 32)
            turn(SHARED)
            pe.wait_ge(x_lo_ready, (last + 2) * KC)
            unit(last, SHARED, None)


SIDE = BATCH * IMW
SCAN_SCALE = 256.0


def scan(nc, io, keep):
    ctx = ExitStack()
    with ctx:
        def sb(name, shape, dt=FP32):
            return ctx.enter_context(nc.sbuf_tensor(name, shape, dt))

        def bank(name):
            return ctx.enter_context(nc.psum_tensor(name, [P, 512], FP32))

        def sem(name):
            return ctx.enter_context(nc.semaphore(name))

        x_tm, ident, state = keep["x_tm"], keep["ident"], keep["state"]
        conv = sb("conv", [P, KC, C])
        conv_hi = sb("conv_hi", [P, KC, C], F16)
        conv_lo = sb("conv_lo", [P, KC, C], F16)
        bias = sb("bias", [1, C])
        bias_hi = sb("bias_hi", [1, C], F16)
        bias_lo = sb("bias_lo", [1, C], F16)
        ones_row = sb("ones_row", [1, SIDE], F16)
        row_hi = sb("row_hi", [P, KC, SIDE], F16)
        row_lo = sb("row_lo", [P, KC, SIDE], F16)
        st = sb("st", [P, NT, 6])
        mv = sb("mv2", [P, NT, 2])
        rstd = sb("rstd2", [P, NT])
        scratch = sb("scratch2", [P, 2 * NT])
        xc = sb("xc", [P, NT, C])

        step_ps = [[bank(f"step_ps{a}{b}") for b in range(2)] for a in range(2)]
        turn_ps = [bank(f"turn2_ps{a}") for a in range(4)]

        conv_in = sem("conv_in")
        hi_ready = sem("conv_hi_ready")
        conv_ready = sem("conv_ready")
        ones_ready = sem("ones_ready")
        xc_ready = sem("xc_ready")
        xc_turned = sem("xc_turned")
        state_ready = sem("state_ready")
        stepped = sem("stepped")
        added = sem("row_added")
        row_hi_ready = sem("row_hi_ready")
        scanned = sem("scanned")
        dve_step = sem("dve_step2")
        block = ctx.enter_context(nc.Block())

        def steps(eng, one):
            with eng.Fori(0, (IMH - 2) // 2) as i:
                one(2 * i, 2 * i + 1, 0)
                one(2 * i + 1, 2 * i + 2, 1)
            one(IMH - 2, IMH - 1, 0)
            one(IMH - 1, IMH - 2, 1)
            with eng.Fori(0, (IMH - 2) // 2) as i:
                one(2 * i + IMH, IMH - 3 - 2 * i, 0)
                one(2 * i + IMH + 1, IMH - 4 - 2 * i, 1)

        @block.sync
        def _(sp):
            sp.dma_start(conv[:, :, :], io["conv_w"].rearrange("(k p) m -> p k m", p=P)).then_inc(conv_in, 16)
            sp.dma_start(bias[:, :], io["conv_b"].rearrange("(a b) -> a b", a=1)).then_inc(conv_in, 16)

        @block.gpsimd
        def _(pool):
            pool.memset(ones_row[:, :], 1.0).then_inc(ones_ready, 1)

        @block.scalar
        def _(act):
            S = nc.scalar
            act.wait_ge(conv_in, 32)
            S.mul(conv_hi[:, :, :], conv[:, :, :], SCAN_SCALE).then_inc(hi_ready, 1)
            S.mul(bias_hi[:, :], bias[:, :], SCAN_SCALE).then_inc(hi_ready, 1)
            for t in range(NT):
                n, h = t // 2, (t % 2) * IMH // 2
                act.wait_ge(xc_turned, t + 1)
                S.copy(state[:, h:h + IMH // 2, :, n, :].rearrange("p h k w -> p k h w"),
                       turn_ps[t % 4][:, :].rearrange("p (k h w) -> p k h w", k=KC, w=IMW)).then_inc(state_ready, 1)

        @block.tensor
        def _(pe):
            T = nc.tensor
            for t in range(NT):
                pe.wait_ge(xc_ready, t + 1)
                if t >= 4:
                    pe.wait_ge(state_ready, t - 3)
                for k in range(KC):
                    mm = T.transpose(turn_ps[t % 4][:, k * P:(k + 1) * P], xc[:, t, k * P:(k + 1) * P], ident[:, :])
                mm.then_inc(xc_turned, 1)
            pe.wait_ge(ones_ready, 1)
            pe.wait_ge(conv_ready, 1)

            def one(s, new, parity):
                def out(m):
                    return step_ps[parity][m // 2][:, (m % 2) * SIDE:(m % 2 + 1) * SIDE]

                pe.wait_ge(added, 2 * s + 1)
                for m in range(KC):
                    T.matmul(out(m), bias_hi[:, m * P:(m + 1) * P], ones_row[:, :], start=(m % 2 == 0), stop=False,
                             skip_group_check=True)
                    T.matmul(out(m), bias_lo[:, m * P:(m + 1) * P], ones_row[:, :], start=False, stop=False,
                             skip_group_check=True)
                for k in range(KC):
                    if k % 2 == 0:
                        pe.wait_ge(scanned, 2 * s + k // 2 + 2)
                    for m in range(KC):
                        c = slice(m * P, (m + 1) * P)
                        T.matmul(out(m), conv_lo[:, k, c], row_hi[:, k, :], start=False, stop=False, skip_group_check=True)
                        T.matmul(out(m), conv_hi[:, k, c], row_hi[:, k, :], start=False, stop=False, skip_group_check=True)
                        mm = T.matmul(out(m), conv_hi[:, k, c], row_lo[:, k, :], start=False, stop=(k == KC - 1),
                                      skip_group_check=True)
                        if k == KC - 1 and m % 2:
                            mm.then_inc(stepped, 1)

            steps(pe, one)

        @block.vector
        def _(dve):
            V = nc.vector
            done = [0]

            def link(ins):
                done[0] += 1
                ins.then_inc(dve_step, 1)
                dve.wait_ge(dve_step, done[0])

            dve.sem_inc(added, 3)
            dve.sem_inc(scanned, 1)
            for t in range(NT):
                V.bn_stats(st[:, t, :], x_tm[:, t, :]).then_inc(dve_step, 1)
            for t in range(NT):
                dve.wait_ge(dve_step, t + 1)
                V.bn_aggr(mv[:, t, :], st[:, t, :]).then_inc(dve_step, 1)
            done[0] = 2 * NT
            dve.wait_ge(dve_step, done[0])
            rsqrt(nc, link, rstd[:, :], mv[:, :, 1], 1.0, LN_C_EPS, scratch)
            link(V.tensor_scalar(rstd[:, :], rstd[:, :], SCAN_SCALE, None, ALU.mult))
            for t in range(NT):
                V.tensor_scalar(xc[:, t, :], x_tm[:, t, :], mv[:, t, 0:1], rstd[:, t:t + 1],
                                ALU.subtract, ALU.mult).then_inc(xc_ready, 1)
            dve.wait_ge(hi_ready, 2)
            V.scalar_tensor_tensor(bias_lo[:, :], bias[:, :], SCAN_SCALE, bias_hi[:, :], ALU.mult, ALU.subtract)
            V.scalar_tensor_tensor(conv_lo[:, :, :], conv[:, :, :], SCAN_SCALE, conv_hi[:, :, :],
                                   ALU.mult, ALU.subtract).then_inc(conv_ready, 1)
            dve.wait_ge(state_ready, NT)

            def chunks(new, g):
                k = slice(2 * g, 2 * g + 2)
                row = state[:, new, k, :, :].rearrange("p k n w -> p k (n w)") if isinstance(new, int) else \
                    state[:, bass.ds(new, 1), k, :, :].rearrange("p o k n w -> p (o k) (n w)")
                return k, row

            for g in range(2):
                k, row = chunks(0, g)
                link(V.tensor_scalar(row_hi[:, k, :], row, 1.0 / SCAN_SCALE, None, ALU.mult))
                V.scalar_tensor_tensor(row_lo[:, k, :], row, 1.0 / SCAN_SCALE, row_hi[:, k, :],
                                       ALU.mult, ALU.subtract).then_inc(scanned, 1)

            def one(s, new, parity):
                for g in range(2):
                    k, row = chunks(new, g)
                    dve.wait_ge(stepped, 2 * s + g + 1)
                    dve.nop(nofuse=True)
                    V.scalar_tensor_tensor(row, step_ps[parity][g][:, 0:2 * SIDE].rearrange("p (k c) -> p k c", k=2),
                                           0.0, row, ALU.max, ALU.add).then_inc(added, 1)
                    dve.wait_ge(added, 2 * s + g + 4)
                    dve.nop(nofuse=True)
                    V.tensor_scalar(row_hi[:, k, :], row, 1.0 / SCAN_SCALE, None, ALU.mult).then_inc(row_hi_ready, 1)
                    dve.wait_ge(row_hi_ready, 2 * s + g + 1)
                    dve.nop(nofuse=True)
                    V.scalar_tensor_tensor(row_lo[:, k, :], row, 1.0 / SCAN_SCALE, row_hi[:, k, :],
                                           ALU.mult, ALU.subtract).then_inc(scanned, 1)

            steps(dve, one)


def ternary_ffn(nc, io, keep):
    ctx = ExitStack()
    with ctx:
        def sb(name, shape, dt=FP32):
            return ctx.enter_context(nc.sbuf_tensor(name, shape, dt))

        def bank(name):
            return ctx.enter_context(nc.psum_tensor(name, [P, 512], FP32))

        def sem(name):
            return ctx.enter_context(nc.semaphore(name))

        x_tm, ident, state = keep["x_tm"], keep["ident"], keep["state"]
        ternary, inv_ws = keep["ternary"], keep["inv_ws"]
        ident_b = sb("ident_b", [P, P], BF16)
        st = sb("st3", [P, NT, 6])
        mv = sb("mv3", [P, NT, 2])
        rstd = sb("rstd3", [P, NT])
        scratch = sb("scratch3", [P, 2])
        z = sb("z3", [P, 2, C])
        zsq = sb("zsq3", [P, C])
        stat = sb("stat", [P, NT, 16])
        zr = sb("zr", [P, C])
        q = sb("q", [P, 2, C], BF16)
        q_cm = sb("q_cm", [P, 2, KC, P], BF16)
        silu = sb("silu", [P, 2, 512])
        h = sb("h", [P, 2, W1])
        hsq = sb("hsq", [P, W1])
        hr = sb("hr", [P, 2, W1])
        hq = sb("hq", [P, 2, W1], BF16)
        h_cm = sb("h_cm", [P, 2, W3, P], BF16)
        stack = sb("stack", [P, NT, KC, P])
        out_cm = sb("out_cm", [P, KC, TOK])

        gu_ps = [bank("g0"), bank("u0"), bank("g1"), bank("u1")]
        ht_ps = [bank("ht0"), bank("ht1")]
        x_ps = bank("x_ps")
        y_ps = bank("y3_ps")

        ident_ready = sem("ident_ready")
        stack_ready = sem("stack_ready")
        stack_turned = sem("stack_turned")
        x3_ready = sem("x3_ready")
        z_ready = sem("z3_ready")
        zsq_ready = sem("zsq3_ready")
        q_ready = sem("q_ready")
        q_turned = sem("q_turned")
        q_cm_ready = sem("q_cm_ready")
        gu_summed = sem("gu3_summed")
        silu_ready = sem("silu3_ready")
        h_ready = sem("h3_ready")
        hsq_ready = sem("hsq_ready")
        hscale_ready = sem("hscale_ready")
        hr_ready = sem("hr_ready")
        hq_ready = sem("hq_ready")
        h_turned = sem("h_turned")
        h_cm_ready = sem("h_cm_ready")
        y_summed = sem("y3_summed")
        x4_ready = sem("x4_ready")
        x4_turned = sem("x4_turned")
        out_ready = sem("out_ready")
        out_sent = sem("out_sent")
        dve_step = sem("dve_step3")
        block = ctx.enter_context(nc.Block())

        PARTS = [(0, 512), (512, 512), (1024, 384)]
        w1 = ternary[:, 0, :].rearrange("p (k m) -> p k m", m=W1)
        w2 = ternary[:, 1, :].rearrange("p (k m) -> p k m", m=W1)
        w3 = ternary[:, 2, :].rearrange("p (k m) -> p k m", m=C)
        INV_Q, Q, G_SCALE, U_SCALE, HMAX, HSS, HRMS, HA, HQ, Y_SCALE, ZMAX, ZSS, ZRMS, ZA = range(14)

        def col(t, i):
            return stat[:, t, i:i + 1]

        def half(ps, n=512):
            return ps[:, :].bitcast(BF16)[:, 0:n]

        @block.sync
        def _(sp):
            for n in range(BATCH):
                sp.wait_ge(out_ready, 2 * n + 2)
                sp.dma_start(io["out"][n].rearrange("(k p) h w -> p k (h w)", p=P),
                             out_cm[:, :, n * SP:(n + 1) * SP]).then_inc(out_sent, 16)
            sp.wait_ge(out_sent, 16 * BATCH)

        @block.gpsimd
        def _(pool):
            for t in range(NT):
                n, row = t // 2, (t % 2) * IMH // 2
                nc.gpsimd.tensor_copy(stack[:, t, :, :].rearrange("p k (h w) -> p k h w", w=IMW),
                                      state[:, row:row + IMH // 2, :, n, :].rearrange("p h k w -> p k h w")).then_inc(stack_ready, 1)

        @block.scalar
        def _(act):
            S = nc.scalar
            S.copy(ident_b[:, :], ident[:, :]).then_inc(ident_ready, 1)

            def square_z(t):
                act.wait_ge(z_ready, t + 1)
                if t:
                    act.wait_ge(zsq_ready, t)
                S.activation(zsq[:, :], z[:, t % 2, :], ACT.Square, accum_out=col(t, ZSS)).then_inc(zsq_ready, 1)

            def q_copy(t):
                act.wait_ge(q_turned, t + 1)
                S.copy(q_cm[:, t % 2, :, :], half(ht_ps[1]).rearrange("p (k m) -> p k m", k=KC)).then_inc(q_cm_ready, 1)

            square_z(0)
            q_copy(0)
            square_z(1)
            for t in range(NT + 2):
                if t < NT:
                    for i, (c, n) in enumerate(PARTS):
                        g = 3 * t + i
                        act.wait_ge(gu_summed, g + 1)
                        if g >= 2:
                            act.wait_ge(h_ready, g - 1)
                        S.activation(silu[:, g % 2, 0:n], gu_ps[2 * (g % 2)][:, 0:n], ACT.Silu,
                                     scale=col(t, G_SCALE)).then_inc(silu_ready, 1)
                    act.wait_ge(h_ready, 3 * t + 3)
                    if t:
                        act.wait_ge(hsq_ready, t)
                    S.activation(hsq[:, :], h[:, t % 2, :], ACT.Square, accum_out=col(t, HSS)).then_inc(hsq_ready, 1)
                if 1 <= t <= NT:
                    s = t - 1
                    act.wait_ge(h_turned, s + 1)
                    S.copy(h_cm[:, s % 2, 0:8, :], half(ht_ps[0], 1024).rearrange("p (k m) -> p k m", k=8)).then_inc(h_cm_ready, 1)
                    S.copy(h_cm[:, s % 2, 8:W3, :], half(ht_ps[1], 384).rearrange("p (k m) -> p k m", k=3)).then_inc(h_cm_ready, 1)
                if t + 2 < NT:
                    square_z(t + 2)
                if t + 1 < NT:
                    q_copy(t + 1)
                if t < NT:
                    act.wait_ge(hscale_ready, t + 1)
                    S.activation(hr[:, t % 2, :], h[:, t % 2, :], ACT.Copy, bias=ROUND, scale=col(t, HQ)).then_inc(hr_ready, 1)
                if t >= 2:
                    s = t - 2
                    act.wait_ge(x4_turned, s + 1)
                    S.copy(out_cm[:, :, s * P:(s + 1) * P], x_ps[:, :].rearrange("p (k m) -> p k m", k=KC)).then_inc(out_ready, 1)

        @block.tensor
        def _(pe):
            T = nc.tensor
            pe.wait_ge(ident_ready, 1)

            def turn_stack(t):
                pe.wait_ge(stack_ready, t + 1)
                if t >= 1:
                    pe.wait_ge(x3_ready, t)
                if t >= 5:
                    pe.wait_ge(out_ready, t - 4)
                for k in range(KC):
                    mm = T.transpose(x_ps[:, k * P:(k + 1) * P], stack[:, t, k, :], ident[:, :])
                mm.then_inc(stack_turned, 1)

            def turn_q(t):
                pe.wait_ge(q_ready, t + 1)
                if t >= 2:
                    pe.wait_ge(h_cm_ready, 2 * (t - 1))
                for k in range(KC):
                    mm = T.transpose(half(ht_ps[1])[:, k * P:(k + 1) * P], q[:, t % 2, k * P:(k + 1) * P], ident_b[:, :])
                mm.then_inc(q_turned, 1)

            turn_stack(0)
            turn_q(0)
            turn_stack(1)
            for t in range(NT + 2):
                if t < NT:
                    pe.wait_ge(q_cm_ready, t + 1)
                    for i, (c, n) in enumerate(PARTS):
                        g = 3 * t + i
                        if g >= 2:
                            pe.wait_ge(h_ready, g - 1)
                        for w, ps in ((w1, gu_ps[2 * (g % 2)]), (w2, gu_ps[2 * (g % 2) + 1])):
                            for k in range(KC):
                                mm = T.matmul(ps[:, 0:n], q_cm[:, t % 2, k, :], w[:, k, c:c + n],
                                              start=(k == 0), stop=(k == KC - 1))
                        mm.then_inc(gu_summed, 1)
                if 1 <= t <= NT:
                    s = t - 1
                    pe.wait_ge(hq_ready, s + 1)
                    if t < NT:
                        pe.wait_ge(q_cm_ready, t + 1)
                    if s >= 1:
                        pe.wait_ge(h_cm_ready, 2 * s)
                    for k in range(W3):
                        dst = half(ht_ps[0], 1024)[:, k * P:(k + 1) * P] if k < 8 else half(ht_ps[1])[:, (k - 8) * P:(k - 7) * P]
                        mm = T.transpose(dst, hq[:, s % 2, k * P:(k + 1) * P], ident_b[:, :])
                    mm.then_inc(h_turned, 1)
                if t + 2 < NT:
                    turn_stack(t + 2)
                if t + 1 < NT:
                    if t >= 1:
                        pe.wait_ge(h_cm_ready, 2 * t)
                    turn_q(t + 1)
                if 1 <= t <= NT:
                    s = t - 1
                    pe.wait_ge(h_cm_ready, 2 * s + 2)
                    if s >= 1:
                        pe.wait_ge(x4_ready, s)
                    for k in range(W3):
                        mm = T.matmul(y_ps[:, :], h_cm[:, s % 2, k, :], w3[:, k, :], start=(k == 0), stop=(k == W3 - 1))
                    mm.then_inc(y_summed, 1)
                if t >= 2:
                    s = t - 2
                    pe.wait_ge(x4_ready, s + 1)
                    pe.wait_ge(x3_ready, min(t + 3, NT))
                    if s >= 1:
                        pe.wait_ge(out_ready, s)
                    for k in range(KC):
                        mm = T.transpose(x_ps[:, k * P:(k + 1) * P], x_tm[:, s, k * P:(k + 1) * P], ident[:, :])
                    mm.then_inc(x4_turned, 1)

        @block.vector
        def _(dve):
            V = nc.vector
            done = [0]

            def link(ins):
                done[0] += 1
                ins.then_inc(dve_step, 1)
                dve.wait_ge(dve_step, done[0])

            def quant_scale(t, rms, top, a, to, inv):
                link(V.tensor_scalar(col(t, a), col(t, top), col(t, rms), QEPS, ALU.mult, ALU.max))
                link(V.tensor_scalar(col(t, inv), col(t, a), 1.0 / 127.0, None, ALU.mult))
                link(V.reciprocal(col(t, to), col(t, a)))
                return V.tensor_scalar(col(t, to), col(t, to), col(t, rms), 127.0, ALU.mult, ALU.mult)

            def norm(t):
                dve.wait_ge(stack_turned, t + 1)
                V.scalar_tensor_tensor(x_tm[:, t, :], x_ps[:, :], 1.0 / SCAN_SCALE, x_tm[:, t, :],
                                       ALU.mult, ALU.add).then_inc(x3_ready, 1)
                dve.wait_ge(x3_ready, t + 1)
                link(V.bn_stats(st[:, t, :], x_tm[:, t, :]))
                link(V.bn_aggr(mv[:, t, :], st[:, t, :]))
                rsqrt(nc, link, rstd[:, t:t + 1], mv[:, t, 1:2], 1.0, LN_T_EPS, scratch)
                V.tensor_scalar(z[:, t % 2, :], x_tm[:, t, :], mv[:, t, 0:1], rstd[:, t:t + 1],
                                ALU.subtract, ALU.mult).then_inc(z_ready, 1)
                dve.wait_ge(z_ready, t + 1)
                link(V.tensor_reduce(col(t, ZMAX), z[:, t % 2, :], AX.X, ALU.max, apply_absolute_value=True))

            def quant(t):
                dve.wait_ge(zsq_ready, t + 1)
                rsqrt(nc, link, col(t, ZRMS), col(t, ZSS), 1.0 / C, RMS_EPS, scratch)
                link(quant_scale(t, ZRMS, ZMAX, ZA, Q, INV_Q))
                link(V.tensor_tensor(col(t, G_SCALE), col(t, INV_Q), inv_ws[:, 0:1], ALU.mult))
                link(V.tensor_tensor(col(t, U_SCALE), col(t, INV_Q), inv_ws[:, 1:2], ALU.mult))
                link(V.tensor_scalar(zr[:, :], z[:, t % 2, :], col(t, Q), ROUND, ALU.mult, ALU.add))
                V.tensor_scalar(q[:, t % 2, :], zr[:, :], -ROUND, -32.0, ALU.add, ALU.max).then_inc(q_ready, 1)

            norm(0)
            quant(0)
            norm(1)
            for t in range(NT + 1):
                if t < NT:
                    for i, (c, n) in enumerate(PARTS):
                        g = 3 * t + i
                        dve.wait_ge(silu_ready, g + 1)
                        V.scalar_tensor_tensor(h[:, t % 2, c:c + n], gu_ps[2 * (g % 2) + 1][:, 0:n], col(t, U_SCALE),
                                               silu[:, g % 2, 0:n], ALU.mult, ALU.mult).then_inc(h_ready, 1)
                    if t + 2 < NT:
                        norm(t + 2)
                    dve.wait_ge(h_ready, 3 * t + 3)
                    link(V.tensor_reduce(col(t, HMAX), h[:, t % 2, :], AX.X, ALU.max, apply_absolute_value=True))
                    dve.wait_ge(hsq_ready, t + 1)
                    rsqrt(nc, link, col(t, HRMS), col(t, HSS), 1.0 / W1, RMS_EPS, scratch)
                    quant_scale(t, HRMS, HMAX, HA, HQ, Y_SCALE).then_inc(hscale_ready, 1)
                    link(V.tensor_tensor(col(t, Y_SCALE), col(t, Y_SCALE), inv_ws[:, 2:3], ALU.mult))
                    if t + 1 < NT:
                        quant(t + 1)
                if t >= 1:
                    s = t - 1
                    dve.wait_ge(y_summed, s + 1)
                    V.scalar_tensor_tensor(x_tm[:, s, :], y_ps[:, :], col(s, Y_SCALE), x_tm[:, s, :],
                                           ALU.mult, ALU.add).then_inc(x4_ready, 1)
                if t < NT:
                    dve.wait_ge(hr_ready, t + 1)
                    V.tensor_scalar(hq[:, t % 2, :], hr[:, t % 2, :], -ROUND, -32.0, ALU.add, ALU.max).then_inc(hq_ready, 1)


def program(nc, io):
    with ExitStack() as ctx:
        def sb(name, shape, dt=FP32):
            return ctx.enter_context(nc.sbuf_tensor(name, shape, dt))
        keep = {
            "x_tm": sb("x_tm", [P, NT, C]),
            "ident": sb("ident", [P, P]),
            "aff": sb("aff", [P, NT, TOPK]),
            "slots": sb("slots", [P, NT, TOPK], U32),
            "rounds": sb("rounds", [P, 1], U32),
            "narrow": sb("narrow", [P, MAX_ROUNDS * EXPERTS], U32),
            "token_ids": sb("token_ids", [P, NT], U32),
            "ternary": sb("ternary", [P, 3, KC * W1], F8),
            "inv_ws": sb("inv_ws", [P, 3]),
        }
        attention_and_routing(nc, io, keep)
        experts(nc, io, keep)
        keep["state"] = sb("state", [P, IMH, KC, BATCH, IMW])
        scan(nc, io, keep)
        ternary_ffn(nc, io, keep)


def kernel(**inputs):
    import concourse.bacc as bacc
    from concourse.bass_utils import run_bass_kernel_spmd

    nc = bacc.Bacc("TRN2", target_bir_lowering=False, num_devices=1)
    a = {k: np.asarray(v) for k, v in inputs.items()}
    host = {
        "x": a["x"],
        "w1t": a["L0_conv_w1"].T, "w2t": a["L0_conv_w2"].T, "w3t": a["L0_conv_w3"].T,
        "b1": a["L0_conv_b1"], "b2": a["L0_conv_b2"], "b3": a["L0_conv_b3"], "alpha": a["L0_conv_alpha"],
        "lnw": a["L0_ffn_ln_weight"], "router": a["L0_ffn_router_weight"],
        "gate_up": a["L0_ffn_gate_up_proj"], "down": a["L0_ffn_down_proj"],
        "sgate": a["L0_ffn_shared_gate_w"], "sup": a["L0_ffn_shared_up_w"], "sdown": a["L0_ffn_shared_down_w"],
        "conv_w": a["L1_conv_W"][:, :, 4, 0].T, "conv_b": a["L1_conv_b"],
        "f1": a["L1_ffn_w1"].T, "f2": a["L1_ffn_w2"].T, "f3": a["L1_ffn_w3"].T,
    }
    host = {k: np.ascontiguousarray(v) for k, v in host.items()}
    io = {k: nc.dram_tensor(f"in_{k}", v.shape, FP32, kind="ExternalInput").ap() for k, v in host.items()}
    io["tokens"] = nc.dram_tensor("tokens", (TOK, C), FP32, kind="Internal").ap()
    io["slot_token"] = nc.dram_tensor("slot_token", (SLOTS, 1), U32, kind="Internal").ap()
    io["slot_y"] = nc.dram_tensor("slot_y", (SLOTS, C), FP32, kind="Internal").ap()
    io["out"] = nc.dram_tensor("out", a["x"].shape, FP32, kind="ExternalOutput").ap()
    program(nc, io)
    r = run_bass_kernel_spmd(nc, [{f"in_{k}": v for k, v in host.items()}], core_ids=[0])
    return r.results[0]["out"]
```

```python
from contextlib import ExitStack

import numpy as np

import concourse.bass as bass
from concourse import mybir
from concourse.alu_op_type import AluOpType as ALU

FP32 = mybir.dt.float32
F32R = mybir.dt.float32r
BF16 = mybir.dt.bfloat16
U32 = mybir.dt.uint32
F16 = mybir.dt.float16
F8 = mybir.dt.float8e4
ACT = mybir.ActivationFunctionType
AX = mybir.AxisListType

P = 128
BATCH, C, IMH, IMW = 4, 512, 16, 16
SP = IMH * IMW
TOK = BATCH * SP
NT = TOK // P
KC = C // P
D = 64
EXPERTS, TOPK = 16, 4
FF = 1024
CAP = 320
MAX_ROUNDS = -(-TOK // CAP)
ROUND_SLOTS = EXPERTS * CAP
SLOTS = -(-(MAX_ROUNDS * EXPERTS + 1) * CAP // P) * P
NARROW = (288, 2 * P)
W1, W3 = 1408, 1408 // P
ROUND = 12582912.0
QEPS = 1e-5
LN_C_EPS, LN_T_EPS, RMS_EPS = 1e-6, 1e-5, 1e-6
BOTH_SCALE, BOTH_EPS = 1.0 + RMS_EPS, LN_T_EPS * RMS_EPS
GROUP = 4
ABS_PARTS = 4
ABS_TILES = 4

FH = FF // P
PIECE = 2048
PIECES = 6
RING = 3
HALF = TOK // 2
DOWN_K = 4
LOW_SCALE = 256.0
BACK_RING = 8


def gu_view(piece):
    return piece.rearrange("p (k g c) -> p k g c", k=KC, g=2)


def gate_up_piece(piece, j, gate, up):
    v, cols = gu_view(piece), slice(j * 256, (j + 1) * 256)
    return [(v[:, :, 0, :], gate[:, :, cols]), (v[:, :, 1, :], up[:, :, cols])]


def shared_sources(io):
    return (io["sgate"].rearrange("(k p) f -> p k f", p=P), io["sup"].rearrange("(k p) f -> p k f", p=P),
            io["sdown"].rearrange("(k p) c -> p k c", p=P))


RSQRT_SEED = 1597463007.0


def rsqrt(nc, link, out, v, scale, eps, scratch):
    V, n = nc.vector, out.shape[-1]
    a, t = scratch[:, 0:n], scratch[:, n:2 * n]
    link(V.tensor_scalar(a, v, scale, eps, ALU.mult, ALU.add))
    link(V.tensor_scalar(t.bitcast(U32), a.bitcast(U32), 1, None, ALU.logical_shift_right))
    link(V.tensor_scalar(out.bitcast(U32), t.bitcast(U32), -1.0, RSQRT_SEED, ALU.mult, ALU.add))
    for _ in range(3):
        link(V.tensor_tensor(t, out, out, ALU.mult))
        link(V.scalar_tensor_tensor(t, t, -0.5, a, ALU.mult, ALU.mult))
        link(V.scalar_tensor_tensor(out, t, 1.5, out, ALU.add, ALU.mult))


def attention_and_routing(nc, io, keep):
    ctx = ExitStack()
    with ctx:
        def sb(name, shape, dt=FP32):
            return ctx.enter_context(nc.sbuf_tensor(name, shape, dt))

        def bank(name):
            return ctx.enter_context(nc.psum_tensor(name, [P, 512], FP32))

        def sem(name):
            return ctx.enter_context(nc.semaphore(name))

        raw = keep["raw"]
        x_cm = raw[:, :, :].rearrange("p a (k t) -> p (a k) t", k=KC // 2)
        x_tm = keep["x_tm"]
        xn_tm = sb("xn_tm", [P, NT, C])
        xn_cm = sb("xn_cm", [P, KC, TOK])
        w12 = sb("w12", [P, KC, 2 * D])
        w3 = sb("w3", [P, KC, C])
        b12 = sb("b12", [D, 2])
        b3 = sb("b3", [P, C])
        part = sb("part", [P, C])
        alpha = sb("alpha", [P, 1])
        lnw = sb("lnw", [P, C])
        router = sb("router", [P, KC, EXPERTS])
        stats = sb("stats", [P, NT, 6])
        mv = sb("mv", [P, NT, 2])
        rstd = sb("rstd", [P, NT])
        e12 = sb("e12", [D, 2, 2, SP])
        nmax = sb("nmax", [P, NT])
        prob = sb("prob", [P, 2, SP])
        psum_row = sb("psum_row", [P, NT])
        gain = sb("gain", [P, NT])
        prob_t = sb("prob_t", [P, 2, SP])
        stats1 = sb("stats1", [P, NT, 6])
        mv1 = sb("mv1", [P, NT, 2])
        rstd1 = sb("rstd1", [P, NT])
        scratch = sb("scratch", [P, 2 * GROUP])
        zn_first = keep["rows"]
        zn_rest = sb("zn_rest", [P, NT - GROUP, C])
        abs_w = zn_rest[:, 0:2, :].rearrange("p t c -> p (t c)").bitcast(BF16)
        zn_cm = sb("zn_cm", [P, 2, KC, P])
        logits = sb("logits", [P, NT, EXPERTS])
        top = sb("top", [P, NT, 8])
        top_at = sb("top_at", [P, NT, 8], U32)
        top_at_f = sb("top_at_f", [P, NT, TOPK])
        elog = sb("elog", [P, NT, EXPERTS])
        esum = sb("esum", [P, NT])
        resum = sb("resum", [P, NT])
        etop = sb("etop", [P, NT, TOPK])
        expert_ids = sb("expert_ids", [P, EXPERTS])
        onehot = sb("onehot", [P, TOPK, NT, EXPERTS])
        mask = sb("mask", [P, NT, EXPERTS])
        before = sb("before", [P, NT, EXPERTS])
        totals = sb("totals", [P, NT, EXPERTS])
        run = sb("run", [P, NT + 1, EXPERTS])
        wraps = sb("wraps", [P, MAX_ROUNDS, NT, EXPERTS])
        slot_e = sb("slot_e", [P, NT, EXPERTS])
        base = sb("base", [P, EXPERTS])
        picked = sb("picked", [P, TOPK, NT, EXPERTS])
        slot_f = sb("slot_f", [P, NT, TOPK])
        most = sb("most", [P, 1])
        most2 = sb("most2", [P, 4])
        room = sb("room", [P, 2, MAX_ROUNDS, EXPERTS])
        zero_list = sb("zero_list", [P, SLOTS // P], U32)
        upper = sb("upper", [P, P])
        ones = sb("ones", [P, P])
        weights = sb("weights", [P, 3, KC * W1])
        abs_part = sb("abs_part", [P, 3, ABS_PARTS])
        abs_sum = sb("abs_sum", [P, 3])
        abs_all = sb("abs_all", [P, 3])
        w_scale = sb("w_scale", [P, 3])
        ternary, inv_ws = keep["ternary"], keep["inv_ws"]
        ident = keep["ident"]
        aff, slots, rounds = keep["aff"], keep["slots"], keep["rounds"]
        token_ids, narrow = keep["token_ids"], keep["narrow"]

        pa = [bank("pa0"), bank("pa1")]
        pb = [bank("pb0"), bank("pb1")]
        pe_ = bank("pe_")
        ps = bank("ps")
        pt = bank("pt")
        pg = bank("pg")

        x_in = [sem(f"x_in{n}") for n in range(BATCH)]
        w_in = sem("w_in")
        last_in = [sem(f"last_in{i}") for i in range(3)]
        abs_ready = sem("abs_ready")
        abs_added = sem("abs_added")
        abs_summed = sem("abs_summed")
        scale_ready = sem("scale_ready")
        rounded = sem("rounded")
        cut = sem("cut")
        const_ready = sem("const_ready")
        pool_step = sem("pool_step")
        x_turned = sem("x_turned")
        x_kept = sem("x_kept")
        xn_ready = sem("xn_ready")
        xn_turned = sem("xn_turned")
        xn_cm_ready = sem("xn_cm_ready")
        e_summed = sem("e_summed")
        e_ready = sem("e_ready")
        scored = sem("scored")
        max_ready = sem("max_ready")
        prob_ready = sem("prob_ready")
        prob_turned = sem("prob_turned")
        prob_t_ready = sem("prob_t_ready")
        w3_summed = sem("w3_summed")
        w3_added = sem("w3_added")
        mixed = sem("mixed")
        x1_ready = sem("x1_ready")
        zn_ready = sem("zn_ready")
        zn_turned = sem("zn_turned")
        zn_cm_ready = sem("zn_cm_ready")
        routed = sem("routed")
        shifted_ready = sem("shifted_ready")
        elog_ready = sem("elog_ready")
        mask_ready = sem("mask_ready")
        counted = sem("counted")
        zeroed = sem("zeroed")
        zn_out = sem("zn_out")
        first_in = sem("first_in")
        dve_step = sem("dve_step")

        block = ctx.enter_context(nc.Block())
        FIRST, REST = range(GROUP), range(GROUP, NT)

        def zn(t):
            return zn_first[:, t, :] if t < GROUP else zn_rest[:, t - GROUP, :]

        def zn_bank(t):
            return pg if t < GROUP else (pa[0], pa[1], pb[0], pt)[t - GROUP]

        @block.sync
        def _(sp):
            for n in range(BATCH):
                sp.dma_start(x_cm[:, :, n * SP:(n + 1) * SP],
                             io["x"][n].rearrange("(k p) h w -> p k (h w)", p=P)).then_inc(x_in[n], 16)
            sp.wait_ge(w_in, 9 * 16)
            for i, name in enumerate(("f1", "f2", "f3")):
                sp.dma_start(weights[:, i, :].rearrange("p (k m) -> p k m", m=io[name].shape[1]),
                             io[name].rearrange("(k p) m -> p k m", p=P)).then_inc(last_in[i], 16)
            sp.wait_ge(x_turned, NT)
            for j in range(2):
                for dst, src in gate_up_piece(raw[:, j, :], j, *shared_sources(io)[0:2]):
                    sp.dma_start(dst, src).then_inc(first_in, 16)
            for t in range(NT):
                sp.wait_ge(zn_ready, t + 1)
                sp.dma_start(io["tokens"][t * P:(t + 1) * P, :], zn(t)).then_inc(zn_out, 16)
            sp.wait_ge(zn_out, 16 * NT)
            sp.wait_ge(first_in, 4 * 16)

        @block.gpsimd
        def _(pool):
            pool.memset(ident[:, :], 0.0).then_inc(pool_step, 1)
            pool.memset(ones[:, :], 1.0).then_inc(pool_step, 1)
            pool.memset(zero_list[:, :], 0).then_inc(pool_step, 1)
            pool.wait_ge(pool_step, 3)
            pool.affine_select(out=ident[:, :], in_=ident[:, :], compare_op=ALU.not_equal, fill=1.0,
                               base=0, pattern=[[-1, P]], channel_multiplier=1).then_inc(const_ready, 1)
            pool.affine_select(out=upper[:, :], in_=ones[:, :], compare_op=ALU.is_gt, fill=0.0,
                               base=0, pattern=[[1, P]], channel_multiplier=-1).then_inc(const_ready, 1)
            pool.iota(expert_ids[:, :], pattern=[[1, EXPERTS]], base=0, channel_multiplier=0,
                      allow_small_or_imprecise_dtypes=True).then_inc(const_ready, 1)
            pool.iota(base[:, :], pattern=[[CAP, EXPERTS]], base=0, channel_multiplier=0,
                      allow_small_or_imprecise_dtypes=True).then_inc(const_ready, 1)
            pool.iota(token_ids[:, :], pattern=[[P, NT]], base=0, channel_multiplier=1).then_inc(const_ready, 1)
            pool.dma_start(io["slot_token"].rearrange("(p a) o -> p (a o)", p=P), zero_list[:, :]).then_inc(zeroed, 16)
            pool.wait_ge(abs_added, 1)
            nc.gpsimd.partition_all_reduce(abs_all[:, :], abs_sum[:, :], P, bass.bass_isa.ReduceOp.add).then_inc(abs_summed, 1)
            pool.wait_ge(scale_ready, 1)
            for i in range(2):
                nc.gpsimd.tensor_scalar(weights[:, i, :], weights[:, i, :], w_scale[:, i:i + 1], ROUND,
                                        ALU.mult, ALU.add).then_inc(rounded, 1)
            pool.wait_ge(zeroed, 16)

        @block.scalar
        def _(act):
            act.dma_start(w12[:, :, 0:D], io["w1t"].rearrange("(k p) m -> p k m", p=P)).then_inc(w_in, 16)
            act.dma_start(w12[:, :, D:2 * D], io["w2t"].rearrange("(k p) m -> p k m", p=P)).then_inc(w_in, 16)
            act.dma_start(b12[:, 0:1], io["b1"].rearrange("(a b) -> a b", b=1)).then_inc(w_in, 16)
            act.dma_start(b12[:, 1:2], io["b2"].rearrange("(a b) -> a b", b=1)).then_inc(w_in, 16)
            act.dma_start(w3[:, :, :], io["w3t"].rearrange("(k p) m -> p k m", p=P)).then_inc(w_in, 16)
            act.dma_start(b3[:, :], io["b3"].rearrange("(a b) -> a b", a=1).to_broadcast([P, C])).then_inc(w_in, 16)
            act.dma_start(alpha[:, :], io["alpha"].rearrange("(a b) -> a b", a=1).to_broadcast([P, 1])).then_inc(w_in, 16)
            act.dma_start(lnw[:, :], io["lnw"].rearrange("(a b) -> a b", a=1).to_broadcast([P, C])).then_inc(w_in, 16)
            act.dma_start(router[:, :, :], io["router"].rearrange("(k p) m -> p k m", p=P)).then_inc(w_in, 16)
            for t in range(NT):
                act.wait_ge(x_turned, t + 1)
                nc.scalar.copy(x_tm[:, t, :], pa[t % 2][:, :]).then_inc(x_kept, 1)

            def xn_copy(t):
                act.wait_ge(xn_turned, t + 1)
                nc.scalar.copy(xn_cm[:, :, t * P:(t + 1) * P],
                               pb[t % 2][:, :].rearrange("p (k m) -> p k m", k=KC)).then_inc(xn_cm_ready, 1)

            def relu(n):
                act.wait_ge(e_summed, n + 1)
                if n >= 2:
                    act.wait_ge(scored, 2 * (n - 1))
                for j in range(2):
                    nc.scalar.activation(e12[:, n % 2, j, :], pe_[0:D, j * SP:(j + 1) * SP], ACT.Relu,
                                         bias=b12[:, j:j + 1]).then_inc(e_ready, 1)

            def exp(s):
                act.wait_ge(max_ready, s + 1)
                if s >= 2:
                    act.wait_ge(prob_turned, s - 1)
                nc.scalar.activation(prob[:, s % 2, :], ps[:, 0:SP], ACT.Exp,
                                     bias=nmax[:, s:s + 1], accum_out=psum_row[:, s:s + 1]).then_inc(prob_ready, 1)

            def sum_abs(j):
                i, part = divmod(j, ABS_PARTS)
                n = KC * W1 // ABS_PARTS
                if part == 0:
                    act.wait_ge(last_in[i], 16)
                if j:
                    act.wait_ge(abs_ready, j)
                nc.scalar.activation(abs_w[:, 0:n], weights[:, i, part * n:(part + 1) * n], ACT.Abs,
                                     accum_out=abs_part[:, i, part:part + 1]).then_inc(abs_ready, 1)

            def make_ternary(i, count):
                act.wait_ge(cut, count)
                nc.scalar.activation(ternary[:, i, :], weights[:, i, :], ACT.Copy, bias=-ROUND, saturate=False)

            def zn_copy(t):
                act.wait_ge(zn_turned, t + 1)
                if t >= 2:
                    act.wait_ge(routed, t - 1)
                nc.scalar.copy(zn_cm[:, t % 2, :, :],
                               zn_bank(t)[:, :].rearrange("p (k m) -> p k m", k=KC)).then_inc(zn_cm_ready, 1)

            for t in FIRST:
                xn_copy(t)
            act.wait_ge(w_in, 9 * 16)
            relu(0)
            exp(0)
            for s in range(NT):
                if s + 1 < NT:
                    if (s + 1) % 2 == 0:
                        relu((s + 1) // 2)
                    exp(s + 1)
                if s < ABS_TILES:
                    for j in range(s * 3 * ABS_PARTS // ABS_TILES, (s + 1) * 3 * ABS_PARTS // ABS_TILES):
                        sum_abs(j)
                if s >= 6:
                    zn_copy(2 * (s - 6))
                act.wait_ge(prob_turned, s + 1)
                if s >= 2:
                    act.wait_ge(mixed, s - 1)
                nc.scalar.copy(prob_t[:, s % 2, :], pt[:, 0:SP]).then_inc(prob_t_ready, 1)
                if s == 0:
                    for t in REST:
                        xn_copy(t)
                if s >= 6:
                    zn_copy(2 * (s - 6) + 1)
            make_ternary(2, 1)
            for t in REST:
                zn_copy(t)
            make_ternary(0, 2)
            act.wait_ge(shifted_ready, 2)
            nc.scalar.activation(elog[:, :, :], elog[:, :, :], ACT.Exp).then_inc(elog_ready, 1)
            nc.scalar.activation(etop[:, :, :], etop[:, :, :], ACT.Exp).then_inc(elog_ready, 1)
            make_ternary(1, 3)

        @block.tensor
        def _(pe):
            pe.wait_ge(const_ready, 2)
            for t in range(NT):
                if t % 2 == 0:
                    pe.wait_ge(x_in[t // 2], 16)
                if t >= 2:
                    pe.wait_ge(x_kept, t - 1)
                for k in range(KC):
                    mm = nc.tensor.transpose(pa[t % 2][:, k * P:(k + 1) * P], x_cm[:, k, t * P:(t + 1) * P],
                                             ident[:, :])
                mm.then_inc(x_turned, 1)

            def turn_xn(t):
                pe.wait_ge(xn_ready, t + 1)
                if t >= 2:
                    pe.wait_ge(xn_cm_ready, t - 1)
                for k in range(KC):
                    mm = nc.tensor.transpose(pb[t % 2][:, k * P:(k + 1) * P], xn_tm[:, t, k * P:(k + 1) * P],
                                             ident[:, :])
                mm.then_inc(xn_turned, 1)

            def reduce(n):
                pe.wait_ge(xn_cm_ready, 2 * n + 2)
                if n >= 1:
                    pe.wait_ge(e_ready, 2 * n)
                for j in range(2):
                    for k in range(KC):
                        mm = nc.tensor.matmul(pe_[0:D, j * SP:(j + 1) * SP], w12[:, k, j * D:(j + 1) * D],
                                              xn_cm[:, k, n * SP:(n + 1) * SP], start=(k == 0), stop=(k == KC - 1))
                mm.then_inc(e_summed, 1)

            def score(s):
                n, i = divmod(s, 2)
                pe.wait_ge(e_ready, 2 * n + 2)
                if s >= 1:
                    pe.wait_ge(prob_ready, s)
                nc.tensor.matmul(ps[:, 0:SP], e12[:, n % 2, 0, i * P:(i + 1) * P], e12[:, n % 2, 1, :],
                                 start=True, stop=True).then_inc(scored, 1)

            def assemble(s):
                if s >= 2:
                    pe.wait_ge(w3_added, s - 1)
                else:
                    pe.wait_ge(x_kept, NT)
                for k in range(KC):
                    mm = nc.tensor.matmul(pa[s % 2][:, :], xn_cm[:, k, s * P:(s + 1) * P], w3[:, k, :],
                                          start=(k == 0), stop=(k == KC - 1))
                mm.then_inc(w3_summed, 1)

            def turn_prob(s):
                pe.wait_ge(prob_ready, s + 1)
                if s >= 1:
                    pe.wait_ge(prob_t_ready, s)
                for j in range(2):
                    mm = nc.tensor.transpose(pt[:, j * P:(j + 1) * P], prob[:, s % 2, j * P:(j + 1) * P], ident[:, :])
                mm.then_inc(prob_turned, 1)

            def mix(s):
                pe.wait_ge(prob_t_ready, s + 1)
                if s >= 2:
                    pe.wait_ge(x1_ready, s - 1)
                else:
                    pe.wait_ge(xn_cm_ready, NT)
                for j in range(2):
                    mm = nc.tensor.matmul(pb[s % 2][:, :], prob_t[:, s % 2, j * P:(j + 1) * P],
                                          xn_tm[:, s // 2 * 2 + j, :], start=(j == 0), stop=(j == 1))
                mm.then_inc(mixed, 1)

            def turn_zn(t):
                pe.wait_ge(zn_ready, t + 1)
                if 1 <= t < GROUP:
                    pe.wait_ge(zn_cm_ready, t)
                for k in range(KC):
                    mm = nc.tensor.transpose(zn_bank(t)[:, k * P:(k + 1) * P], zn(t)[:, k * P:(k + 1) * P], ident[:, :])
                mm.then_inc(zn_turned, 1)

            def route(t):
                pe.wait_ge(zn_cm_ready, t + 1)
                if t == 0:
                    pe.wait_ge(e_ready, 2 * BATCH)
                for k in range(KC):
                    mm = nc.tensor.matmul(pe_[:, t * EXPERTS:(t + 1) * EXPERTS], zn_cm[:, t % 2, k, :], router[:, k, :],
                                          start=(k == 0), stop=(k == KC - 1))
                mm.then_inc(routed, 1)

            for t in FIRST:
                turn_xn(t)
            pe.wait_ge(w_in, 9 * 16)
            reduce(0)
            score(0)
            for s in range(NT):
                if s + 1 < NT:
                    if (s + 1) % 2 == 0:
                        reduce((s + 1) // 2)
                    score(s + 1)
                assemble(s)
                if s == 7:
                    route(1)
                if s >= 6:
                    turn_zn(2 * (s - 6))
                turn_prob(s)
                if s == 0:
                    for t in REST:
                        turn_xn(t)
                else:
                    mix(s - 1)
                if s >= 6:
                    route(2 * (s - 6))
                    turn_zn(2 * (s - 6) + 1)
            mix(NT - 1)
            route(GROUP - 1)
            pe.wait_ge(w3_added, NT)
            turn_zn(GROUP)
            turn_zn(GROUP + 1)
            pe.wait_ge(x1_ready, NT)
            for t in REST:
                route(t)
                if t + 2 < NT:
                    turn_zn(t + 2)
            pe.wait_ge(mask_ready, 1)
            nc.tensor.matmul(ps[:, 0:P], upper[:, :], mask[:, :, :].rearrange("p t e -> p (t e)"), start=True, stop=True)
            nc.tensor.matmul(ps[:, P:2 * P], ones[:, :], mask[:, :, :].rearrange("p t e -> p (t e)"),
                             start=True, stop=True).then_inc(counted, 1)

        @block.vector
        def _(dve):
            steps = [0]

            def step(ins):
                steps[0] += 1
                ins.then_inc(dve_step, 1)

            def settle():
                dve.wait_ge(dve_step, steps[0])

            def link(ins):
                step(ins)
                settle()

            V = nc.vector

            def normalise(tiles):
                t0, t1 = tiles[0], tiles[-1] + 1
                for t in tiles:
                    dve.wait_ge(x_kept, t + 1)
                    step(V.bn_stats(stats[:, t, :], x_tm[:, t, :]))
                settle()
                for t in tiles:
                    step(V.bn_aggr(mv[:, t, :], stats[:, t, :]))
                settle()
                rsqrt(nc, link, rstd[:, t0:t1], mv[:, t0:t1, 1], 1.0, LN_C_EPS, scratch)
                for t in tiles:
                    V.tensor_scalar(xn_tm[:, t, :], x_tm[:, t, :], mv[:, t, 0:1], rstd[:, t:t + 1],
                                    ALU.subtract, ALU.mult).then_inc(xn_ready, 1)

            def row_max(s):
                dve.wait_ge(scored, s + 1)
                V.tensor_reduce(nmax[:, s:s + 1], ps[:, 0:SP], AX.X, ALU.max,
                                negate=True).then_inc(max_ready, 1)

            def add_assembly(s):
                dve.wait_ge(w3_summed, s + 1)
                if s:
                    dve.wait_ge(w3_added, s)
                link(V.tensor_tensor(part[:, :], pa[s % 2][:, :], b3[:, :], ALU.add))
                V.scalar_tensor_tensor(x_tm[:, s, :], part[:, :], 0.0, x_tm[:, s, :],
                                       ALU.max, ALU.add).then_inc(w3_added, 1)

            def add_attention(s):
                link(V.reciprocal(gain[:, s:s + 1], psum_row[:, s:s + 1]))
                link(V.tensor_tensor(gain[:, s:s + 1], gain[:, s:s + 1], alpha[:, :], ALU.mult))
                dve.wait_ge(mixed, s + 1)
                dve.wait_ge(w3_added, s + 1)
                V.scalar_tensor_tensor(x_tm[:, s, :], pb[s % 2][:, :], gain[:, s:s + 1], x_tm[:, s, :],
                                       ALU.mult, ALU.add).then_inc(x1_ready, 1)
                dve.wait_ge(x1_ready, s + 1)
                step(V.bn_stats(stats1[:, s, :], x_tm[:, s, :]))

            def make_tokens(tiles):
                t0, t1 = tiles[0], tiles[-1] + 1
                settle()
                for t in tiles:
                    step(V.bn_aggr(mv1[:, t, :], stats1[:, t, :]))
                settle()
                rsqrt(nc, link, rstd1[:, t0:t1], mv1[:, t0:t1, 1], BOTH_SCALE, BOTH_EPS, scratch)
                for i, t in enumerate(tiles):
                    step(V.tensor_scalar(zn(t), x_tm[:, t, :], mv1[:, t, 0:1], rstd1[:, t:t + 1],
                                         ALU.subtract, ALU.mult))
                    if i:
                        weigh(tiles[i - 1], steps[0] - 1)
                weigh(tiles[-1], steps[0])

            def weigh(t, made):
                dve.wait_ge(dve_step, made)
                V.tensor_tensor(zn(t), zn(t), lnw[:, :], ALU.mult).then_inc(zn_ready, 1)

            def cut_weights(i):
                V.tensor_scalar(weights[:, i, :], weights[:, i, :], ROUND + 1.0, ROUND - 1.0,
                                ALU.min, ALU.max).then_inc(cut, 1)

            normalise(FIRST)
            normalise(REST)
            dve.wait_ge(w_in, 9 * 16)
            dve.wait_ge(const_ready, 5)
            row_max(0)
            for s in range(NT):
                if s + 1 < NT:
                    row_max(s + 1)
                add_assembly(s)
                if s >= 1:
                    add_attention(s - 1)
                if s == ABS_TILES - 1:
                    dve.wait_ge(abs_ready, 3 * ABS_PARTS)
                    V.tensor_reduce(abs_sum[:, :], abs_part[:, :, :], AX.X, ALU.add).then_inc(abs_added, 1)
                if s == GROUP:
                    dve.wait_ge(abs_summed, 1)
                    link(V.tensor_scalar(inv_ws[:, :], abs_all[:, :], 1.0 / (C * W1), QEPS, ALU.mult, ALU.max))
                    V.reciprocal(w_scale[:, :], inv_ws[:, :]).then_inc(scale_ready, 1)
                    make_tokens(FIRST)
                if s == GROUP + 1:
                    dve.wait_ge(scale_ready, 1)
                    link(V.tensor_scalar(weights[:, 2, :], weights[:, 2, :], w_scale[:, 2:3], ROUND, ALU.mult, ALU.add))
                if s == GROUP + 2:
                    cut_weights(2)
            add_attention(NT - 1)
            make_tokens(REST)
            for i in range(2):
                dve.wait_ge(rounded, i + 1)
                cut_weights(i)
            dve.wait_ge(routed, NT)
            link(V.tensor_copy(logits[:, :, :], pe_[:, 0:NT * EXPERTS].rearrange("p (t e) -> p t e", e=EXPERTS)))
            for t in range(NT):
                step(V.max(top[:, t, :], logits[:, t, :]))
            settle()
            for t in range(NT):
                step(V.max_index(top_at[:, t, :], top[:, t, :], logits[:, t, :]))
            best = top[:, :, 0:1]
            V.tensor_tensor(elog[:, :, :], logits[:, :, :], best.to_broadcast([P, NT, EXPERTS]), ALU.subtract).then_inc(shifted_ready, 1)
            V.tensor_tensor(etop[:, :, :], top[:, :, 0:TOPK], best.to_broadcast([P, NT, TOPK]), ALU.subtract).then_inc(shifted_ready, 1)
            settle()
            link(V.tensor_copy(top_at_f[:, :, :], top_at[:, :, 0:TOPK]))
            for k in range(TOPK):
                step(V.tensor_tensor(onehot[:, k, :, :],
                                     top_at_f[:, :, k:k + 1].to_broadcast([P, NT, EXPERTS]),
                                     expert_ids[:, :].rearrange("p (o e) -> p o e", o=1).to_broadcast([P, NT, EXPERTS]),
                                     ALU.is_equal))
            settle()
            link(V.tensor_tensor(mask[:, :, :], onehot[:, 0, :, :], onehot[:, 1, :, :], ALU.add))
            link(V.tensor_tensor(mask[:, :, :], mask[:, :, :], onehot[:, 2, :, :], ALU.add))
            V.tensor_tensor(mask[:, :, :], mask[:, :, :], onehot[:, 3, :, :], ALU.add).then_inc(mask_ready, 1)
            step(V.memset(run[:, 0, :], 0.0))
            dve.wait_ge(elog_ready, 2)
            link(V.tensor_reduce(esum[:, :], elog[:, :, :], AX.X, ALU.add))
            link(V.reciprocal(resum[:, :], esum[:, :]))
            step(V.tensor_tensor(aff[:, :, :], etop[:, :, :],
                                 resum[:, :].rearrange("p (t o) -> p t o", o=1).to_broadcast([P, NT, TOPK]), ALU.mult))
            dve.wait_ge(counted, 1)
            link(V.tensor_copy(totals[:, :, :], ps[:, P:2 * P].rearrange("p (t e) -> p t e", e=EXPERTS)))
            for t in range(NT):
                link(V.tensor_tensor(run[:, t + 1, :], run[:, t, :], totals[:, t, :], ALU.add))
            link(V.tensor_tensor(before[:, :, :], ps[:, 0:P].rearrange("p (t e) -> p t e", e=EXPERTS),
                                 run[:, 0:NT, :], ALU.add))
            step(V.tensor_tensor(slot_e[:, :, :], before[:, :, :],
                                 base[:, :].rearrange("p (o e) -> p o e", o=1).to_broadcast([P, NT, EXPERTS]), ALU.add))
            for r in range(1, MAX_ROUNDS):
                step(V.tensor_scalar(wraps[:, r, :, :], before[:, :, :], float(r * CAP), float(ROUND_SLOTS - CAP),
                                     ALU.is_ge, ALU.mult))
            settle()
            for r in range(1, MAX_ROUNDS):
                link(V.tensor_tensor(slot_e[:, :, :], slot_e[:, :, :], wraps[:, r, :, :], ALU.add))
            for k in range(TOPK):
                step(V.tensor_tensor(picked[:, k, :, :], onehot[:, k, :, :], slot_e[:, :, :], ALU.mult))
            settle()
            for k in range(TOPK):
                step(V.tensor_reduce(slot_f[:, :, k:k + 1], picked[:, k, :, :], AX.X, ALU.add))
            step(V.tensor_reduce(most[:, :], run[:, NT, :], AX.X, ALU.max))
            for i, width in enumerate(NARROW):
                for r in range(MAX_ROUNDS):
                    step(V.tensor_scalar(room[:, i, r, :], run[:, NT, :], float(r * CAP + width), None, ALU.is_le))
            step(V.memset(most2[:, 0:1], 1.0))
            settle()
            V.tensor_copy(slots[:, :, :], slot_f[:, :, :])
            V.tensor_tensor(narrow[:, :], room[:, 0, :, :].rearrange("p r e -> p (r e)"),
                            room[:, 1, :, :].rearrange("p r e -> p (r e)"), ALU.add)
            for r in range(1, MAX_ROUNDS):
                step(V.tensor_scalar(most2[:, r:r + 1], most[:, :], float(r * CAP), None, ALU.is_gt))
            settle()
            link(V.tensor_reduce(most[:, :], most2[:, :], AX.X, ALU.add))
            V.tensor_copy(rounds[:, :], most[:, :])


def tiles_of(n):
    return [min(P, n - j * P) for j in range(-(-n // P))]


def experts(nc, io, keep):
    ctx = ExitStack()
    with ctx:
        def sb(name, shape, dt=FP32):
            return ctx.enter_context(nc.sbuf_tensor(name, shape, dt))

        def bank(name):
            return ctx.enter_context(nc.psum_tensor(name, [P, 512], FP32))

        def sem(name):
            return ctx.enter_context(nc.semaphore(name))

        x_tm, ident, rounds, narrow = keep["x_tm"], keep["ident"], keep["rounds"], keep["narrow"]
        aff, slots, token_ids = keep["aff"], keep["slots"], keep["token_ids"]
        raw_last = sb("raw_last", [P, PIECE])
        raw = [keep["raw"][:, 0, :], keep["raw"][:, 1, :], raw_last[:, :]]
        w_hi = sb("w_hi", [P, RING, PIECE], F32R)
        w_lo = sb("w_lo", [P, RING, PIECE], F32R)
        rows = keep["rows"]
        slot_ids = sb("slot_ids", [P, 4], U32)
        x_hi = sb("x_hi", [P, KC, HALF], F32R)
        x_lo = sb("x_lo", [P, KC, HALF], F32R)
        gated = sb("gated", [P, 2, HALF])
        hid = sb("hid", [P, 2, HALF])
        h_hi = sb("h_hi", [P, FH, HALF], F32R)
        h_lo = sb("h_lo", [P, FH, HALF], F32R)
        y_sb = sb("y_sb", [P, 3, C])
        got = sb("got", [P, BACK_RING, C])
        conv, bias = got[:, 0:KC, :], got[0:1, KC, :]
        conv_hi, conv_lo = keep["conv_hi"], keep["conv_lo"]
        bias_hi, bias_lo = keep["bias_hi"], keep["bias_lo"]
        mv, rstd = keep["scan_mv"], keep["scan_rstd"]
        st = sb("st", [P, NT, 6])
        scratch = sb("scratch2", [P, 2 * NT])

        gate_ps = [bank("gate_ps0"), bank("gate_ps1")]
        up_ps = [bank("up_ps0"), bank("up_ps1")]
        y_ps = [bank(f"y_ps{j}") for j in range(4)]
        turn_ps = [gate_ps[0], up_ps[0], gate_ps[1], up_ps[1]]

        raw_in = [sem(f"raw_in{j}") for j in range(RING)]
        hi_ready = sem("hi_ready")
        split_ready = sem("split_ready")
        half_summed = sem("half_summed")
        shared_in = sem("shared_in")
        listed = sem("listed")
        ids_in = sem("ids_in")
        rows_in = sem("rows_in")
        rows_turned = sem("rows_turned")
        x_hi_ready = sem("x_hi_ready")
        x_lo_ready = sem("x_lo_ready")
        gu_summed = sem("gu_summed")
        silu_ready = sem("silu_ready")
        hid_ready = sem("hid_ready")
        h_hi_ready = sem("h_hi_ready")
        h_ready = sem("h_ready")
        y_summed = sem("y_summed")
        y_taken = sem("y_taken")
        y_out = sem("y_out")
        y_free = sem("y_free")
        got_in = [sem(f"got_in{j}") for j in range(BACK_RING)]
        added = sem("added")
        conv_in = sem("conv_in")
        conv_hi_ready = sem("conv_hi_ready")
        dve_step = sem("dve_step2")

        block = ctx.enter_context(nc.Block())
        ROUTED = tiles_of(CAP)
        SHARED = tiles_of(HALF)
        FIRST_HALVES = [(j, part) for j in range(2) for part in range(2)]

        def down_view(piece):
            return piece.rearrange("p (k c) -> p k c", k=DOWN_K)

        def rounds_of(eng):
            return eng.value_load(rounds[0:1, 0:1], min_val=1, max_val=MAX_ROUNDS)

        @block.sync
        def _(sp):
            def load(U, j, sources):
                slot = j % RING
                sp.wait_ge(split_ready, U * (2 * PIECES) + (2 * j + 2))
                for dst, src in sources:
                    sp.dma_start(dst, src).then_inc(raw_in[slot], 16)

            def pieces(U, gate, up, down, first, last):
                for j in range(first, last):
                    if j < 4:
                        load(U, j, gate_up_piece(raw[j % RING], j, gate, up))
                    else:
                        v = down_view(raw[j % RING])
                        k = (j - 4) * DOWN_K
                        load(U, j, [(v[:, 0:2, :], down[:, k:k + 2, :]), (v[:, 2:4, :], down[:, k + 2:k + 4, :])])

            shared = shared_sources(io)
            for j in range(2):
                sp.sem_inc(raw_in[j], 32)
            pieces(0, *shared, 2, PIECES)
            sp.dma_start(conv, io["conv_w"].rearrange("(k p) m -> p k m", p=P)).then_inc(conv_in, 16)
            sp.dma_start(bias, io["conv_b"].rearrange("(a b) -> a b", a=1)).then_inc(conv_in, 16)
            n = rounds_of(sp)
            with sp.Fori(0, n) as r:
                with sp.Fori(0, EXPERTS) as e:
                    gu = io["gate_up"][bass.ds(e, 1), :, :].rearrange("o (k p) f -> p (o k) f", p=P)
                    dn = io["down"][bass.ds(e, 1), :, :].rearrange("o (k p) c -> p (o k) c", p=P)
                    pieces(r * EXPERTS + e + 1, gu[:, :, 0:FF], gu[:, :, FF:2 * FF], dn, 0, PIECES)
            last = n * EXPERTS + 1
            pieces(last, *shared, 0, RING)
            sp.wait_ge(rows_turned, (last + 1) * KC)
            sp.dma_start(rows[:, :, :], io["tokens"][HALF:TOK, :].rearrange("(j p) c -> p j c", p=P)).then_inc(shared_in, 16)
            pieces(last, *shared, RING, PIECES)

        @block.gpsimd
        def _(pool):
            def gather(u):
                pool.wait_ge(rows_turned, (u + 1) * KC)
                base = u * CAP
                ids = io["slot_token"]
                pool.dma_start(slot_ids[:, 0:2], ids[bass.ds(base, 2 * P), :]
                               .rearrange("(p j) o -> p (j o)", p=P)).then_inc(ids_in, 16)
                pool.dma_start(slot_ids[0:CAP - 2 * P, 2:3], ids[bass.ds(base + 2 * P, CAP - 2 * P), :]).then_inc(ids_in, 16)
                pool.wait_ge(ids_in, u * 32 + 32)
                pool.nop(nofuse=True)
                for j, w in enumerate(ROUTED):
                    pool.indirect_dma_start(
                        out=rows[0:w, j, :], out_offset=None, in_=io["tokens"],
                        in_offset=bass.IndirectOffsetOnAxis(ap=slot_ids[0:w, j:j + 1], axis=0)).then_inc(rows_in, 16)

            def store(u):
                pool.wait_ge(y_taken, u + 2)
                base = u * CAP
                pool.dma_start(io["slot_y"][bass.ds(base, 2 * P), :].rearrange("(p j) c -> p j c", p=P),
                               y_sb[:, 0:2, :]).then_inc(y_out, 16)
                pool.dma_start(io["slot_y"][bass.ds(base + 2 * P, CAP - 2 * P), :],
                               y_sb[0:CAP - 2 * P, 2, :]).then_inc(y_out, 16)
                pool.wait_ge(y_out, u * 32 + 32)
                pool.sem_inc(y_free, 1)

            def bring_back(source):
                for i in range(NT * TOPK):
                    k, t = divmod(i, NT)
                    if i >= BACK_RING:
                        pool.wait_ge(added, i - BACK_RING + 1)
                    pool.indirect_dma_start(
                        out=got[:, i % BACK_RING, :], out_offset=None, in_=source,
                        in_offset=bass.IndirectOffsetOnAxis(ap=slots[:, t, k:k + 1], axis=0)).then_inc(got_in[i % BACK_RING], 16)

            for t in range(NT):
                for k in range(TOPK):
                    pool.indirect_dma_start(
                        out=io["slot_token"], out_offset=bass.IndirectOffsetOnAxis(ap=slots[:, t, k:k + 1], axis=0),
                        in_=token_ids[:, t:t + 1], in_offset=None).then_inc(listed, 16)
            pool.sem_inc(y_free, 1)
            pool.wait_ge(listed, 16 * NT * TOPK)
            gather(0)
            n = rounds_of(pool)
            with pool.Fori(0, n * EXPERTS) as u:
                gather(u + 1)
                store(u)
            pool.wait_ge(rows_in, n * (EXPERTS * 48) + 48)
            pool.nop(nofuse=True)
            with pool.If(n < 2):
                bring_back(io["slot_y"][0:ROUND_SLOTS, :])
            with pool.Else():
                bring_back(io["slot_y"])

        @block.scalar
        def _(act):
            S = nc.scalar

            def hi(U, j, part):
                act.wait_ge(raw_in[j % RING], (U * (PIECES // RING) + j // RING) * 32 + 32)
                if j == 0:
                    act.wait_ge(gu_summed, U * FH)
                elif j == 1:
                    act.wait_ge(half_summed, U)
                elif j == 2:
                    act.wait_ge(y_summed, U)
                else:
                    act.wait_ge(gu_summed, U * FH + 2 * (j - 2))
                c = slice(part * PIECE // 2, (part + 1) * PIECE // 2)
                S.copy(w_hi[:, j % RING, c], raw[j % RING][:, c]).then_inc(hi_ready, 1)

            def hidden(U, m, n):
                act.wait_ge(gu_summed, U * FH + m + 1)
                S.activation(gated[:, m % 2, 0:n], gate_ps[m % 2][:, 0:n], ACT.Silu).then_inc(silu_ready, 1)
                act.wait_ge(hid_ready, U * FH + m + 1 + 2)
                S.copy(h_hi[:, m, 0:n], hid[:, m % 2, 0:n]).then_inc(h_hi_ready, 1)

            def turn(i, n):
                for k in range(KC):
                    act.wait_ge(rows_turned, i * KC + k + 1)
                    S.copy(x_hi[:, k, 0:n], turn_ps[k][:, 0:n]).then_inc(x_hi_ready, 1)

            def take(u):
                act.wait_ge(y_summed, u + 2)
                act.wait_ge(y_free, u + 1)
                for j, w in enumerate(ROUTED):
                    ins = S.copy(y_sb[0:w, j, :], y_ps[j][0:w, :])
                ins.then_inc(y_taken, 1)

            def unit(U, n):
                for j in range(4):
                    for part in range(2):
                        hidden(U, 2 * j + part, n)
                        hi(U, j + 2, part)

            for j, part in FIRST_HALVES:
                if (j, part) == (1, 0):
                    turn(0, HALF)
                hi(0, j, part)
            unit(0, HALF)
            act.wait_ge(conv_in, 32)
            S.copy(conv_hi[:, :, :], conv).then_inc(conv_hi_ready, 1)
            S.copy(bias_hi[:, :], bias).then_inc(conv_hi_ready, 1)
            turn(1, CAP)
            for j, part in FIRST_HALVES:
                hi(1, j, part)
            n = rounds_of(act)
            with act.Fori(0, n * EXPERTS) as u:
                unit(u + 1, CAP)
                turn(u + 2, CAP)
                for j, part in FIRST_HALVES:
                    hi(u + 2, j, part)
                take(u)
            last = n * EXPERTS + 1
            turn(last + 1, HALF)
            unit(last, HALF)

        @block.vector
        def _(dve):
            V = nc.vector
            done = [0]

            def step(ins):
                done[0] += 1
                ins.then_inc(dve_step, 1)

            def link(ins):
                done[0] += 1
                ins.then_inc(dve_step, 1)
                dve.wait_ge(dve_step, done[0])

            def lo(U, j, part):
                dve.wait_ge(hi_ready, U * (2 * PIECES) + (2 * j + part + 1))
                c = slice(part * PIECE // 2, (part + 1) * PIECE // 2)
                V.tensor_tensor(w_lo[:, j % RING, c], raw[j % RING][:, c], w_hi[:, j % RING, c].bitcast(FP32),
                                ALU.subtract).then_inc(split_ready, 1)

            def hidden(U, m, n):
                dve.wait_ge(silu_ready, U * FH + m + 1)
                V.tensor_tensor(hid[:, m % 2, 0:n], gated[:, m % 2, 0:n], up_ps[m % 2][:, 0:n],
                                ALU.mult).then_inc(hid_ready, 1)
                dve.wait_ge(h_hi_ready, U * FH + m + 1)
                V.tensor_tensor(h_lo[:, m, 0:n], hid[:, m % 2, 0:n], h_hi[:, m, 0:n].bitcast(FP32),
                                ALU.subtract).then_inc(h_ready, 1)

            def turn(i, n):
                for k in range(KC):
                    dve.wait_ge(x_hi_ready, i * KC + k + 1)
                    V.tensor_tensor(x_lo[:, k, 0:n], turn_ps[k][:, 0:n], x_hi[:, k, 0:n].bitcast(FP32),
                                    ALU.subtract).then_inc(x_lo_ready, 1)

            def add_shared():
                dve.wait_ge(y_summed, 1)
                for t in range(len(SHARED)):
                    last = V.tensor_tensor(x_tm[:, t, :], x_tm[:, t, :], y_ps[t][:, :], ALU.add)
                last.then_inc(y_taken, 1)

            def unit(U, n, beside):
                for j in range(4):
                    for part in range(2):
                        hidden(U, 2 * j + part, n)
                        beside(2 * j + part)
                        lo(U, j + 2, part)

            def add_back(i):
                k, t = divmod(i, NT)
                dve.wait_ge(got_in[i % BACK_RING], 16 * (i // BACK_RING + 1))
                if k:
                    dve.wait_ge(added, i - NT + 1)
                V.scalar_tensor_tensor(x_tm[:, t, :], got[:, i % BACK_RING, :], aff[:, t, k:k + 1], x_tm[:, t, :],
                                       ALU.mult, ALU.add).then_inc(added, 1)

            def beside_last(m):
                for i in range(3 * (m - 1), 3 * m):
                    if i >= 0:
                        add_back(i)

            dve.sem_inc(split_ready, 2 * RING)
            dve.sem_inc(hid_ready, 2)
            for j, part in FIRST_HALVES:
                if (j, part) == (1, 0):
                    turn(0, HALF)
                lo(0, j, part)
            unit(0, HALF, lambda m: None)
            dve.wait_ge(conv_hi_ready, 2)
            link(V.tensor_tensor(conv, conv, conv_hi[:, :, :], ALU.subtract))
            link(V.tensor_tensor(bias, bias, bias_hi[:, :], ALU.subtract))
            V.tensor_scalar(conv_lo[:, :, :], conv, LOW_SCALE, None, ALU.mult)
            V.tensor_scalar(bias_lo[:, :], bias, LOW_SCALE, None, ALU.mult)
            turn(1, CAP)
            for j, part in FIRST_HALVES:
                lo(1, j, part)
            add_shared()
            n = rounds_of(dve)
            with dve.Fori(0, n * EXPERTS) as u:
                unit(u + 1, CAP, lambda m: None)
                turn(u + 2, CAP)
                for j, part in FIRST_HALVES:
                    lo(u + 2, j, part)
            last = n * EXPERTS + 1
            turn(last + 1, HALF)
            unit(last, HALF, beside_last)
            for i in range(3 * (FH - 1), NT * TOPK):
                add_back(i)
            dve.wait_ge(added, NT * TOPK)
            for t in range(len(SHARED)):
                step(V.bn_stats(st[:, t, :], x_tm[:, t, :]))
            for j in range(len(SHARED)):
                t = len(SHARED) + j
                dve.wait_ge(y_summed, last + (j + 1))
                link(V.tensor_tensor(x_tm[:, t, :], x_tm[:, t, :], y_ps[j][:, :], ALU.add))
                step(V.bn_stats(st[:, t, :], x_tm[:, t, :]))
            dve.wait_ge(dve_step, done[0])
            for t in range(NT):
                step(V.bn_aggr(mv[:, t, :], st[:, t, :]))
            dve.wait_ge(dve_step, done[0])
            rsqrt(nc, link, rstd[:, :], mv[:, :, 1], 1.0, LN_C_EPS, scratch)

        @block.tensor
        def _(pe):
            T = nc.tensor

            def turn(tiles):
                for k in range(KC):
                    for j, w in enumerate(tiles):
                        mm = T.transpose(turn_ps[k][:, j * P:j * P + w], rows[0:w, j, k * P:(k + 1) * P], ident[0:w, 0:w])
                    mm.then_inc(rows_turned, 1)

            def three(out, hi_a, lo_a, hi_b, lo_b, first, last):
                T.matmul(out, hi_a, hi_b, start=first, stop=False)
                T.matmul(out, hi_a, lo_b, start=False, stop=False)
                return T.matmul(out, lo_a, hi_b, start=False, stop=last)

            def unit(U, tiles, next_rows):
                n = sum(tiles)
                for j in range(4):
                    pe.wait_ge(split_ready, U * (2 * PIECES) + 2 * (j + 1 + RING))
                    hi_w, lo_w = gu_view(w_hi[:, j % RING, :]), gu_view(w_lo[:, j % RING, :])
                    for i in range(2):
                        m = 2 * j + i
                        pe.wait_ge(hid_ready, U * FH + m + 1)
                        for g, ps in enumerate((gate_ps[i], up_ps[i])):
                            for k in range(KC):
                                c = slice(i * P, (i + 1) * P)
                                mm = three(ps[:, 0:n], hi_w[:, k, g, c], lo_w[:, k, g, c], x_hi[:, k, 0:n], x_lo[:, k, 0:n],
                                           k == 0, k == KC - 1)
                        mm.then_inc(gu_summed, 1)
                for d in range(2):
                    j = 4 + d
                    pe.wait_ge(split_ready, U * (2 * PIECES) + 2 * (j + 1 + RING))
                    if d == 0 and not (isinstance(U, int) and U == 0):
                        pe.wait_ge(y_taken, U)
                    hi_w, lo_w = down_view(w_hi[:, j % RING, :]), down_view(w_lo[:, j % RING, :])
                    steps = [(k, i) for k in range(DOWN_K) for i in range(len(tiles))]
                    if d == 1 and not next_rows:
                        steps = [(k, i) for i in range(len(tiles)) for k in range(DOWN_K)]
                        pe.wait_ge(h_ready, U * FH + FH)
                    for k, i in steps:
                        m, w = d * DOWN_K + k, tiles[i]
                        c = slice(i * P, i * P + w)
                        if i == 0 and (d == 0 or next_rows):
                            pe.wait_ge(h_ready, U * FH + m + 1)
                        mm = three(y_ps[i][0:w, :], h_hi[:, m, c], h_lo[:, m, c], hi_w[:, k, :], lo_w[:, k, :],
                                   m == 0, m == FH - 1)
                        if k == DOWN_K - 1 and d == 1 and not next_rows:
                            mm.then_inc(y_summed, 1)
                    if d == 0:
                        mm.then_inc(half_summed, 1)
                        pe.wait_ge(h_ready, U * FH + FH)
                        if next_rows:
                            pe.wait_ge(*next_rows)
                            turn(ROUTED)
                    elif next_rows:
                        mm.then_inc(y_summed, 1)

            turn(SHARED)
            pe.wait_ge(x_lo_ready, KC)
            unit(0, SHARED, (rows_in, 16 * len(ROUTED)))
            n = rounds_of(pe)
            with pe.Fori(0, n * EXPERTS) as u:
                pe.wait_ge(x_lo_ready, (u + 2) * KC)
                few = pe.value_load(narrow[0:1, bass.ds(u, 1)], min_val=0, max_val=2)
                next_rows = (rows_in, (u + 2) * (16 * len(ROUTED)))
                with pe.If(few > 1):
                    unit(u + 1, tiles_of(NARROW[1]), next_rows)
                with pe.Else():
                    with pe.If(few > 0):
                        unit(u + 1, tiles_of(NARROW[0]), next_rows)
                    with pe.Else():
                        unit(u + 1, ROUTED, next_rows)
            last = n * EXPERTS + 1
            pe.wait_ge(x_lo_ready, (last + 1) * KC)
            pe.wait_ge(shared_in, 16)
            turn(SHARED)
            pe.wait_ge(x_lo_ready, (last + 2) * KC)
            unit(last, SHARED, None)


SIDE = BATCH * IMW


def scan(nc, io, keep):
    ctx = ExitStack()
    with ctx:
        def sb(name, shape, dt=FP32):
            return ctx.enter_context(nc.sbuf_tensor(name, shape, dt))

        def bank(name):
            return ctx.enter_context(nc.psum_tensor(name, [P, 512], FP32))

        def sem(name):
            return ctx.enter_context(nc.semaphore(name))

        x_tm, ident, state = keep["x_tm"], keep["ident"], keep["state"]
        conv_hi, conv_lo = keep["conv_hi"], keep["conv_lo"]
        bias_hi, bias_lo = keep["bias_hi"], keep["bias_lo"]
        mv, rstd = keep["scan_mv"], keep["scan_rstd"]
        ones_row = sb("ones_row", [1, SIDE], F16)
        low_row = sb("low_row", [1, SIDE], F16)
        row_hi = sb("row_hi", [P, KC, SIDE], F16)
        row_hi_low = sb("row_hi_low", [P, KC, SIDE], F16)
        row_lo = sb("row_lo", [P, KC, SIDE], F16)
        xc = sb("xc", [P, NT, C])

        step_ps = [[bank(f"step_ps{a}{b}") for b in range(2)] for a in range(2)]
        turn_ps = [bank(f"turn2_ps{a}") for a in range(4)]

        ones_ready = sem("ones_ready")
        xc_ready = sem("xc_ready")
        xc_turned = sem("xc_turned")
        state_ready = sem("state_ready")
        stepped = sem("stepped")
        hi_made = sem("hi_made")
        hi_low_made = sem("hi_low_made")
        lo_made = sem("lo_made")
        added = sem("row_added")
        block = ctx.enter_context(nc.Block())

        def steps(eng, one):
            with eng.Fori(0, (IMH - 2) // 2) as i:
                one(2 * i, 2 * i + 1, 0)
                one(2 * i + 1, 2 * i + 2, 1)
            one(IMH - 2, IMH - 1, 0)
            one(IMH - 1, IMH - 2, 1)
            with eng.Fori(0, (IMH - 2) // 2) as i:
                one(2 * i + IMH, IMH - 3 - 2 * i, 0)
                one(2 * i + IMH + 1, IMH - 4 - 2 * i, 1)

        @block.gpsimd
        def _(pool):
            pool.memset(ones_row[:, :], 1.0).then_inc(ones_ready, 1)
            pool.memset(low_row[:, :], 1.0 / LOW_SCALE).then_inc(ones_ready, 1)

        @block.scalar
        def _(act):
            S = nc.scalar
            for t in range(NT):
                n, h = t // 2, (t % 2) * IMH // 2
                act.wait_ge(xc_turned, t + 1)
                S.copy(state[:, h:h + IMH // 2, :, n, :].rearrange("p h k w -> p k h w"),
                       turn_ps[t % 4][:, :].rearrange("p (k h w) -> p k h w", k=KC, w=IMW)).then_inc(state_ready, 1)

            def low(s):
                for g in range(2):
                    k = slice(2 * g, 2 * g + 2)
                    act.wait_ge(hi_made, 2 * s + g + 3)
                    act.nop(nofuse=True)
                    S.mul(row_hi_low[:, k, :], row_hi[:, k, :], 1.0 / LOW_SCALE).then_inc(hi_low_made, 1)

            low(-1)
            steps(act, lambda s, new, parity: low(s))

        @block.tensor
        def _(pe):
            T = nc.tensor
            for t in range(NT):
                pe.wait_ge(xc_ready, t + 1)
                if t >= 4:
                    pe.wait_ge(state_ready, t - 3)
                for k in range(KC):
                    mm = T.transpose(turn_ps[t % 4][:, k * P:(k + 1) * P], xc[:, t, k * P:(k + 1) * P], ident[:, :])
                mm.then_inc(xc_turned, 1)
            pe.wait_ge(ones_ready, 2)

            def one(s, new, parity):
                def out(m):
                    return step_ps[parity][m // 2][:, (m % 2) * SIDE:(m % 2 + 1) * SIDE]

                def products(weights, row, k, m, **flags):
                    return T.matmul(out(m), weights[:, k, m * P:(m + 1) * P], row[:, k, :], skip_group_check=True,
                                    start=False, **flags)

                pe.wait_ge(added, 2 * s + 1)
                for m in range(KC):
                    T.matmul(out(m), bias_hi[:, m * P:(m + 1) * P], ones_row[:, :], start=(m % 2 == 0), stop=False,
                             skip_group_check=True)
                    T.matmul(out(m), bias_lo[:, m * P:(m + 1) * P], low_row[:, :], start=False, stop=False,
                             skip_group_check=True)
                for g in range(2):
                    pe.wait_ge(hi_made, 2 * s + g + 1)
                    for k in (2 * g, 2 * g + 1):
                        for m in range(KC):
                            products(conv_hi, row_hi, k, m, stop=False)
                for g in range(2):
                    pe.wait_ge(hi_low_made, 2 * s + g + 1)
                    for k in (2 * g, 2 * g + 1):
                        for m in range(KC):
                            products(conv_lo, row_hi_low, k, m, stop=False)
                pe.wait_ge(lo_made, 2 * s + 1)
                for k in (0, 1):
                    for m in range(KC):
                        products(conv_hi, row_lo, k, m, stop=False)
                pe.wait_ge(lo_made, 2 * s + 2)
                for g in range(2):
                    for m in (2 * g, 2 * g + 1):
                        for k in (2, 3):
                            mm = products(conv_hi, row_lo, k, m, stop=(k == 3))
                    mm.then_inc(stepped, 1)

            steps(pe, one)

        @block.vector
        def _(dve):
            V = nc.vector
            dve.sem_inc(added, 3)
            def centre(t):
                V.tensor_scalar(xc[:, t, :], x_tm[:, t, :], mv[:, t, 0:1], rstd[:, t:t + 1],
                                ALU.subtract, ALU.mult).then_inc(xc_ready, 1)

            for t in range(NT):
                centre(t)
            dve.wait_ge(state_ready, NT)

            def chunks(new, g):
                k = slice(2 * g, 2 * g + 2)
                row = state[:, new, k, :, :].rearrange("p k n w -> p k (n w)") if isinstance(new, int) else \
                    state[:, bass.ds(new, 1), k, :, :].rearrange("p o k n w -> p (o k) (n w)")
                return k, row

            for g in range(2):
                k, row = chunks(0, g)
                V.tensor_copy(row_hi[:, k, :], row).then_inc(hi_made, 1)
                dve.wait_ge(hi_made, g + 1)
                V.tensor_tensor(row_lo[:, k, :], row, row_hi[:, k, :], ALU.subtract).then_inc(lo_made, 1)

            def one(s, new, parity):
                def add(g, out):
                    k, row = chunks(new, g)
                    return V.scalar_tensor_tensor(out if out is not None else row,
                                                  step_ps[parity][g][:, 0:2 * SIDE].rearrange("p (k c) -> p k c", k=2),
                                                  0.0, row, ALU.max, ALU.add)

                for g in range(2):
                    k, row = chunks(new, g)
                    dve.wait_ge(stepped, 2 * s + g + 1)
                    dve.wait_ge(hi_low_made, 2 * s + g + 1)
                    dve.nop(nofuse=True)
                    add(g, row_hi[:, k, :]).then_inc(hi_made, 1)
                for g in range(2):
                    k, row = chunks(new, g)
                    dve.wait_ge(hi_made, 2 * s + 4)
                    dve.nop(nofuse=True)
                    add(g, None).then_inc(added, 1)
                for g in range(2):
                    k, row = chunks(new, g)
                    dve.wait_ge(added, 2 * s + g + 4)
                    dve.nop(nofuse=True)
                    V.tensor_tensor(row_lo[:, k, :], row, row_hi[:, k, :], ALU.subtract).then_inc(lo_made, 1)

            steps(dve, one)


def ternary_ffn(nc, io, keep):
    ctx = ExitStack()
    with ctx:
        def sb(name, shape, dt=FP32):
            return ctx.enter_context(nc.sbuf_tensor(name, shape, dt))

        def bank(name):
            return ctx.enter_context(nc.psum_tensor(name, [P, 512], FP32))

        def sem(name):
            return ctx.enter_context(nc.semaphore(name))

        x_tm, ident, state = keep["x_tm"], keep["ident"], keep["state"]
        ternary, inv_ws = keep["ternary"], keep["inv_ws"]
        ident_b = sb("ident_b", [P, P], BF16)
        st = sb("st3", [P, NT, 6])
        mv = sb("mv3", [P, NT, 2])
        stat = sb("stat", [P, 16, NT])
        scratch = sb("scratch3", [P, 2 * NT])
        z = sb("z3", [P, NT, C])
        q = sb("q", [P, NT, C], BF16)
        q_cm = sb("q_cm", [P, NT, KC, P], BF16)
        silu = sb("silu", [P, 2, 512])
        h = sb("h", [P, 4, W1])
        hsq = sb("hsq", [P, W1])
        hq = sb("hq", [P, 4, W1], BF16)
        h_cm = sb("h_cm", [P, 2, W3, P], BF16)
        stack = sb("stack", [P, NT, KC, P])
        out_cm = sb("out_cm", [P, KC, TOK])

        gu_ps = [bank("g0"), bank("u0"), bank("g1"), bank("u1")]
        ht_ps = [bank("ht0"), bank("ht1")]
        x_ps = bank("x_ps")
        y_ps = bank("y3_ps")

        ident_ready = sem("ident_ready")
        stack_ready = sem("stack_ready")
        stack_turned = sem("stack_turned")
        x3_ready = sem("x3_ready")
        rstd_ready = sem("rstd_ready")
        z_ready = [sem("z_even_ready"), sem("z_odd_ready")]
        q_scale_ready = sem("q_scale_ready")
        zr_ready = [sem("zr_act_ready"), sem("zr_pool_ready")]
        q_ready = sem("q_ready")
        q_turned = sem("q_turned")
        q_cm_ready = sem("q_cm_ready")
        gu_summed = sem("gu3_summed")
        silu_ready = sem("silu3_ready")
        h_ready = sem("h3_ready")
        hsq_ready = sem("hsq_ready")
        hscale_ready = sem("hscale_ready")
        hr_ready = sem("hr_ready")
        hq_ready = sem("hq_ready")
        h_turned = sem("h_turned")
        h_cm_ready = sem("h_cm_ready")
        y_summed = sem("y3_summed")
        x4_ready = sem("x4_ready")
        x4_turned = sem("x4_turned")
        out_ready = sem("out_ready")
        out_sent = sem("out_sent")
        dve_step = sem("dve_step3")
        block = ctx.enter_context(nc.Block())

        PARTS = [(0, 512), (512, 512), (1024, 384)]
        w1 = ternary[:, 0, :].rearrange("p (k m) -> p k m", m=W1)
        w2 = ternary[:, 1, :].rearrange("p (k m) -> p k m", m=W1)
        w3 = ternary[:, 2, :].rearrange("p (k m) -> p k m", m=C)
        RSTD, SHIFT, ZMAX, Q, INV_Q, G_SCALE, U_SCALE, HSS, HRMS, HMAX, HA, HQ, Y_SCALE = range(13)
        HALF_TILES = NT // 2
        ACT_ZR, POOL_ZR = [0, 2], [1, 3, 4, 5, 6, 7]

        QUANT_AFTER = {0: (4, 5), 1: (6, 7)}
        TURN_AFTER = {0: (2, 3), 1: (4, 5), 2: (6, 7)}

        def col(i, t):
            return stat[:, i, t:t + 1]

        def cols(i, t0, t1):
            return stat[:, i, t0:t1]

        def half(ps, n=512):
            return ps[:, :].bitcast(BF16)[:, 0:n]

        def scale_and_round(eng, engine, t, done):
            eng.wait_ge(q_scale_ready, t // HALF_TILES + 1)
            engine.tensor_scalar(z[:, t, :], z[:, t, :], col(Q, t), ROUND, ALU.mult, ALU.add).then_inc(done, 1)

        @block.sync
        def _(sp):
            for n in range(BATCH):
                sp.wait_ge(out_ready, 2 * n + 2)
                sp.dma_start(io["out"][n].rearrange("(k p) h w -> p k (h w)", p=P),
                             out_cm[:, :, n * SP:(n + 1) * SP]).then_inc(out_sent, 16)
            sp.wait_ge(out_sent, 16 * BATCH)

        @block.gpsimd
        def _(pool):
            pool.wait_ge(rstd_ready, 1)
            for t in range(1, NT, 2):
                nc.gpsimd.tensor_scalar(z[:, t, :], x_tm[:, t, :], col(RSTD, t), col(SHIFT, t),
                                        ALU.mult, ALU.add).then_inc(z_ready[1], 1)
            for t in POOL_ZR:
                scale_and_round(pool, nc.gpsimd, t, zr_ready[1])

        @block.scalar
        def _(act):
            S = nc.scalar
            for t in range(NT):
                n, row = t // 2, (t % 2) * IMH // 2
                S.copy(stack[:, t, :, :].rearrange("p k (h w) -> p k h w", w=IMW),
                       state[:, row:row + IMH // 2, :, n, :].rearrange("p h k w -> p k h w")).then_inc(stack_ready, 1)
            S.copy(ident_b[:, :], ident[:, :]).then_inc(ident_ready, 1)
            act.wait_ge(rstd_ready, 1)
            for t in range(0, NT, 2):
                S.activation(z[:, t, :], x_tm[:, t, :], ACT.Identity, bias=col(SHIFT, t),
                             scale=col(RSTD, t)).then_inc(z_ready[0], 1)
            act.wait_ge(q_scale_ready, 1)
            for t in ACT_ZR:
                S.activation(z[:, t, :], z[:, t, :], ACT.Copy, bias=ROUND, scale=col(Q, t)).then_inc(zr_ready[0], 1)

            def q_copy(t):
                act.wait_ge(q_turned, t + 1)
                S.copy(q_cm[:, t, :, :], half(ht_ps[t % 2]).rearrange("p (k m) -> p k m", k=KC)).then_inc(q_cm_ready, 1)

            def square(t):
                act.wait_ge(h_ready, 3 * t + 3)
                if t:
                    act.wait_ge(hsq_ready, t)
                S.activation(hsq[:, :], h[:, t % 4, :], ACT.Square, accum_out=col(HSS, t)).then_inc(hsq_ready, 1)

            def h_round(t):
                act.wait_ge(hscale_ready, t // 2 + 1)
                S.activation(h[:, t % 4, :], h[:, t % 4, :], ACT.Copy, bias=ROUND, scale=col(HQ, t)).then_inc(hr_ready, 1)

            def h_copy(t):
                act.wait_ge(h_turned, t + 1)
                if t >= 2:
                    act.wait_ge(y_summed, t - 1)
                S.copy(h_cm[:, t % 2, 0:8, :], half(ht_ps[0], 1024).rearrange("p (k m) -> p k m", k=8)).then_inc(h_cm_ready, 1)
                S.copy(h_cm[:, t % 2, 8:W3, :], half(ht_ps[1], 384).rearrange("p (k m) -> p k m", k=3)).then_inc(h_cm_ready, 1)

            def out_copy(t):
                act.wait_ge(x4_turned, t + 1)
                S.copy(out_cm[:, :, t * P:(t + 1) * P], x_ps[:, :].rearrange("p (k m) -> p k m", k=KC)).then_inc(out_ready, 1)

            q_copy(0)
            q_copy(1)
            for t in range(NT):
                for i, (c, n) in enumerate(PARTS):
                    g = 3 * t + i
                    act.wait_ge(gu_summed, g + 1)
                    if g >= 2:
                        act.wait_ge(h_ready, g - 1)
                    S.activation(silu[:, g % 2, 0:n], gu_ps[2 * (g % 2)][:, 0:n], ACT.Silu,
                                 scale=col(G_SCALE, t)).then_inc(silu_ready, 1)
                    if t % 2 == 0 and t >= 2 and i < 2:
                        h_round(t - 2 + i)
                    if t % 2 and t >= 3 and i == 0:
                        h_copy(t - 3)
                    if t % 2 and i == 1:
                        square(t - 1)
                for j in TURN_AFTER.get(t, ()):
                    q_copy(j)
                if t >= 4 and t % 2 == 0:
                    out_copy(t - 4)
                if t % 2:
                    if t >= 3:
                        h_copy(t - 2)
                    square(t)
                    if t >= 5:
                        out_copy(t - 4)
            h_round(NT - 2)
            h_round(NT - 1)
            out_copy(NT - 4)
            h_copy(NT - 2)
            out_copy(NT - 3)
            h_copy(NT - 1)
            out_copy(NT - 2)
            out_copy(NT - 1)

        @block.tensor
        def _(pe):
            T = nc.tensor
            for t in range(NT):
                ps = (x_ps, y_ps)[t % 2]
                pe.wait_ge(stack_ready, t + 1)
                if t >= 2:
                    pe.wait_ge(x3_ready, t - 1)
                for k in range(KC):
                    mm = T.transpose(ps[:, k * P:(k + 1) * P], stack[:, t, k, :], ident[:, :])
                mm.then_inc(stack_turned, 1)
            pe.wait_ge(ident_ready, 1)

            def turn_q(t):
                pe.wait_ge(q_ready, t + 1)
                if t >= 2:
                    pe.wait_ge(q_cm_ready, t - 1)
                for k in range(KC):
                    mm = T.transpose(half(ht_ps[t % 2])[:, k * P:(k + 1) * P], q[:, t, k * P:(k + 1) * P], ident_b[:, :])
                mm.then_inc(q_turned, 1)

            def turn_h(t):
                pe.wait_ge(hq_ready, t + 1)
                if t == 0:
                    pe.wait_ge(q_cm_ready, NT)
                else:
                    pe.wait_ge(h_cm_ready, 2 * t)
                for k in range(W3):
                    dst = half(ht_ps[0], 1024)[:, k * P:(k + 1) * P] if k < 8 else half(ht_ps[1])[:, (k - 8) * P:(k - 7) * P]
                    mm = T.transpose(dst, hq[:, t % 4, k * P:(k + 1) * P], ident_b[:, :])
                mm.then_inc(h_turned, 1)

            def second(t):
                pe.wait_ge(h_cm_ready, 2 * t + 2)
                if t:
                    pe.wait_ge(x4_ready, t)
                else:
                    pe.wait_ge(x3_ready, NT)
                for k in range(W3):
                    mm = T.matmul(y_ps[:, :], h_cm[:, t % 2, k, :], w3[:, k, :], start=(k == 0), stop=(k == W3 - 1))
                mm.then_inc(y_summed, 1)

            def turn_out(t):
                pe.wait_ge(x4_ready, t + 1)
                if t:
                    pe.wait_ge(out_ready, t)
                for k in range(KC):
                    mm = T.transpose(x_ps[:, k * P:(k + 1) * P], x_tm[:, t, k * P:(k + 1) * P], ident[:, :])
                mm.then_inc(x4_turned, 1)

            turn_q(0)
            turn_q(1)
            for t in range(NT):
                pe.wait_ge(q_cm_ready, t + 1)
                for i, (c, n) in enumerate(PARTS):
                    g = 3 * t + i
                    if g >= 2:
                        pe.wait_ge(h_ready, g - 1)
                    for w, ps in ((w1, gu_ps[2 * (g % 2)]), (w2, gu_ps[2 * (g % 2) + 1])):
                        for k in range(KC):
                            mm = T.matmul(ps[:, 0:n], q_cm[:, t, k, :], w[:, k, c:c + n],
                                          start=(k == 0), stop=(k == KC - 1))
                    mm.then_inc(gu_summed, 1)
                    if t % 2 and t >= 3 and i == 0:
                        turn_h(t - 3)
                for j in TURN_AFTER.get(t, ()):
                    turn_q(j)
                if t >= 4 and t % 2 == 0:
                    turn_out(t - 4)
                if t % 2 and t >= 3:
                    turn_h(t - 2)
                    second(t - 3)
                    if t >= 5:
                        turn_out(t - 4)
                    second(t - 2)
            turn_out(NT - 4)
            turn_h(NT - 2)
            turn_out(NT - 3)
            second(NT - 2)
            turn_h(NT - 1)
            second(NT - 1)
            turn_out(NT - 2)
            turn_out(NT - 1)

        @block.vector
        def _(dve):
            V = nc.vector
            done = [0]

            def link(ins):
                done[0] += 1
                ins.then_inc(dve_step, 1)
                dve.wait_ge(dve_step, done[0])

            def step(ins):
                done[0] += 1
                ins.then_inc(dve_step, 1)

            def quant_scale(t0, t1, rms, top, a, to, inv):
                a, to, inv, rms = cols(a, t0, t1), cols(to, t0, t1), cols(inv, t0, t1), cols(rms, t0, t1)
                link(V.tensor_tensor(a, cols(top, t0, t1), rms, ALU.mult))
                link(V.tensor_scalar(a, a, QEPS, None, ALU.max))
                step(V.tensor_scalar(inv, a, 1.0 / 127.0, None, ALU.mult))
                link(V.reciprocal(to, a))
                return V.scalar_tensor_tensor(to, to, 127.0, rms, ALU.mult, ALU.mult)

            def stats(t):
                dve.wait_ge(x3_ready, t + 1)
                step(V.bn_stats(st[:, t, :], x_tm[:, t, :]))

            def z_max(t):
                dve.wait_ge(z_ready[t % 2], t // 2 + 1)
                step(V.tensor_reduce(col(ZMAX, t), z[:, t, :], AX.X, ALU.max, apply_absolute_value=True))

            def q_scales(part):
                t0, t1 = part * HALF_TILES, (part + 1) * HALF_TILES
                dve.wait_ge(dve_step, done[0])
                link(V.tensor_scalar(cols(ZMAX, t0, t1), cols(ZMAX, t0, t1), QEPS, None, ALU.max))
                step(V.tensor_scalar(cols(INV_Q, t0, t1), cols(ZMAX, t0, t1), 1.0 / 127.0, None, ALU.mult))
                link(V.reciprocal(cols(Q, t0, t1), cols(ZMAX, t0, t1)))
                V.tensor_scalar(cols(Q, t0, t1), cols(Q, t0, t1), 127.0, None, ALU.mult).then_inc(q_scale_ready, 1)
                step(V.tensor_scalar(cols(G_SCALE, t0, t1), cols(INV_Q, t0, t1), inv_ws[:, 0:1], None, ALU.mult))
                step(V.tensor_scalar(cols(U_SCALE, t0, t1), cols(INV_Q, t0, t1), inv_ws[:, 1:2], None, ALU.mult))

            def quant(t):
                mine, ready = (ACT_ZR, zr_ready[0]) if t in ACT_ZR else (POOL_ZR, zr_ready[1])
                dve.wait_ge(ready, mine.index(t) + 1)
                V.tensor_scalar(q[:, t, :], z[:, t, :], -ROUND, -32.0, ALU.add, ALU.max).then_inc(q_ready, 1)

            def h_max(t):
                dve.wait_ge(h_ready, 3 * t + 3)
                step(V.tensor_reduce(col(HMAX, t), h[:, t % 4, :], AX.X, ALU.max, apply_absolute_value=True))

            def h_quant(t):
                dve.wait_ge(hr_ready, t + 1)
                if t >= 4:
                    dve.wait_ge(h_turned, t - 3)
                V.tensor_scalar(hq[:, t % 4, :], h[:, t % 4, :], -ROUND, -32.0, ALU.add, ALU.max).then_inc(hq_ready, 1)

            def add_y(t):
                dve.wait_ge(y_summed, t + 1)
                V.scalar_tensor_tensor(x_tm[:, t, :], y_ps[:, :], col(Y_SCALE, t), x_tm[:, t, :],
                                       ALU.mult, ALU.add).then_inc(x4_ready, 1)

            for t in range(NT):
                dve.wait_ge(stack_turned, t + 1)
                V.tensor_tensor(x_tm[:, t, :], (x_ps, y_ps)[t % 2][:, :], x_tm[:, t, :], ALU.add).then_inc(x3_ready, 1)
                if t:
                    stats(t - 1)
            stats(NT - 1)
            dve.wait_ge(dve_step, done[0])
            for t in range(NT):
                step(V.bn_aggr(mv[:, t, :], st[:, t, :]))
            dve.wait_ge(dve_step, done[0])
            rsqrt(nc, link, cols(RSTD, 0, NT), mv[:, :, 1], BOTH_SCALE, BOTH_EPS, scratch)
            V.scalar_tensor_tensor(cols(SHIFT, 0, NT), mv[:, :, 0], -1.0, cols(RSTD, 0, NT),
                                   ALU.mult, ALU.mult).then_inc(rstd_ready, 1)
            for t in range(HALF_TILES):
                z_max(t)
            q_scales(0)
            for t in range(HALF_TILES):
                quant(t)
            for t in range(HALF_TILES, NT):
                z_max(t)
            q_scales(1)
            dve.wait_ge(dve_step, done[0])
            for t in range(NT):
                for i, (c, n) in enumerate(PARTS):
                    g = 3 * t + i
                    dve.wait_ge(silu_ready, g + 1)
                    V.scalar_tensor_tensor(h[:, t % 4, c:c + n], gu_ps[2 * (g % 2) + 1][:, 0:n], col(U_SCALE, t),
                                           silu[:, g % 2, 0:n], ALU.mult, ALU.mult).then_inc(h_ready, 1)
                    if t % 2 == 0 and t >= 2 and i >= 1:
                        h_quant(t - 3 + i)
                    if t % 2 and i == 0:
                        h_max(t - 1)
                for j in QUANT_AFTER.get(t, ()):
                    quant(j)
                if t % 2:
                    h_max(t)
                    if t >= 3:
                        add_y(t - 3)
                    dve.wait_ge(dve_step, done[0])
                    dve.wait_ge(hsq_ready, t + 1)
                    rsqrt(nc, link, cols(HRMS, t - 1, t + 1), cols(HSS, t - 1, t + 1), 1.0 / W1, RMS_EPS, scratch)
                    quant_scale(t - 1, t + 1, HRMS, HMAX, HA, HQ, Y_SCALE).then_inc(hscale_ready, 1)
                    link(V.tensor_scalar(cols(Y_SCALE, t - 1, t + 1), cols(Y_SCALE, t - 1, t + 1), inv_ws[:, 2:3], None, ALU.mult))
                    if t >= 3:
                        add_y(t - 2)
            for t in (NT - 2, NT - 1):
                h_quant(t)
            for t in (NT - 2, NT - 1):
                add_y(t)


def program(nc, io):
    with ExitStack() as ctx:
        def sb(name, shape, dt=FP32):
            return ctx.enter_context(nc.sbuf_tensor(name, shape, dt))
        keep = {
            "x_tm": sb("x_tm", [P, NT, C]),
            "ident": sb("ident", [P, P]),
            "aff": sb("aff", [P, NT, TOPK]),
            "slots": sb("slots", [P, NT, TOPK], U32),
            "rounds": sb("rounds", [P, 1], U32),
            "narrow": sb("narrow", [P, MAX_ROUNDS * EXPERTS], U32),
            "token_ids": sb("token_ids", [P, NT], U32),
            "rows": sb("rows", [P, GROUP, C]),
            "raw": sb("raw", [P, 2, PIECE]),
            "ternary": sb("ternary", [P, 3, KC * W1], F8),
            "inv_ws": sb("inv_ws", [P, 3]),
        }
        attention_and_routing(nc, io, keep)
        keep["conv_hi"] = sb("conv_hi", [P, KC, C], F16)
        keep["conv_lo"] = sb("conv_lo", [P, KC, C], F16)
        keep["bias_hi"] = sb("bias_hi", [1, C], F16)
        keep["bias_lo"] = sb("bias_lo", [1, C], F16)
        keep["scan_mv"] = sb("scan_mv", [P, NT, 2])
        keep["scan_rstd"] = sb("scan_rstd", [P, NT])
        experts(nc, io, keep)
        keep["state"] = sb("state", [P, IMH, KC, BATCH, IMW])
        scan(nc, io, keep)
        ternary_ffn(nc, io, keep)


def kernel(**inputs):
    import concourse.bacc as bacc
    from concourse.bass_utils import run_bass_kernel_spmd

    nc = bacc.Bacc("TRN2", target_bir_lowering=False, num_devices=1)
    a = {k: np.asarray(v) for k, v in inputs.items()}
    host = {
        "x": a["x"],
        "w1t": a["L0_conv_w1"].T, "w2t": a["L0_conv_w2"].T, "w3t": a["L0_conv_w3"].T,
        "b1": a["L0_conv_b1"], "b2": a["L0_conv_b2"], "b3": a["L0_conv_b3"], "alpha": a["L0_conv_alpha"],
        "lnw": a["L0_ffn_ln_weight"], "router": a["L0_ffn_router_weight"],
        "gate_up": a["L0_ffn_gate_up_proj"], "down": a["L0_ffn_down_proj"],
        "sgate": a["L0_ffn_shared_gate_w"], "sup": a["L0_ffn_shared_up_w"], "sdown": a["L0_ffn_shared_down_w"],
        "conv_w": a["L1_conv_W"][:, :, 4, 0].T, "conv_b": a["L1_conv_b"],
        "f1": a["L1_ffn_w1"].T, "f2": a["L1_ffn_w2"].T, "f3": a["L1_ffn_w3"].T,
    }
    host = {k: np.ascontiguousarray(v) for k, v in host.items()}
    io = {k: nc.dram_tensor(f"in_{k}", v.shape, FP32, kind="ExternalInput").ap() for k, v in host.items()}
    io["tokens"] = nc.dram_tensor("tokens", (TOK, C), FP32, kind="Internal").ap()
    io["slot_token"] = nc.dram_tensor("slot_token", (SLOTS, 1), U32, kind="Internal").ap()
    io["slot_y"] = nc.dram_tensor("slot_y", (SLOTS, C), FP32, kind="Internal").ap()
    io["out"] = nc.dram_tensor("out", a["x"].shape, FP32, kind="ExternalOutput").ap()
    program(nc, io)
    r = run_bass_kernel_spmd(nc, [{f"in_{k}": v for k, v in host.items()}], core_ids=[0])
    return r.results[0]["out"]
```
